# Optimizing a Trainium2 kernel written in Bass

```python
import numpy as np
import jax
import jax.numpy as jnp

def _softmax(x, axis=-1):
    return jax.nn.softmax(x, axis=axis)

def _gelu(x):
    return jax.nn.gelu(x, approximate=True)

def _silu(x):
    return jax.nn.silu(x)

def _sigmoid(x):
    return jax.nn.sigmoid(x)

def _layernorm(x, axis=-1, eps=1e-05):
    m = jnp.mean(x, axis=axis, keepdims=True)
    v = jnp.var(x, axis=axis, keepdims=True)
    return (x - m) / jnp.sqrt(v + eps)

def _scatter_add(tgt, idx, src, axis=0):
    return tgt.at[idx].add(src)

def _segment_sum(src, seg, n):
    return jax.ops.segment_sum(src, seg, n)
kernel_name = 'mk_seq_postln_d2_jaxref_r8_c03132'

def setup_inputs(seed: int=0):
    np.random.seed(seed)
    _w = jnp.asarray

    def _L0_attn_setup():
        import jax, jax.numpy as jnp
        import numpy as np
        import math
        D_MODEL, D_STATE, D_CONV, EXPAND = (128, 16, 4, 2)
        D_INNER = EXPAND * D_MODEL
        DT_RANK = math.ceil(D_INNER / 16)
        DT_MIN, DT_MAX = (0.001, 0.1)

        def _rmsnorm(x, w, eps=1e-05):
            return x * jax.lax.rsqrt(jnp.mean(x * x, axis=-1, keepdims=True) + eps) * w

        def _silu(x):
            return x * jax.nn.sigmoid(x)

        def _selective_scan(u, delta, A, B_ssm, C_ssm, D):
            b, L, dim = u.shape
            n = A.shape[1]
            h0 = jnp.zeros((b, dim, n), u.dtype)

            def step(h, inp):
                u_t, dt_t, B_t, C_t = inp
                dA = jnp.exp(dt_t[..., None] * A)
                h = dA * h + (dt_t * u_t)[..., None] * B_t[:, None, :]
                y = jnp.einsum('bdn,bn->bd', h, C_t)
                return (h, y)
            xs = (u.transpose(1, 0, 2), delta.transpose(1, 0, 2), B_ssm.transpose(1, 0, 2), C_ssm.transpose(1, 0, 2))
            _, ys = jax.lax.scan(step, h0, xs)
            return ys.transpose(1, 0, 2) + u * D
        key = jax.random.key(seed)
        ks = jax.random.split(key, 12)
        B, L = (4, 256)
        x = jax.random.normal(ks[0], (B, L, D_MODEL), dtype=jnp.float32)
        in_proj_w = jax.random.normal(ks[1], (2 * D_INNER, D_MODEL), jnp.float32) * (1.0 / np.sqrt(D_MODEL))
        conv_w = jax.random.normal(ks[2], (D_INNER, D_CONV), jnp.float32) * (1.0 / np.sqrt(D_CONV))
        conv_b = jax.random.normal(ks[3], (D_INNER,), jnp.float32) * 0.02
        x_proj_w = jax.random.normal(ks[4], (DT_RANK + 2 * D_STATE, D_INNER), jnp.float32) * (1.0 / np.sqrt(D_INNER))
        dt_proj_w = jax.random.uniform(ks[5], (D_INNER, DT_RANK), jnp.float32, -0.1, 0.1)
        dt = jnp.exp(jax.random.uniform(ks[6], (D_INNER,), jnp.float32) * (np.log(DT_MAX) - np.log(DT_MIN)) + np.log(DT_MIN))
        dt = jnp.clip(dt, 0.0001, None)
        dt_proj_b = dt + jnp.log(-jnp.expm1(-dt))
        A_log = jnp.log(jnp.tile(jnp.arange(1, D_STATE + 1, dtype=jnp.float32)[None, :], (D_INNER, 1)))
        D = jnp.ones((D_INNER,), jnp.float32)
        out_proj_w = jax.random.normal(ks[7], (D_MODEL, D_INNER), jnp.float32) * (1.0 / np.sqrt(D_INNER))
        norm_w = jnp.ones((D_MODEL,), jnp.float32)
        norm_f_w = jnp.ones((D_MODEL,), jnp.float32)
        return dict(x=x, norm_w=norm_w, in_proj_w=in_proj_w, conv_w=conv_w, conv_b=conv_b, x_proj_w=x_proj_w, dt_proj_w=dt_proj_w, dt_proj_b=dt_proj_b, A_log=A_log, D=D, out_proj_w=out_proj_w, norm_f_w=norm_f_w)
    _L0_attn_in = _L0_attn_setup()

    def _L0_ffn_setup():
        import jax, jax.numpy as jnp
        import numpy as np
        B, S, D, E, H, DO = (4, 256, 128, 8, 512, 128)
        TOP_K = 2
        LN_EPS = 1e-05
        key = jax.random.key(seed)
        ks = jax.random.split(key, 9)
        s = 0.02
        return {'x': jax.random.normal(ks[0], (B, S, D), dtype=jnp.float32), 'W1': jax.random.normal(ks[1], (E, D, H), dtype=jnp.float32) * s, 'b1': jnp.zeros((E, H), dtype=jnp.float32), 'W2': jax.random.normal(ks[2], (E, H, DO), dtype=jnp.float32) * s, 'b2': jnp.zeros((E, DO), dtype=jnp.float32), 'gate_W': jax.random.normal(ks[3], (D, E), dtype=jnp.float32) * s, 'shared_W': jax.random.normal(ks[4], (D, DO), dtype=jnp.float32) * s, 'shared_b': jnp.zeros((DO,), dtype=jnp.float32), 'gamma': jnp.ones((DO,), dtype=jnp.float32), 'beta': jnp.zeros((DO,), dtype=jnp.float32)}
    _L0_ffn_in = _L0_ffn_setup()

    def _L1_attn_setup():
        import jax, jax.numpy as jnp
        import numpy as np
        B, S, D, H = (2, 256, 128, 16)
        DK = D // H
        key = jax.random.key(seed)
        ks = jax.random.split(key, 9)
        s = 0.02
        return {'embeddings': jax.random.normal(ks[0], (B, S, D), jnp.float32), 'Wq': jax.random.normal(ks[1], (H, D, DK), jnp.float32) * s, 'bq': jax.random.normal(ks[2], (H, DK), jnp.float32) * s, 'Wk': jax.random.normal(ks[3], (H, D, DK), jnp.float32) * s, 'bk': jax.random.normal(ks[4], (H, DK), jnp.float32) * s, 'Wv': jax.random.normal(ks[5], (H, D, DK), jnp.float32) * s, 'bv': jax.random.normal(ks[6], (H, DK), jnp.float32) * s, 'Wo': jax.random.normal(ks[7], (D, D), jnp.float32) * s, 'bo': jax.random.normal(ks[8], (D,), jnp.float32) * s}
    _L1_attn_in = _L1_attn_setup()

    def _L1_ffn_setup():
        import jax, jax.numpy as jnp
        import numpy as np
        S, B, H = (256, 4, 128)
        E = 64
        K = 4
        I = 64
        CAP = 128
        key = jax.random.key(seed)
        k1, k2, k3, k4 = jax.random.split(key, 4)
        return {'hidden_states': jax.random.normal(k1, (S, B, H), dtype=jnp.float32), 'router_w': jax.random.normal(k2, (H, E), dtype=jnp.float32) * 0.02, 'w1': jax.random.normal(k3, (E, H, 2 * I), dtype=jnp.float32) * 0.02, 'w2': jax.random.normal(k4, (E, I, H), dtype=jnp.float32) * 0.02}
    _L1_ffn_in = _L1_ffn_setup()
    _d = {'L0_attn_x': _L0_attn_in['x'], 'L0_attn_norm_w': _L0_attn_in['norm_w'], 'L0_attn_in_proj_w': _L0_attn_in['in_proj_w'], 'L0_attn_conv_w': _L0_attn_in['conv_w'], 'L0_attn_conv_b': _L0_attn_in['conv_b'], 'L0_attn_x_proj_w': _L0_attn_in['x_proj_w'], 'L0_attn_dt_proj_w': _L0_attn_in['dt_proj_w'], 'L0_attn_dt_proj_b': _L0_attn_in['dt_proj_b'], 'L0_attn_A_log': _L0_attn_in['A_log'], 'L0_attn_D': _L0_attn_in['D'], 'L0_attn_out_proj_w': _L0_attn_in['out_proj_w'], 'L0_attn_norm_f_w': _L0_attn_in['norm_f_w'], 'L0_ffn_W1': _L0_ffn_in['W1'], 'L0_ffn_b1': _L0_ffn_in['b1'], 'L0_ffn_W2': _L0_ffn_in['W2'], 'L0_ffn_b2': _L0_ffn_in['b2'], 'L0_ffn_gate_W': _L0_ffn_in['gate_W'], 'L0_ffn_shared_W': _L0_ffn_in['shared_W'], 'L0_ffn_shared_b': _L0_ffn_in['shared_b'], 'L0_ffn_gamma': _L0_ffn_in['gamma'], 'L0_ffn_beta': _L0_ffn_in['beta'], 'L1_attn_Wq': _L1_attn_in['Wq'], 'L1_attn_bq': _L1_attn_in['bq'], 'L1_attn_Wk': _L1_attn_in['Wk'], 'L1_attn_bk': _L1_attn_in['bk'], 'L1_attn_Wv': _L1_attn_in['Wv'], 'L1_attn_bv': _L1_attn_in['bv'], 'L1_attn_Wo': _L1_attn_in['Wo'], 'L1_attn_bo': _L1_attn_in['bo'], 'L1_ffn_router_w': _L1_ffn_in['router_w'], 'L1_ffn_w1': _L1_ffn_in['w1'], 'L1_ffn_w2': _L1_ffn_in['w2']}
    _x0 = _d['L0_attn_x']
    _d['L0_attn_x'] = jax.random.normal(jax.random.fold_in(jax.random.key(seed), 1), (4, 1024, 128), dtype=_x0.dtype)
    del _x0
    return _d

def reference(L0_attn_x, L0_attn_norm_w, L0_attn_in_proj_w, L0_attn_conv_w, L0_attn_conv_b, L0_attn_x_proj_w, L0_attn_dt_proj_w, L0_attn_dt_proj_b, L0_attn_A_log, L0_attn_D, L0_attn_out_proj_w, L0_attn_norm_f_w, L0_ffn_W1, L0_ffn_b1, L0_ffn_W2, L0_ffn_b2, L0_ffn_gate_W, L0_ffn_shared_W, L0_ffn_shared_b, L0_ffn_gamma, L0_ffn_beta, L1_attn_Wq, L1_attn_bq, L1_attn_Wk, L1_attn_bk, L1_attn_Wv, L1_attn_bv, L1_attn_Wo, L1_attn_bo, L1_ffn_router_w, L1_ffn_w1, L1_ffn_w2):

    def _L0_attn_ref(x, norm_w, in_proj_w, conv_w, conv_b, x_proj_w, dt_proj_w, dt_proj_b, A_log, D, out_proj_w, norm_f_w):
        import jax, jax.numpy as jnp
        import numpy as np
        import math
        D_MODEL, D_STATE, D_CONV, EXPAND = (128, 16, 4, 2)
        D_INNER = EXPAND * D_MODEL
        DT_RANK = math.ceil(D_INNER / 16)
        DT_MIN, DT_MAX = (0.001, 0.1)

        def _rmsnorm(x, w, eps=1e-05):
            return x * jax.lax.rsqrt(jnp.mean(x * x, axis=-1, keepdims=True) + eps) * w

        def _silu(x):
            return x * jax.nn.sigmoid(x)

        def _selective_scan(u, delta, A, B_ssm, C_ssm, D):
            b, L, dim = u.shape
            n = A.shape[1]
            h0 = jnp.zeros((b, dim, n), u.dtype)

            def step(h, inp):
                u_t, dt_t, B_t, C_t = inp
                dA = jnp.exp(dt_t[..., None] * A)
                h = dA * h + (dt_t * u_t)[..., None] * B_t[:, None, :]
                y = jnp.einsum('bdn,bn->bd', h, C_t)
                return (h, y)
            xs = (u.transpose(1, 0, 2), delta.transpose(1, 0, 2), B_ssm.transpose(1, 0, 2), C_ssm.transpose(1, 0, 2))
            _, ys = jax.lax.scan(step, h0, xs)
            return ys.transpose(1, 0, 2) + u * D
        residual = x
        out = _rmsnorm(x, norm_w)
        B, L, _ = out.shape
        xz = out @ in_proj_w.T
        x_branch, z_branch = jnp.split(xz, 2, axis=-1)
        xp = jnp.pad(x_branch, ((0, 0), (D_CONV - 1, 0), (0, 0)))
        x_conv = conv_b
        for k in range(D_CONV):
            x_conv = x_conv + xp[:, k:k + L, :] * conv_w[:, k]
        x_conv = _silu(x_conv)
        x_dbl = x_conv @ x_proj_w.T
        dt_low = x_dbl[..., :DT_RANK]
        B_ssm = x_dbl[..., DT_RANK:DT_RANK + D_STATE]
        C_ssm = x_dbl[..., DT_RANK + D_STATE:]
        dt = jax.nn.softplus(dt_low @ dt_proj_w.T + dt_proj_b)
        A = -jnp.exp(A_log)
        y = _selective_scan(x_conv, dt, A, B_ssm, C_ssm, D)
        y = y * _silu(z_branch)
        out = y @ out_proj_w.T + residual
        return _rmsnorm(out, norm_f_w)

    def _L0_ffn_ref(x, W1, b1, W2, b2, gate_W, shared_W, shared_b, gamma, beta):
        import jax, jax.numpy as jnp
        import numpy as np
        B, S, D, E, H, DO = (4, 256, 128, 8, 512, 128)
        TOP_K = 2
        LN_EPS = 1e-05
        d = x.shape[-1]
        flat = x.reshape(-1, d)
        n_exp = gate_W.shape[-1]
        probs = jax.nn.softmax(flat @ gate_W, axis=-1)
        topk_w, topk_idx = jax.lax.top_k(probs, TOP_K)
        topk_w = topk_w / topk_w.sum(axis=-1, keepdims=True)
        combine = (jax.nn.one_hot(topk_idx, n_exp, dtype=flat.dtype) * topk_w[..., None]).sum(axis=1)
        out = 0.5 * jax.nn.gelu(flat @ shared_W + shared_b, approximate=False)
        for e in range(n_exp):
            h = jax.nn.gelu(flat @ W1[e] + b1[e], approximate=False)
            out = out + combine[:, e:e + 1] * (h @ W2[e] + b2[e])
        mean = out.mean(axis=-1, keepdims=True)
        var = ((out - mean) ** 2).mean(axis=-1, keepdims=True)
        out = (out - mean) * jax.lax.rsqrt(var + LN_EPS) * gamma + beta
        return out.reshape(*x.shape[:-1], out.shape[-1])

    def _L1_attn_ref(embeddings, Wq, bq, Wk, bk, Wv, bv, Wo, bo):
        import jax, jax.numpy as jnp
        import numpy as np
        B, S, D, H = (2, 256, 128, 16)
        DK = D // H
        b, s, d = embeddings.shape
        dk = Wq.shape[-1]
        q = jnp.einsum('bsd,hdk->bhsk', embeddings, Wq) + bq[None, :, None, :]
        k = jnp.einsum('bsd,hdk->bhsk', embeddings, Wk) + bk[None, :, None, :]
        v = jnp.einsum('bsd,hdk->bhsk', embeddings, Wv) + bv[None, :, None, :]
        scores = jnp.einsum('bhqk,bhsk->bhqs', q, k) / jnp.sqrt(jnp.float32(dk))
        causal_mask = jnp.triu(jnp.ones((s, s), dtype=bool), k=1)
        scores = jnp.where(causal_mask, jnp.float32(-1000000000.0), scores)
        weights = jax.nn.softmax(scores, axis=-1)
        ctx = jnp.einsum('bhqs,bhsk->bhqk', weights, v)
        concat = ctx.transpose(0, 2, 1, 3).reshape(b, s, d)
        return concat @ Wo + bo

    def _L1_ffn_ref(hidden_states, router_w, w1, w2):
        import jax, jax.numpy as jnp
        import numpy as np
        S, B, H = (256, 4, 128)
        E = 64
        K = 4
        I = 64
        CAP = 128
        s, b, h = hidden_states.shape
        x = hidden_states.reshape(-1, h)
        T = x.shape[0]
        P = T * K
        logits = x @ router_w
        probs_all = jax.nn.softmax(logits, axis=-1)
        top_p, top_i = jax.lax.top_k(probs_all, K)
        rows = jnp.arange(T)[:, None]
        routing_map = jnp.zeros((T, E), dtype=bool).at[rows, top_i].set(True)
        probs = jnp.zeros((T, E), dtype=x.dtype).at[rows, top_i].set(top_p)
        flat = routing_map.T.reshape(-1)
        order = jnp.argsort((~flat).astype(jnp.int32), stable=True)[:P]
        expert_id = order // T
        token_idx = order % T
        group_sizes = routing_map.sum(axis=0)
        starts = jnp.cumsum(group_sizes) - group_sizes
        pos = jnp.arange(P) - starts[expert_id]
        perm_x = x[token_idx]
        buf = jnp.zeros((E, CAP, h), dtype=x.dtype).at[expert_id, pos].set(perm_x)
        h1 = jnp.einsum('ech,ehf->ecf', buf, w1)
        g = jax.nn.silu(h1[..., :I]) * h1[..., I:]
        y = jnp.einsum('eci,eih->ech', g, w2)
        perm_y = y[expert_id, pos]
        perm_probs = probs.T.reshape(-1)[order]
        out = jnp.zeros((T, h), dtype=x.dtype).at[token_idx].add(perm_y * perm_probs[:, None])
        return out.reshape(s, b, h)
    x = L0_attn_x
    x = _layernorm(x + _L0_attn_ref(x, L0_attn_norm_w, L0_attn_in_proj_w, L0_attn_conv_w, L0_attn_conv_b, L0_attn_x_proj_w, L0_attn_dt_proj_w, L0_attn_dt_proj_b, L0_attn_A_log, L0_attn_D, L0_attn_out_proj_w, L0_attn_norm_f_w), axis=-1)
    x = _layernorm(x + _L0_ffn_ref(x, L0_ffn_W1, L0_ffn_b1, L0_ffn_W2, L0_ffn_b2, L0_ffn_gate_W, L0_ffn_shared_W, L0_ffn_shared_b, L0_ffn_gamma, L0_ffn_beta), axis=-1)
    x = _layernorm(x + _L1_attn_ref(x, L1_attn_Wq, L1_attn_bq, L1_attn_Wk, L1_attn_bk, L1_attn_Wv, L1_attn_bv, L1_attn_Wo, L1_attn_bo), axis=-1)
    x = _layernorm(x + _L1_ffn_ref(x, L1_ffn_router_w, L1_ffn_w1, L1_ffn_w2), axis=-1)
    return x

_drawn_inputs = setup_inputs


def setup_inputs(seed=0):
    import zlib

    import numpy as np

    out = dict(_drawn_inputs(seed))
    spreads = {'L0_attn_norm_w': (1.0, 0.2),
     'L0_attn_D': (1.0, 0.2),
     'L0_attn_norm_f_w': (1.0, 0.2),
     'L0_ffn_b1': (0.0, 0.1),
     'L0_ffn_b2': (0.0, 0.1),
     'L0_ffn_shared_b': (0.0, 0.1),
     'L0_ffn_gamma': (1.0, 0.2),
     'L0_ffn_beta': (0.0, 0.1)}
    factors = {'L1_attn_Wq': 8.0,
     'L1_attn_bq': 8.0,
     'L1_attn_Wk': 8.0,
     'L1_attn_bk': 8.0,
     'L1_attn_Wv': 3.513,
     'L1_attn_bv': 8.0,
     'L1_attn_Wo': 3.022,
     'L1_attn_bo': 2.719,
     'L1_ffn_router_w': 8.0,
     'L1_ffn_w1': 8.0,
     'L1_ffn_w2': 8.0}
    for name, (base, spread) in spreads.items():
        noise = np.random.default_rng([zlib.crc32(name.encode()), seed]).standard_normal(out[name].shape)
        drawn = base * np.exp(spread * noise) if base else spread * noise
        out[name] = jnp.asarray(drawn.astype(out[name].dtype))
    for name, factor in factors.items():
        out[name] = (out[name] * factor).astype(out[name].dtype)
    return out
```

```python
from contextlib import ExitStack

import numpy as np

import concourse.bass as bass
from concourse import mybir

F32 = mybir.dt.float32
F32R = mybir.dt.float32r
BF16 = mybir.dt.bfloat16
I32 = mybir.dt.int32
U32 = mybir.dt.uint32
ALU = mybir.AluOpType
ACT = mybir.ActivationFunctionType
AX = mybir.AxisListType

P = 128
T = 4096
BATCH = 4
SEQ = T // BATCH
CH = 512
NCH = T // CH
EPS = 1e-5


def chunk(tile, i, n=CH):
    return tile[:, bass.ds(i * n, n)]


def chunk2(tile, c, i, n=CH):
    return tile[:, c, bass.ds(i * n, n)]


def twos(eng, n, step):
    step(0, 0)
    step(1, 1)
    with eng.Fori(1, n // 2) as j:
        for k in range(2):
            step(j * 2 + k, k)


def past(i, n=2):
    return not (isinstance(i, int) and i < n)


D_IN = 256
NST = 16
RANK = 16
TAPS = 4


def mamba_front(nc, io, keep):
    XN, U, DT, G, XT = keep["XN"], keep["U"], keep["DT"], keep["G"], keep["XT"]
    with ExitStack() as ctx:
        sb = lambda n, s, d=F32: ctx.enter_context(nc.sbuf_tensor("a_" + n, s, d))
        sem = lambda n: ctx.enter_context(nc.semaphore(n))
        pad = SEQ + TAPS - 1
        XB = sb("XB", [P, 2, BATCH * pad])
        E = XB
        R = sb("R", [P, T])
        ones = keep["ones"]
        in_w = sb("in_w", [P, D_IN])
        conv_w = sb("conv_w", [P, 2, TAPS])
        conv_b = sb("conv_b", [P, 2])
        norm_w = sb("norm_w", [P, 1])
        xp_bc = sb("xp_bc", [P, 2, P])
        xp_dt = sb("xp_dt", [P, 2, RANK])
        dt_w = sb("dt_w", [RANK, D_IN])
        dt_b = sb("dt_b", [P, 2])
        dt_low = sb("dt_low", [RANK, T])
        tmp = sb("tmp", [P, 2, CH])
        eps, one, ident = keep["eps"], keep["one"], keep["ident"]
        ps_rms = [ctx.enter_context(nc.psum_tensor(f"ps_rms{k}", [P, CH], F32)) for k in range(2)]
        ps_x = [ctx.enter_context(nc.psum_tensor(f"ps_x{k}", [P, CH], F32)) for k in range(2)]
        ps_bc = [ctx.enter_context(nc.psum_tensor(f"ps_bc{k}", [P, CH], F32)) for k in range(2)]
        ps_dt = [ctx.enter_context(nc.psum_tensor(f"ps_dt{k}", [P, CH], F32)) for k in range(2)]
        s_w = sem("a_weights")
        s_zero = sem("a_zeroed")
        s_id = sem("a_identity")
        s_xp = sem("a_xp_loaded")
        s_x = [sem(f"a_x_loaded{b}") for b in range(BATCH)]
        s_sq = sem("a_squares")
        s_ms = sem("a_mean_square")
        s_lnr = sem("a_ln_rms")
        s_r = sem("a_inv_rms")
        s_xn = sem("a_normed")
        s_xps = sem("a_x_proj_psum")
        s_xb = sem("a_x_branch")
        s_tap = sem("a_tap")
        s_cv = sem("a_conv")
        s_u = sem("a_silu")
        s_bcps = sem("a_bc_psum")
        s_hi = sem("a_bc_high")
        s_g = sem("a_bc_split")
        s_dlps = sem("a_dt_low_psum")
        s_dl = sem("a_dt_low")
        s_dtps = sem("a_dt_psum")
        s_abs = sem("a_abs_dt")
        s_rel = sem("a_relu_dt")
        s_e = sem("a_exp_dt")
        s_l = sem("a_ln_dt")
        s_c = sem("a_dve_dt")
        s_own = sem("a_own_step")
        keep["used"] += [s_w, s_zero, s_id, s_xp, *s_x, s_sq, s_ms, s_lnr, s_r, s_xn, s_xps, s_xb, s_tap, s_cv, s_u,
                         s_bcps, s_hi, s_g, s_dlps, s_dl, s_dtps, s_abs, s_rel, s_e, s_l, s_c, s_own]

        ctx.enter_context(nc.allow_non_contiguous_dma(reason="small per-feature vectors"))
        block = ctx.enter_context(nc.Block())

        @block.sync
        def _(sp):
            for b in range(BATCH):
                cols = slice(b * SEQ, (b + 1) * SEQ)
                sp.dma_start(XT[:, cols], io["xT"][:, cols]).then_inc(s_x[b], 16)
                if b == 0:
                    for dst, src in (
                        (norm_w[:], io["norm_w"].rearrange("(p a) -> p a", a=1)),
                        (in_w[:], io["in_wT"][:, 0:D_IN]),
                        (conv_w[:], io["conv_w"].rearrange("(c p) k -> p c k", p=P)),
                        (conv_b[:], io["conv_b"].rearrange("(c p) -> p c", p=P)),
                        (xp_dt[:], io["xp_wT"].rearrange("(c p) n -> p c n", p=P)[:, :, 0:RANK]),
                        (dt_w[:], io["dt_wT"]),
                        (dt_b[:], io["dt_b"].rearrange("(c p) -> p c", p=P)),
                    ):
                        sp.dma_start(dst, src).then_inc(s_w, 16)
            sp.wait_ge(s_zero, 2)
            for col, src in ((0, RANK), (32, RANK), (64, RANK + NST), (96, RANK + NST)):
                sp.dma_start(xp_bc[:, :, col:col + NST],
                             io["xp_wT"].rearrange("(c p) n -> p c n", p=P)[:, :, src:src + NST]).then_inc(s_xp, 16)

        @block.gpsimd
        def _(pool):
            nc.gpsimd.memset(ones[:], 1.0 / P).then_inc(s_zero, 1)
            nc.gpsimd.memset(xp_bc[:], 0.0).then_inc(s_zero, 1)
            nc.gpsimd.memset(eps[:], EPS).then_inc(s_zero, 1)
            nc.gpsimd.memset(one[:], 1.0).then_inc(s_zero, 1)
            nc.gpsimd.memset(ident[:], 0.0).then_inc(s_id, 1)
            pool.wait_ge(s_id, 1)
            nc.gpsimd.affine_select(out=ident[:], in_=ident[:], compare_op=ALU.not_equal, fill=1.0, base=0,
                                    pattern=[[-1, P]], channel_multiplier=1).then_inc(s_id, 1)
            for c in range(2):
                for b in range(BATCH):
                    nc.gpsimd.memset(XB[:, c, b * pad:b * pad + TAPS - 1], 0.0).then_inc(s_zero, 1)

        @block.scalar
        def _(act):
            act.wait_ge(s_zero, 4)
            for i in range(NCH):
                act.wait_ge(s_x[i // 2], 16)
                nc.scalar.activation(chunk(R, i), chunk(XT, i), ACT.Square).then_inc(s_sq, 1)

            def ln_rms(i, k):
                act.wait_ge(s_ms, i + 1)
                nc.scalar.activation(chunk(R, i), ps_rms[k][:], ACT.Ln, bias=eps[:, 0:1]).then_inc(s_lnr, 1)
            twos(act, NCH, ln_rms)
            with act.Fori(0, NCH) as i:
                act.wait_ge(s_lnr, i + 1)
                nc.scalar.activation(chunk(R, i), chunk(R, i), ACT.Exp, scale=-0.5).then_inc(s_r, 1)
            with act.Fori(0, BATCH) as b:
                for h in range(2):
                    for c in range(2):
                        act.wait_ge(s_xps, b * 4 + h * 2 + c + 1)
                        nc.scalar.activation(XB[:, c, bass.ds(b * pad + TAPS - 1 + h * CH, CH)], ps_x[c][:],
                                             ACT.Copy).then_inc(s_xb, 1)
            for c in range(2):
                with act.Fori(0, NCH) as i:
                    act.wait_ge(s_cv, i + c * NCH + 1)
                    nc.scalar.activation(chunk2(U, c, i), chunk2(U, c, i), ACT.Silu).then_inc(s_u, 1)

            def high(i, k):
                act.wait_ge(s_bcps, i + 1)
                nc.scalar.activation(chunk(G, i), ps_bc[k][:], ACT.Copy).then_inc(s_hi, 1)
                act.wait_ge(s_dlps, i + 1)
                nc.scalar.activation(chunk(dt_low, i), ps_rms[k][0:RANK, :], ACT.Copy).then_inc(s_dl, 1)
            twos(act, NCH, high)
            act.wait_ge(s_cv, 2 * NCH)
            with act.Fori(0, NCH) as i:
                for c in range(2):
                    act.wait_ge(s_rel, i * 2 + c + 1)
                    nc.scalar.activation(chunk2(E, c, i), ps_dt[c][:], ACT.Abs, bias=dt_b[:, c:c + 1]).then_inc(s_abs, 1)
            with act.Fori(0, NCH) as i:
                for c in range(2):
                    act.wait_ge(s_abs, i * 2 + c + 1)
                    nc.scalar.activation(chunk2(E, c, i), chunk2(E, c, i), ACT.Exp, scale=-1.0).then_inc(s_e, 1)
            act.wait_ge(s_xn, NCH)
            for c in range(2):
                with act.Fori(0, NCH) as i:
                    act.wait_ge(s_e, i * 2 + c + 1)
                    if c == 1:
                        act.wait_ge(s_c, i + NCH + 1)
                    nc.scalar.activation(chunk(R, i), chunk2(E, c, i), ACT.Ln, bias=one[:, 0:1]).then_inc(s_l, 1)

        @block.vector
        def _(dve):
            dve.wait_ge(s_w, 16 * 7)
            for b in range(BATCH):
                dve.wait_ge(s_x[b], 16)
            with dve.Fori(0, NCH) as i:
                dve.wait_ge(s_r, i + 1)
                nc.vector.scalar_tensor_tensor(out=chunk(XN, i), in0=chunk(XT, i), scalar=norm_w[:, 0:1],
                                               in1=chunk(R, i), op0=ALU.mult, op1=ALU.mult).then_inc(s_xn, 1)
            dve.wait_ge(s_zero, 4 + 2 * BATCH)
            for c in range(2):
                with dve.Fori(0, BATCH) as b:
                    for h in range(2):
                        dve.wait_ge(s_xb, b * 4 + h * 2 + c + 1)
                        src = lambda k: XB[:, c, bass.ds(b * pad + h * CH + k, CH)]
                        out = chunk2(U, c, b * 2 + h)
                        n = b * 6 + (c * 24 + h * 3)
                        nc.vector.tensor_scalar(out, src(0), conv_w[:, c, 0:1], conv_b[:, c:c + 1],
                                                ALU.mult, ALU.add).then_inc(s_tap, 1)
                        for k in range(1, TAPS):
                            dve.wait_ge(s_tap, n + k)
                            ins = nc.vector.scalar_tensor_tensor(out=out, in0=src(k), scalar=conv_w[:, c, k:k + 1],
                                                                 in1=out, op0=ALU.mult, op1=ALU.add)
                            ins.then_inc(s_cv if k == TAPS - 1 else s_tap, 1)
            def low(i, k):
                dve.wait_ge(s_hi, i + 1)
                for q in (32, 96):
                    part = G[q:q + 32, bass.ds(i * CH, CH)]
                    nc.vector.tensor_tensor(part, ps_bc[k][q:q + 32, :], part.bitcast(F32), ALU.subtract).then_inc(s_g, 1)
            twos(dve, NCH, low)
            with dve.Fori(0, NCH) as i:
                for c in range(2):
                    dve.wait_ge(s_dtps, i * 2 + c + 1)
                    nc.vector.tensor_scalar(chunk2(DT, c, i), ps_dt[c][:], dt_b[:, c:c + 1], 0.0,
                                            ALU.add, ALU.max).then_inc(s_rel, 1)
            for c in range(2):
                with dve.Fori(0, NCH) as i:
                    dve.wait_ge(s_e, i * 2 + c + 1)
                    n = i * 2 + 2 * NCH * c
                    nc.vector.tensor_scalar(tmp[:, 0, :], chunk2(E, c, i), 1.0, -1.0, ALU.add, ALU.add).then_inc(s_tap, 1)
                    dve.wait_ge(s_tap, 48 + n + 1)
                    nc.vector.tensor_tensor(tmp[:, 1, :], chunk2(E, c, i), tmp[:, 0, :], ALU.subtract).then_inc(s_tap, 1)
                    dve.wait_ge(s_tap, 48 + n + 2)
                    dve.wait_ge(s_rel, i * 2 + c + 1)
                    nc.vector.tensor_tensor(chunk2(DT, c, i), chunk2(DT, c, i), tmp[:, 1, :], ALU.add).then_inc(s_c, 1)
                with dve.Fori(0, NCH) as i:
                    dve.wait_ge(s_l, c * NCH + i + 1)
                    dve.wait_ge(s_c, 2 * c * NCH + i + 1)
                    nc.vector.tensor_tensor(chunk2(DT, c, i), chunk2(DT, c, i), chunk(R, i), ALU.add).then_inc(s_c, 1)

        @block.tensor
        def _(pe):
            pe.wait_ge(s_zero, 3)

            def mean_square(i, k):
                pe.wait_ge(s_sq, i + 1)
                if past(i):
                    pe.wait_ge(s_lnr, i - 1)
                nc.tensor.matmul(ps_rms[k][:], ones[:], chunk(R, i), start=True, stop=True).then_inc(s_ms, 1)
            twos(pe, NCH, mean_square)
            pe.wait_ge(s_w, 16 * 7)

            def x_branch(i, k):
                pe.wait_ge(s_xn, i + 1)
                for c in range(2):
                    if past(i, 1):
                        pe.wait_ge(s_xb, i * 2 + c - 1)
                    nc.tensor.matmul(ps_x[c][:], in_w[:, c * P:(c + 1) * P], chunk(XN, i),
                                     start=True, stop=True).then_inc(s_xps, 1)
            twos(pe, NCH, x_branch)
            pe.wait_ge(s_xp, 16 * 4)
            pe.wait_ge(s_lnr, NCH)

            def x_proj(i, k):
                pe.wait_ge(s_u, i + NCH + 1)
                if past(i):
                    pe.wait_ge(s_g, i * 2 - 2)
                for c in range(2):
                    mm = nc.tensor.matmul(ps_bc[k][:], xp_bc[:, c, :], chunk2(U, c, i), start=c == 0, stop=c == 1)
                mm.then_inc(s_bcps, 1)
                if past(i):
                    pe.wait_ge(s_dl, i - 1)
                    pe.sem_inc(s_own, 1)
                for c in range(2):
                    mm = nc.tensor.matmul(ps_rms[k][0:RANK, :], xp_dt[:, c, :], chunk2(U, c, i),
                                          start=c == 0, stop=c == 1)
                mm.then_inc(s_dlps, 1)
            twos(pe, NCH, x_proj)

            def dt_proj(i, k):
                pe.wait_ge(s_dl, i + 1)
                for c in range(2):
                    if past(i, 1):
                        pe.wait_ge(s_abs, i * 2 + c - 1)
                        pe.sem_inc(s_own, 1)
                    nc.tensor.matmul(ps_dt[c][:], dt_w[:, c * P:(c + 1) * P], dt_low[:, bass.ds(i * CH, CH)],
                                     start=True, stop=True).then_inc(s_dtps, 1)
            twos(pe, NCH, dt_proj)


def mamba_scan(nc, io, keep):
    U, DT, G = keep["U"], keep["DT"], keep["G"]
    with ExitStack() as ctx:
        sb = lambda n, s, d=F32: ctx.enter_context(nc.sbuf_tensor("s_" + n, s, d))
        sem = lambda n: ctx.enter_context(nc.semaphore(n))
        bank = lambda n: ctx.enter_context(nc.psum_tensor(n, [P, CH], F32))
        sel = sb("sel", [P, 2 * NST, P], F32R)
        selw = sb("selw", [P, 2 * NST, P // 4])
        ident = keep["ident"]
        A = sb("A", [P, 2, NST])
        Dw = sb("D", [P, 2])
        DU = sb("DU", [P, 2, 2, CH])
        dA = sb("dA", [P, 2, 2, CH])
        H = sb("H", [P, 2, 2, CH])
        HC = sb("HC", [P, 2, 2, CH])
        C_sb = sb("C_sb", [P, 2, CH])
        last = sb("last", [P, 2, NST])
        ps_b = [bank(f"ps_b{k}") for k in range(2)]
        ps_d = [bank(f"ps_d{k}") for k in range(2)]
        ps_c = [bank(f"ps_c{k}") for k in range(2)]
        ps_y = [bank(f"ps_y{c}") for c in range(2)]
        s_w = sem("s_weights")
        s_sel0 = sem("s_sel_shape")
        s_sel = sem("s_sel")
        s_a = sem("s_A")
        s_b = sem("s_b_spread")
        s_c = sem("s_c_spread")
        s_da = sem("s_decay")
        s_cs = sem("s_c_copied")
        s_du = sem("s_dt_u")
        s_in = sem("s_input")
        s_h = sem("s_state")
        s_hl = sem("s_state_saved")
        s_hc = sem("s_c_times_state")
        s_y = sem("s_y_added")
        s_out = sem("s_y_out")
        s_own = sem("s_own_step")

        ctx.enter_context(nc.allow_non_contiguous_dma(reason="small per-feature vectors"))
        block = ctx.enter_context(nc.Block())
        N = NST

        @block.sync
        def _(sp):
            sp.dma_start(A[:], io["A_log"].rearrange("(c p) n -> p c n", p=P)).then_inc(s_w, 16)
            sp.dma_start(Dw[:], io["D"].rearrange("(c p) -> p c", p=P)).then_inc(s_w, 16)

        @block.gpsimd
        def _(pool):
            for used in keep["used"]:
                pool.sem_clear(used)
            nc.gpsimd.memset(selw[:], 0.0).then_inc(s_sel0, 1)
            for q in range(4):
                pool.wait_ge(s_sel0, q + 1)
                half = selw[:, (q // 2) * N:(q // 2 + 1) * N, :]
                nc.gpsimd.affine_select(out=half, in_=half, compare_op=ALU.not_equal, fill=1.0, base=-32 * q,
                                        pattern=[[-1, N], [0, P // 4]], channel_multiplier=1).then_inc(s_sel0, 1)

            def times_c(i, g):
                k = g % 2
                pool.wait_ge(s_cs, i * N + g + 1)
                for c in range(2):
                    pool.wait_ge(s_h, i * 2 * N + 2 * g + c + 1)
                    if past(i, 1) or g >= 2:
                        pool.wait_ge(s_y, i * 2 * N + 2 * (g - 2) + c + 1)
                    nc.gpsimd.tensor_tensor(HC[:, k, c, :], H[:, k, c, :], C_sb[:, k, :], ALU.mult).then_inc(s_hc, 1)
            for g in range(N):
                times_c(0, g)
            with pool.Fori(1, NCH) as i:
                for g in range(N):
                    times_c(i, g)

        @block.scalar
        def _(act):
            act.wait_ge(s_w, 32)
            nc.scalar.activation(A[:], A[:], ACT.Exp).then_inc(s_a, 1)
            act.wait_ge(s_a, 2)

            def chunk_of(i):
                for g in range(N):
                    k = g % 2
                    for c in range(2):
                        if past(i, 1) or g >= 2:
                            act.wait_ge(s_h, i * 2 * N + 2 * (g - 2) + c + 1)
                            act.sem_inc(s_own, 1)
                        nc.scalar.activation(dA[:, k, c, :], chunk2(DT, c, i), ACT.Exp,
                                             scale=A[:, c, g:g + 1]).then_inc(s_da, 1)
                    act.wait_ge(s_c, i * N + g + 1)
                    if past(i, 1) or g >= 2:
                        act.wait_ge(s_hc, i * 2 * N + 2 * (g - 1))
                    nc.scalar.activation(C_sb[:, k, :], ps_c[k][:], ACT.Copy).then_inc(s_cs, 1)
            chunk_of(0)
            with act.Fori(1, NCH) as i:
                chunk_of(i)

        @block.vector
        def _(dve):
            dve.wait_ge(s_sel0, 5)
            for q in range(4):
                nc.vector.tensor_copy(sel[:, :, q * 32:(q + 1) * 32], selw[:]).then_inc(s_sel, 1)
            dve.wait_ge(s_a, 1)
            nc.vector.tensor_scalar(A[:], A[:], -1.0, None, ALU.mult).then_inc(s_a, 1)
            dve.wait_ge(s_w, 32)

            def chunk_of(b, h):
                i = b * 2 + h
                for c in range(2):
                    nc.vector.tensor_tensor(DU[:, h, c, :], chunk2(DT, c, i), chunk2(U, c, i), ALU.mult).then_inc(s_du, 1)
                for g in range(N):
                    k = g % 2
                    dve.wait_ge(s_b, i * N + g + 1)
                    for c in range(2):
                        if g == 0:
                            dve.wait_ge(s_du, i * 2 + c + 1)
                        if past(i, 1) or g >= 2:
                            dve.wait_ge(s_h, i * 2 * N + 2 * (g - 2) + c + 1)
                        nc.vector.tensor_tensor((ps_d[k] if c == 0 else ps_b[k])[:], DU[:, h, c, :], ps_b[k][:],
                                                ALU.mult).then_inc(s_in, 1)
                    for c in range(2):
                        n = i * 2 * N + 2 * g + c
                        dve.wait_ge(s_in, n + 1)
                        dve.wait_ge(s_da, n + 1)
                        if past(i, 1) or g >= 2:
                            dve.wait_ge(s_hc, n - 3)
                            dve.wait_ge(s_hl, n - 3)
                        if h == 1:
                            dve.wait_ge(s_hl, n - 2 * N + 1)
                        nc.vector.tensor_tensor_scan(H[:, k, c, :], dA[:, k, c, :], (ps_d[k] if c == 0 else ps_b[k])[:],
                                                     last[:, c, g:g + 1] if h else 0.0, ALU.mult, ALU.add).then_inc(s_h, 1)
                    for c in range(2):
                        n = i * 2 * N + 2 * g + c
                        dve.wait_ge(s_h, n + 1)
                        nc.vector.tensor_copy(last[:, c, g:g + 1], H[:, k, c, CH - 1:CH]).then_inc(s_hl, 1)
                for c in range(2):
                    dve.wait_ge(s_y, i * 2 * N + 2 * N - 1 + c)
                    nc.vector.scalar_tensor_tensor(out=chunk2(U, c, i), in0=chunk2(U, c, i), scalar=Dw[:, c:c + 1],
                                                   in1=ps_y[c][:], op0=ALU.mult, op1=ALU.add).then_inc(s_out, 1)
            chunk_of(0, 0)
            chunk_of(0, 1)
            with dve.Fori(1, BATCH) as b:
                for h in range(2):
                    chunk_of(b, h)

        @block.tensor
        def _(pe):
            pe.wait_ge(s_sel, 4)

            def spread(i, g):
                k = g % 2
                if past(i, 1) or g >= 2:
                    pe.wait_ge(s_h, i * 2 * N + 2 * (g - 1))
                nc.tensor.matmul(ps_b[k][:], sel[:, g, :], chunk(G, i), start=True, stop=True).then_inc(s_b, 1)
                if past(i, 1) or g >= 2:
                    pe.wait_ge(s_cs, i * N + g - 1)
                nc.tensor.matmul(ps_c[k][:], sel[:, N + g, :], chunk(G, i), start=True, stop=True).then_inc(s_c, 1)

            def add(i, g):
                for c in range(2):
                    pe.wait_ge(s_hc, i * 2 * N + 2 * g + c + 1)
                    if g == 0 and past(i, 1):
                        pe.wait_ge(s_out, i * 2 - 1 + c)
                    nc.tensor.matmul(ps_y[c][:], ident[:], HC[:, g % 2, c, :], start=g == 0, stop=g == N - 1).then_inc(s_y, 1)

            def chunk_of(i):
                for g in range(N + 1):
                    if g < N:
                        spread(i, g)
                    if g > 0:
                        add(i, g - 1)
            chunk_of(0)
            with pe.Fori(1, NCH) as i:
                chunk_of(i)


def mamba_back(nc, io, keep):
    XN, U, XT, X1 = keep["XN"], keep["U"], keep["XT"], keep["X1"]
    ones, eps = keep["ones"], keep["eps"]
    with ExitStack() as ctx:
        sb = lambda n, s, d=F32: ctx.enter_context(nc.sbuf_tensor("k_" + n, s, d))
        sem = lambda n: ctx.enter_context(nc.semaphore(n))
        bank = lambda n: ctx.enter_context(nc.psum_tensor(n, [P, CH], F32))
        z_w = sb("z_w", [P, D_IN])
        out_w = sb("out_w", [P, 2, P])
        norm_w = sb("norm_w", [P, 1])
        SZ = sb("SZ", [P, 2, T])
        SQ, R = SZ[:, 0, :], SZ[:, 1, :]
        ps_z = [bank(f"k_ps_z{c}") for c in range(2)]
        ps_o = [bank(f"k_ps_o{k}") for k in range(2)]
        ps_m = [bank(f"k_ps_m{k}") for k in range(2)]
        ps_v = [bank(f"k_ps_v{k}") for k in range(2)]
        s_w = sem("k_weights")
        s_z = sem("k_z_psum")
        s_sz = sem("k_silu_z")
        s_g = sem("k_gated")
        s_o = sem("k_out_psum")
        s_t = sem("k_out")
        s_sq = sem("k_squares")
        s_m = sem("k_mean")
        s_ln = sem("k_ln")
        s_r = sem("k_inv")
        s_n = sem("k_dve")

        ctx.enter_context(nc.allow_non_contiguous_dma(reason="small per-feature vectors"))
        block = ctx.enter_context(nc.Block())

        @block.sync
        def _(sp):
            sp.dma_start(z_w[:], io["in_wT"][:, D_IN:2 * D_IN]).then_inc(s_w, 16)
            sp.dma_start(out_w[:], io["out_wT"].rearrange("(c p) n -> p c n", p=P)).then_inc(s_w, 16)
            sp.dma_start(norm_w[:], io["norm_f_w"].rearrange("(p a) -> p a", a=1)).then_inc(s_w, 16)

        @block.scalar
        def _(act):
            with act.Fori(0, NCH) as i:
                for c in range(2):
                    act.wait_ge(s_z, i * 2 + c + 1)
                    nc.scalar.activation(chunk2(SZ, c, i), ps_z[c][:], ACT.Silu).then_inc(s_sz, 1)
            act.wait_ge(s_g, 2 * NCH)
            with act.Fori(0, NCH) as i:
                act.wait_ge(s_t, i + 1)
                nc.scalar.activation(chunk(SQ, i), chunk(X1, i), ACT.Square).then_inc(s_sq, 1)
            for r in range(2):
                def ln(i, k):
                    act.wait_ge(s_m, i + r * NCH + 1)
                    if r:
                        act.wait_ge(s_n, i + 1)
                    nc.scalar.activation(chunk(R, i), (ps_m, ps_v)[r][k][:], ACT.Ln, bias=eps[:, 0:1]).then_inc(s_ln, 1)
                twos(act, NCH, ln)
                with act.Fori(0, NCH) as i:
                    act.wait_ge(s_ln, i + r * NCH + 1)
                    nc.scalar.activation(chunk(R, i), chunk(R, i), ACT.Exp, scale=-0.5).then_inc(s_r, 1)
                if r == 0:
                    with act.Fori(0, NCH) as i:
                        act.wait_ge(s_n, i + 2 * NCH + 1)
                        nc.scalar.activation(chunk(SQ, i), chunk(X1, i), ACT.Square).then_inc(s_sq, 1)

        @block.vector
        def _(dve):
            for c in range(2):
                with dve.Fori(0, NCH) as i:
                    dve.wait_ge(s_sz, i * 2 + c + 1)
                    nc.vector.tensor_tensor(chunk2(U, c, i), chunk2(U, c, i), chunk2(SZ, c, i), ALU.mult).then_inc(s_g, 1)

            def residual(i, k):
                dve.wait_ge(s_o, i + 1)
                nc.vector.tensor_tensor(chunk(X1, i), ps_o[k][:], chunk(XT, i), ALU.add).then_inc(s_t, 1)
            twos(dve, NCH, residual)
            dve.wait_ge(s_w, 48)
            with dve.Fori(0, NCH) as i:
                dve.wait_ge(s_r, i + 1)
                dve.wait_ge(s_sq, i + 1)
                nc.vector.scalar_tensor_tensor(out=chunk(X1, i), in0=chunk(X1, i), scalar=norm_w[:, 0:1],
                                               in1=chunk(R, i), op0=ALU.mult, op1=ALU.mult).then_inc(s_n, 1)
            with dve.Fori(0, NCH) as i:
                dve.wait_ge(s_n, i + 1)
                nc.vector.tensor_tensor(chunk(X1, i), chunk(X1, i), chunk(XT, i), ALU.add).then_inc(s_n, 1)

            def centre(i, k):
                dve.wait_ge(s_o, i + NCH + 1)
                nc.vector.tensor_tensor(chunk(X1, i), chunk(X1, i), ps_o[k][:], ALU.subtract).then_inc(s_n, 1)
            twos(dve, NCH, centre)
            with dve.Fori(0, NCH) as i:
                dve.wait_ge(s_r, i + NCH + 1)
                nc.vector.tensor_tensor(chunk(X1, i), chunk(X1, i), chunk(R, i), ALU.mult).then_inc(s_n, 1)

        @block.tensor
        def _(pe):
            pe.wait_ge(s_w, 48)

            def z_proj(i, k):
                for c in range(2):
                    if past(i, 1):
                        pe.wait_ge(s_sz, i * 2 + c - 1)
                    nc.tensor.matmul(ps_z[c][:], z_w[:, c * P:(c + 1) * P], chunk(XN, i), start=True, stop=True).then_inc(s_z, 1)
            twos(pe, NCH, z_proj)

            def out_proj(i, k):
                pe.wait_ge(s_g, i + NCH + 1)
                if past(i):
                    pe.wait_ge(s_t, i - 1)
                for c in range(2):
                    mm = nc.tensor.matmul(ps_o[k][:], out_w[:, c, :], chunk2(U, c, i), start=c == 0, stop=c == 1)
                mm.then_inc(s_o, 1)
            twos(pe, NCH, out_proj)

            def mean_square(i, k):
                pe.wait_ge(s_sq, i + 1)
                if past(i):
                    pe.wait_ge(s_ln, i - 1)
                nc.tensor.matmul(ps_m[k][:], ones[:], chunk(SQ, i), start=True, stop=True).then_inc(s_m, 1)
            twos(pe, NCH, mean_square)

            def mean(i, k):
                pe.wait_ge(s_n, i + NCH + 1)
                if past(i):
                    pe.wait_ge(s_n, i + 2 * NCH - 1)
                nc.tensor.matmul(ps_o[k][:], ones[:], chunk(X1, i), start=True, stop=True).then_inc(s_o, 1)
            twos(pe, NCH, mean)

            def variance(i, k):
                pe.wait_ge(s_sq, i + NCH + 1)
                if past(i):
                    pe.wait_ge(s_ln, i + NCH - 1)
                nc.tensor.matmul(ps_v[k][:], ones[:], chunk(SQ, i), start=True, stop=True).then_inc(s_m, 1)
            twos(pe, NCH, variance)


def mamba(nc, io, keep):
    with ExitStack() as ctx:
        sb = lambda n, s, d=F32: ctx.enter_context(nc.sbuf_tensor("m_" + n, s, d))
        own = dict(keep, used=[], XT=sb("XT", [P, T]), XN=sb("XN", [P, T]), U=sb("U", [P, 2, T]))
        with ExitStack() as inner:
            sb = lambda n, s, d=F32: inner.enter_context(nc.sbuf_tensor("m_" + n, s, d))
            own.update(DT=sb("DT", [P, 2, T]), G=sb("G", [P, T], F32R))
            mamba_front(nc, io, own)
            mamba_scan(nc, io, own)
        mamba_back(nc, io, own)


NT = T // P
PER = CH // P


E0 = 8
HID = 512
HM = HID // P
BIG = 1e30


def wide(ap, n):
    return ap.unsqueeze(2).broadcast_to([ap.shape[0], ap.shape[1], n])


def row_wide(ap, n):
    return ap.unsqueeze(1).broadcast_to([ap.shape[0], n, ap.shape[1]])


def ffn(nc, io, keep):
    X1, X2, X2t, ident, eps = keep["X1"], keep["X2"], keep["X2t"], keep["ident"], keep["eps"]
    with ExitStack() as ctx:
        sb = lambda n, s, d=F32: ctx.enter_context(nc.sbuf_tensor("f_" + n, s, d))
        sem = lambda n: ctx.enter_context(nc.semaphore("f_" + n))
        bank = lambda n: ctx.enter_context(nc.psum_tensor("f_" + n, [P, CH], F32))
        ACC = X2t
        X1t = sb("X1t", [P, NT, P])
        stage = sb("stage", [P, 2, CH])
        gate_w = sb("gate_w", [P, E0])
        sh_w = sb("sh_w", [P, P])
        sh_b = sb("sh_b", [1, PER, P])
        ones_row = sb("ones_row", [1, P])
        b2big = sb("b2big", [P, NT // 2, P])
        gamma = sb("gamma", [P, P])
        beta = sb("beta", [P, P])
        L = sb("L", [P, NT, E0])
        iota_i = sb("iota_i", [P, NT, E0], I32)
        iota = sb("iota", [P, NT, E0])
        oh = sb("oh", [P, 2, NT, E0])
        eq = sb("eq", [P, NT, E0])
        top = sb("top", [P, 2, NT])
        idx = sb("idx", [P, 2, NT])
        wt = sb("wt", [P, 3, NT])
        comb = sb("comb", [P, NT, E0])
        combE = sb("combE", [P, E0 * NT])
        combT = sb("combT", [P, 2, P])
        w1 = sb("w1", [P, 2, HID])
        w2 = sb("w2", [P, 2, HM, P])
        b1 = sb("b1", [P, 2, HM])
        HT = sb("HT", [P, 2, HM, CH])
        stats = sb("stats", [P, NT, 6])
        mv = sb("mv", [P, NT, 2])
        rstd = sb("rstd", [P, NT])
        ps_h = [bank(f"ps_h{m}") for m in range(HM)]
        ps_y = [bank(f"ps_y{k}") for k in range(2)]
        ps_t = [bank(f"ps_t{k}") for k in range(2)]
        s_w, s_b2, s_z, s_st, s_g, s_sh, s_tr = (sem(n) for n in ("weights", "b2_loaded", "zeroed", "staged", "logits", "shared", "transposed"))
        s_l, s_gelu, s_x1t, s_rt, s_exp, s_ct, s_ctc, s_b2m = (sem(n) for n in ("logits_copied", "shared_gelu", "x_token_major", "route", "gate_exp", "comb_t", "comb_t_copied", "b2_sum"))
        s_acc = sem("acc")
        s_ew = [sem(f"expert_weights{k}") for k in range(2)]
        s_h, s_ht, s_y = sem("hidden"), sem("hidden_gelu"), sem("expert_out")
        s_ln, s_sq, s_fin, s_x2 = sem("norm"), sem("norm_sqrt"), sem("x2_token_major"), sem("x2_transposed")

        ctx.enter_context(nc.allow_non_contiguous_dma(reason="small per-feature vectors"))
        block = ctx.enter_context(nc.Block())

        @block.sync
        def _(sp):
            for dst, src in (
                (gate_w[:], io["gate_w"]), (sh_w[:], io["sh_w"]),
                (sh_b[:], io["sh_b"].rearrange("(a b n) -> a b n", a=1, b=1).broadcast_to([1, PER, P])),
                (gamma[:], io["gamma"].rearrange("(a n) -> a n", a=1).broadcast_to([P, P])),
                (beta[:], io["beta"].rearrange("(a n) -> a n", a=1).broadcast_to([P, P])),
            ):
                sp.dma_start(dst, src).then_inc(s_w, 16)
            sp.wait_ge(s_z, 1)
            for t in range(NT // 2):
                sp.dma_start(b2big[t * E0:(t + 1) * E0, t, :], io["b2"]).then_inc(s_b2, 16)

            def weights(e, k):
                if past(e):
                    sp.wait_ge(s_y, (e - 1) * NCH)
                one_e = bass.ds(e, 1)
                sp.dma_start(w1[:, k, :], io["W1"][one_e].rearrange("a p n -> p (a n)")).then_inc(s_ew[k], 16)
                sp.dma_start(w2[:, k, :, :], io["W2"][one_e].rearrange("a (m p) n -> p (a m) n", p=P)).then_inc(s_ew[k], 16)
                sp.dma_start(b1[:, k, :], io["b1T"][one_e].rearrange("a p m -> p (a m)")).then_inc(s_ew[k], 16)
            twos(sp, E0, weights)

        @block.gpsimd
        def _(pool):
            nc.gpsimd.memset(b2big[:], 0.0).then_inc(s_z, 1)
            nc.gpsimd.memset(ones_row[:], 1.0).then_inc(s_z, 1)
            nc.gpsimd.iota(iota_i[:], pattern=[[0, NT], [1, E0]], base=0, channel_multiplier=0).then_inc(s_z, 1)

            def stage_in(i, k):
                if past(i):
                    pool.wait_ge(s_tr, i - 1)
                nc.gpsimd.tensor_copy(stage[:, k, :], chunk(X1, i)).then_inc(s_st, 1)
            twos(pool, NCH, stage_in)

        @block.scalar
        def _(act):
            def shared(i, k):
                act.wait_ge(s_sh, i + 1)
                nc.scalar.activation(ACC[:, bass.ds(i * PER, PER), :].rearrange("p t n -> p (t n)"), ps_y[k][:], ACT.Gelu).then_inc(s_gelu, 1)
                act.wait_ge(s_tr, i + 1)
                nc.scalar.activation(X1t[:, bass.ds(i * PER, PER), :].rearrange("p t n -> p (t n)"), ps_t[k][:], ACT.Copy).then_inc(s_x1t, 1)
            twos(act, NCH, shared)
            act.wait_ge(s_rt, 15)
            nc.scalar.activation(wt[:, 2, :], wt[:, 0, :], ACT.Exp).then_inc(s_exp, 1)

            def hidden(e, i, ke, k):
                g = e * NCH + i
                for m in range(HM):
                    act.wait_ge(s_h, g * HM + m + 1)
                    if past(e, 1) or past(i):
                        act.wait_ge(s_y, g - 1)
                    nc.scalar.activation(HT[:, k, m, :], ps_h[m][:], ACT.Gelu, bias=b1[:, ke, m:m + 1]).then_inc(s_ht, 1)
            twos(act, NCH, lambda i, k: hidden(0, i, 0, k))
            with act.Fori(0, NCH // 2) as j:
                for k in range(2):
                    hidden(1, j * 2 + k, 1, k)
            with act.Fori(1, E0 // 2) as ep:
                for ke in range(2):
                    with act.Fori(0, NCH // 2) as j:
                        for k in range(2):
                            hidden(ep * 2 + ke, j * 2 + k, ke, k)
            for r in range(2):
                act.wait_ge(s_ln, r * (3 * NT + 2 + 3) + 2 * NT + 1)
                nc.scalar.activation(rstd[:], rstd[:], ACT.Sqrt).then_inc(s_sq, 1)

            def x2_copy(i, k):
                act.wait_ge(s_x2, i + 1)
                nc.scalar.activation(chunk(X2, i), ps_t[k][:], ACT.Copy).then_inc(s_fin, 1)
            twos(act, NCH, x2_copy)

        @block.vector
        def _(dve):
            def logits(i, k):
                dve.wait_ge(s_g, i + 1)
                nc.vector.tensor_copy(L[:, bass.ds(i * PER, PER), :].rearrange("p t e -> p (t e)"), ps_h[k][:, 0:PER * E0]).then_inc(s_l, 1)
            twos(dve, NCH, logits)
            dve.wait_ge(s_z, 3)
            nc.vector.tensor_copy(iota[:], iota_i[:]).then_inc(s_rt, 1)
            dve.wait_ge(s_l, NCH)
            dve.wait_ge(s_rt, 1)
            n = 1
            for r in range(2):
                nc.vector.tensor_reduce(top[:, r, :], L[:], AX.X, ALU.max).then_inc(s_rt, 1)
                dve.wait_ge(s_rt, n + 1)
                nc.vector.tensor_tensor(eq[:], L[:], wide(top[:, r, :], E0), ALU.is_equal).then_inc(s_rt, 1)
                dve.wait_ge(s_rt, n + 2)
                nc.vector.scalar_tensor_tensor(out=eq[:], in0=eq[:], scalar=-float(E0), in1=iota[:], op0=ALU.mult, op1=ALU.add).then_inc(s_rt, 1)
                dve.wait_ge(s_rt, n + 3)
                nc.vector.tensor_reduce(idx[:, r, :], eq[:], AX.X, ALU.min).then_inc(s_rt, 1)
                dve.wait_ge(s_rt, n + 4)
                nc.vector.tensor_scalar(idx[:, r, :], idx[:, r, :], float(E0), None, ALU.add).then_inc(s_rt, 1)
                dve.wait_ge(s_rt, n + 5)
                nc.vector.tensor_tensor(oh[:, r], iota[:], wide(idx[:, r, :], E0), ALU.is_equal).then_inc(s_rt, 1)
                n += 6
                dve.wait_ge(s_rt, n)
                if r == 0:
                    nc.vector.scalar_tensor_tensor(out=L[:], in0=oh[:, 0], scalar=-BIG, in1=L[:], op0=ALU.mult, op1=ALU.add).then_inc(s_rt, 1)
                    n += 1
                    dve.wait_ge(s_rt, n)
            nc.vector.tensor_tensor(wt[:, 0, :], top[:, 1, :], top[:, 0, :], ALU.subtract).then_inc(s_rt, 1)
            dve.wait_ge(s_exp, 1)
            nc.vector.tensor_scalar(wt[:, 0, :], wt[:, 2, :], 1.0, None, ALU.add).then_inc(s_rt, 1)
            dve.wait_ge(s_rt, 16)
            nc.vector.reciprocal(wt[:, 1, :], wt[:, 0, :]).then_inc(s_rt, 1)
            dve.wait_ge(s_rt, 17)
            nc.vector.tensor_tensor(wt[:, 2, :], wt[:, 2, :], wt[:, 1, :], ALU.mult).then_inc(s_rt, 1)
            dve.wait_ge(s_rt, 18)
            for r in range(2):
                nc.vector.tensor_tensor(oh[:, r], oh[:, r], wide(wt[:, 1 + r, :], E0), ALU.mult).then_inc(s_rt, 1)
            dve.wait_ge(s_rt, 20)
            nc.vector.tensor_tensor(comb[:], oh[:, 0], oh[:, 1], ALU.add).then_inc(s_rt, 1)
            dve.wait_ge(s_rt, 21)
            nc.vector.tensor_copy(combE[:].rearrange("p (e t) -> p e t", e=E0), comb[:].rearrange("p t e -> p e t")).then_inc(s_rt, 1)
            for h in range(2):
                dve.wait_ge(s_ct, h + 1)
                nc.vector.tensor_copy(combT[:, h, :], ps_t[h][:, 0:P]).then_inc(s_ctc, 1)
            dve.wait_ge(s_gelu, NCH)

            def start_acc(i, k):
                dve.wait_ge(s_b2m, i + 1)
                part = ACC[:, bass.ds(i * PER, PER), :].rearrange("p t n -> p (t n)")
                nc.vector.scalar_tensor_tensor(out=part, in0=part, scalar=0.5, in1=ps_y[k][:], op0=ALU.mult, op1=ALU.add).then_inc(s_acc, PER)
            twos(dve, NCH, start_acc)
            dve.wait_ge(s_rt, 22)

            def add_expert(e, i, k):
                g = e * NCH + i
                dve.wait_ge(s_y, g + 1)
                for t in range(PER):
                    dve.wait_ge(s_acc, g * PER + t + 1)
                    tile = ACC[:, bass.ds(i * PER + t, 1), :].rearrange("p a n -> p (a n)")
                    nc.vector.scalar_tensor_tensor(out=tile, in0=ps_y[k][:, t * P:(t + 1) * P],
                                                   scalar=combE[:, bass.ds(e * NT + i * PER + t, 1)], in1=tile,
                                                   op0=ALU.mult, op1=ALU.add).then_inc(s_acc, 1)
            with dve.Fori(0, E0) as e:
                with dve.Fori(0, NCH // 2) as j:
                    for k in range(2):
                        add_expert(e, j * 2 + k, k)
            dve.wait_ge(s_w, 16 * 5)
            dve.wait_ge(s_acc, NT * (E0 + 1))

            def norm(n):
                for t in range(NT):
                    nc.vector.bn_stats(stats[:, t, :], ACC[:, t, :]).then_inc(s_ln, 1)
                for t in range(NT):
                    dve.wait_ge(s_ln, n + t + 1)
                    nc.vector.bn_aggr(mv[:, t, :], stats[:, t, :]).then_inc(s_ln, 1)
                dve.wait_ge(s_ln, n + 2 * NT)
                nc.vector.tensor_scalar(rstd[:], mv[:, :, 1], EPS, None, ALU.add).then_inc(s_ln, 1)
                dve.wait_ge(s_sq, 1 if n == 0 else 2)
                nc.vector.reciprocal(rstd[:], rstd[:]).then_inc(s_ln, 1)
                dve.wait_ge(s_ln, n + 2 * NT + 2)
                for t in range(NT):
                    nc.vector.tensor_scalar(ACC[:, t, :], ACC[:, t, :], mv[:, t, 0:1], rstd[:, t:t + 1],
                                            ALU.subtract, ALU.mult).then_inc(s_ln, 1)
                dve.wait_ge(s_ln, n + 3 * NT + 2)
                return n + 3 * NT + 2
            n = norm(0)
            dve.wait_ge(s_x1t, NCH)
            for other, op in ((row_wide(gamma[:], NT), ALU.mult), (row_wide(beta[:], NT), ALU.add), (X1t[:], ALU.add)):
                nc.vector.tensor_tensor(ACC[:], ACC[:], other, op).then_inc(s_ln, 1)
                n += 1
                dve.wait_ge(s_ln, n)
            norm(n)

        @block.tensor
        def _(pe):
            pe.wait_ge(s_w, 16 * 5)
            pe.wait_ge(s_z, 2)

            def token_major(i, k):
                pe.wait_ge(s_st, i + 1)
                tiles = [stage[:, k, t * P:(t + 1) * P] for t in range(PER)]
                if past(i):
                    pe.wait_ge(s_l, i - 1)
                for t in range(PER):
                    mm = nc.tensor.matmul(ps_h[k][:, t * E0:(t + 1) * E0], tiles[t], gate_w[:], start=True, stop=True)
                mm.then_inc(s_g, 1)
                if past(i):
                    pe.wait_ge(s_gelu, i - 1)
                nc.tensor.matmul(ps_y[k][:], ones_row[:], sh_b[:].rearrange("a t n -> a (t n)"), start=True, stop=False)
                for t in range(PER):
                    mm = nc.tensor.matmul(ps_y[k][:, t * P:(t + 1) * P], tiles[t], sh_w[:], start=False, stop=t == PER - 1)
                mm.then_inc(s_sh, 1)
                if past(i):
                    pe.wait_ge(s_x1t, i - 1)
                for t in range(PER):
                    mm = nc.tensor.transpose(ps_t[k][:, t * P:(t + 1) * P], tiles[t], ident[:])
                mm.then_inc(s_tr, 1)
            twos(pe, NCH, token_major)
            pe.wait_ge(s_rt, 21)
            pe.wait_ge(s_x1t, NCH)
            for h in range(2):
                nc.tensor.transpose(ps_t[h][:, 0:P], comb[:, h * 16:(h + 1) * 16, :].rearrange("p t e -> p (t e)"), ident[:]).then_inc(s_ct, 1)
            pe.wait_ge(s_b2, 16 * NT // 2)
            pe.wait_ge(s_ctc, 2)
            pe.wait_ge(s_gelu, NCH)

            for i in range(NCH):
                if i >= 2:
                    pe.wait_ge(s_acc, PER * (i - 1))
                cols = b2big[:, (i % 4) * PER:(i % 4 + 1) * PER, :].rearrange("p t n -> p (t n)")
                nc.tensor.matmul(ps_y[i % 2][:], combT[:, i // 4, :], cols, start=True, stop=True).then_inc(s_b2m, 1)

            def up(e, i, ke):
                g = e * NCH + i
                for m in range(HM):
                    if past(e, 1) or past(i, 1):
                        pe.wait_ge(s_ht, g * HM + m - HM + 1)
                    nc.tensor.matmul(ps_h[m][:], w1[:, ke, m * P:(m + 1) * P], chunk(X1, i), start=True, stop=True).then_inc(s_h, 1)

            def down(e, i, ke, k):
                g = e * NCH + i
                pe.wait_ge(s_ht, g * HM + HM)
                pe.wait_ge(s_acc, g * PER + NT - PER)
                for t in range(PER):
                    for m in range(HM):
                        mm = nc.tensor.matmul(ps_y[k][:, t * P:(t + 1) * P], HT[:, k, m, t * P:(t + 1) * P], w2[:, ke, m, :],
                                              start=m == 0, stop=m == HM - 1)
                mm.then_inc(s_y, 1)

            def expert(e, ke, first, last):
                if first:
                    up(e, 1, ke)
                    down(e, 0, ke, 0)
                    up(e, 2, ke)
                    down(e, 1, ke, 1)
                with pe.Fori(1 if first else 0, NCH // 2 - 1) as j:
                    for k in range(2):
                        up(e, j * 2 + k + 1, ke)
                        down(e, j * 2 + k, ke, k)
                up(e, NCH - 1, ke)
                down(e, NCH - 2, ke, 0)
                if not last:
                    pe.wait_ge(s_ew[1 - ke], (e + 1 - (1 - ke)) * 24 + 48)
                    up(e + 1, 0, 1 - ke)
                down(e, NCH - 1, ke, 1)
            pe.wait_ge(s_ew[0], 48)
            up(0, 0, 0)
            expert(0, 0, True, False)
            expert(1, 1, False, False)
            with pe.Fori(1, E0 // 2 - 1) as ep:
                for ke in range(2):
                    expert(ep * 2 + ke, ke, False, False)
            expert(E0 - 2, 0, False, False)
            expert(E0 - 1, 1, False, True)

            for i in range(NCH):
                pe.wait_ge(s_ln, (3 * NT + 2 + 3) + 2 * NT + 2 + (i + 1) * PER)
                if i >= 2:
                    pe.wait_ge(s_fin, i - 1)
                for t in range(PER):
                    mm = nc.tensor.transpose(ps_t[i % 2][:, t * P:(t + 1) * P], ACC[:, i * PER + t, :], ident[:])
                mm.then_inc(s_x2, 1)


NH = 16
DK = 8
PARTS = 3
GH = 4
NG = NH // GH
QT = SEQ // P
ROWS = PARTS * PARTS * DK
MROW = ROWS
VW = 32
NEG = -1e30
BLOCKS = [(c, kt, max(kt - c * PER, 0)) for c in range(2) for kt in range((c + 1) * PER)]
ITEMS = [(j, qt, c) for j in range(GH) for c in range(2) for qt in range(c * PER, QT)]
NB, NI = len(BLOCKS), len(ITEMS)


E1 = 64
TOPK = 4
CAP = P
SLOTS = E1 * CAP


def attn_project(nc, io, keep, dram):
    X2, Vt = keep["X2"], keep["Vt"]
    with ExitStack() as ctx:
        sb = lambda n, s, d=F32: ctx.enter_context(nc.sbuf_tensor("p_" + n, s, d))
        sem = lambda n: ctx.enter_context(nc.semaphore("p_" + n))
        bank = lambda n: ctx.enter_context(nc.psum_tensor("p_" + n, [P, CH], F32))
        w = [sb(f"w{j}", [P, P]) for j in range(3)]
        bias = sb("bias", [P, 2])
        v_b = sb("v_b", [1, PER, P])
        ones_row = sb("ones_row", [1, P])
        stage = sb("stage", [P, 2, CH])
        zero = sb("zero", [P, 2 * CH], BF16)
        parts = sb("parts", [P, 2, PARTS, CH], BF16)
        rest = sb("rest", [P, 2, CH])
        ps = [bank(f"ps{k}") for k in range(2)]
        ps_v = [bank(f"ps_v{k}") for k in range(2)]
        s_w, s_z, s_zd, s_ps, s_p0, s_r, s_p1, s_p2 = (sem(n) for n in ("weights", "zeroed", "zeros_stored", "qk_psum", "part0", "rest", "part1", "part2"))
        s_st, s_v, s_vt = sem("staged"), sem("v_psum"), sem("v")
        s_d = [sem(f"stored{x}") for x in range(2)]

        ctx.enter_context(nc.allow_non_contiguous_dma(reason="small per-feature vectors"))
        block = ctx.enter_context(nc.Block())

        @block.sync
        def _(sp):
            for dst, src in (
                [(w[j][:].rearrange("p (h k) -> p h k", k=DK), io[n].rearrange("h d k -> d h k")) for j, n in enumerate(("Wq", "Wk", "Wv"))]
                + [(bias[:, j:j + 1], io[n].rearrange("h (k a) -> (h k) a", a=1)) for j, n in enumerate(("bq", "bk"))]
                + [(v_b[:], io["bv"].rearrange("(a b h) k -> a b (h k)", a=1, b=1).broadcast_to([1, PER, P]))]
            ):
                sp.dma_start(dst, src).then_inc(s_w, 16)
            sp.wait_ge(s_z, 2)
            rows = PARTS * GH
            sp.dma_start(dram["zeros"].rearrange("r (a n) -> (r a) n", a=GH), zero[0:rows, :]).then_inc(s_zd, 16)

            def store(i):
                for x in range(2):
                    sp.wait_ge(s_p2, i * 2 + x + 1)
                    for a in range(PARTS):
                        sp.dma_start(dram["qk"][x, a, :, bass.ds(i * CH, CH)], parts[:, x, a, :]).then_inc(s_d[x], 16)
            with sp.Fori(0, NCH) as i:
                store(i)
            for x in range(2):
                sp.wait_ge(s_d[x], 16 * PARTS * NCH)
            sp.wait_ge(s_zd, 16)

        @block.gpsimd
        def _(pool):
            nc.gpsimd.memset(ones_row[:], 1.0).then_inc(s_z, 1)
            nc.gpsimd.memset(zero[:], 0.0).then_inc(s_z, 1)

            def stage_in(i, k):
                if past(i):
                    pool.wait_ge(s_v, i - 1)
                nc.gpsimd.tensor_copy(stage[:, k, :], chunk(X2, i)).then_inc(s_st, 1)
            twos(pool, NCH, stage_in)

        @block.scalar
        def _(act):
            act.wait_ge(s_w, 16 * 6)

            def split(i, k):
                for x in range(2):
                    act.wait_ge(s_ps, i * 2 + x + 1)
                    if past(i, 1):
                        act.wait_ge(s_d[x], i * 16 * PARTS)
                    nc.scalar.activation(parts[:, x, 0, :], ps[x][:], ACT.Identity, bias=bias[:, x:x + 1]).then_inc(s_p0, 1)
                    act.wait_ge(s_r, i * 2 + x + 1)
                    nc.scalar.activation(parts[:, x, 1, :], rest[:, x, :], ACT.Copy).then_inc(s_p1, 1)
                act.wait_ge(s_v, i + 1)
                nc.scalar.activation(Vt[:, bass.ds(i * PER, PER), :].rearrange("p t n -> p (t n)"), ps_v[k][:], ACT.Copy).then_inc(s_vt, 1)
            twos(act, NCH, split)

        @block.vector
        def _(dve):
            dve.wait_ge(s_w, 16 * 6)

            def split(i, k):
                for x in range(2):
                    dve.wait_ge(s_p0, i * 2 + x + 1)
                    if past(i, 1):
                        dve.wait_ge(s_p2, i * 2 + x - 1)
                    nc.vector.scalar_tensor_tensor(out=rest[:, x, :], in0=ps[x][:], scalar=bias[:, x:x + 1], in1=parts[:, x, 0, :],
                                                   op0=ALU.add, op1=ALU.subtract).then_inc(s_r, 1)
                for x in range(2):
                    dve.wait_ge(s_p1, i * 2 + x + 1)
                    nc.vector.tensor_tensor(parts[:, x, 2, :], rest[:, x, :], parts[:, x, 1, :], ALU.subtract).then_inc(s_p2, 1)
            twos(dve, NCH, split)

        @block.tensor
        def _(pe):
            pe.wait_ge(s_w, 16 * 6)
            pe.wait_ge(s_z, 1)

            def project(i, k):
                for x in range(2):
                    if past(i, 1):
                        pe.wait_ge(s_r, i * 2 + x - 1)
                    nc.tensor.matmul(ps[x][:], w[x][:], chunk(X2, i), start=True, stop=True).then_inc(s_ps, 1)
                pe.wait_ge(s_st, i + 1)
                if past(i):
                    pe.wait_ge(s_vt, i - 1)
                nc.tensor.matmul(ps_v[k][:], ones_row[:], v_b[:].rearrange("a t n -> a (t n)"), start=True, stop=False)
                for t in range(PER):
                    mm = nc.tensor.matmul(ps_v[k][:, t * P:(t + 1) * P], stage[:, k, t * P:(t + 1) * P], w[2][:], start=False, stop=t == PER - 1)
                mm.then_inc(s_v, 1)
            twos(pe, NCH, project)


def attn_scores(nc, io, keep, dram):
    Vt, CX, ident = keep["Vt"], keep["CX"], keep["ident"]
    with ExitStack() as ctx:
        sb = lambda n, s, d=F32: ctx.enter_context(nc.sbuf_tensor("t_" + n, s, d))
        sem = lambda n: ctx.enter_context(nc.semaphore("t_" + n))
        bank = lambda n, m=1: ctx.enter_context(nc.psum_tensor("t_" + n, [P, m * CH], F32))
        Q = [sb(f"Q{g}", [P, GH, SEQ], BF16) for g in range(NG)]
        K = [sb(f"K{g}", [P, GH, SEQ], BF16) for g in range(NG)]
        VG = sb("VG", [P, 2, QT, GH * VW])
        PT = sb("PT", [P, 2, GH, CH])
        CT = sb("CT", [P, 2, CH])
        den = sb("den", [P, 2, PER, GH])
        negm = sb("negm", [P, 2, GH, QT])
        negm2 = sb("negm2", [P, 2, GH, PER])
        msb = sb("msb", [GH * QT, P])
        mrest = sb("mrest", [GH * QT, P])
        mp = sb("mp", [GH * QT, 2, PARTS, P], BF16)
        maskf = sb("maskf", [P, P])
        mask = sb("mask", [P, P], BF16)
        identb = sb("identb", [P, P], BF16)
        ps_1 = [bank(f"ps_1{k}") for k in range(2)]
        ps_s = [bank(f"ps_s{p}", 2) for p in range(2)]
        ps_c = [bank(f"ps_c{c}") for c in range(2)]
        s_z, s_m, s_mb = sem("zeroed"), sem("mask_f32"), sem("mask")
        s_ld = [sem(f"loaded{g}") for g in range(NG)]
        s_ms = [sem(f"max_stored{g}") for g in range(NG)]
        s_ml = [sem(f"max_loaded{g}") for g in range(NG)]
        s_p1, s_mx, s_cmb, s_mt, s_mc, s_mp = (sem(n) for n in ("scores1", "maxed", "max_joined", "max_transposed", "max_copied", "max_parts"))
        s_st, s_exp, s_mk, s_pv, s_vg = (sem(n) for n in ("scores2", "exped", "masked", "context", "v_group"))
        s_ev, s_ct, s_cx = sem("context_copied"), sem("context_transposed"), sem("normed")
        s_pool, s_sp = sem("pool_step"), sem("sync_step")
        s_dr, s_mq = sem("reciprocal"), sem("max_chain")
        AHEAD = 2

        ctx.enter_context(nc.allow_non_contiguous_dma(reason="rows of heads"))
        block = ctx.enter_context(nc.Block())

        def batches(eng, body):
            with eng.Fori(0, BATCH - 1) as b:
                body(b, False)
            body(BATCH - 1, True)

        @block.sync
        def _(sp):
            def load(b, g):
                heads = lambda x, a: dram["qk"][x, a, g * GH * DK:(g + 1) * GH * DK, bass.ds(b * SEQ, SEQ)].rearrange("(j d) t -> d j t", d=DK)
                for a in range(PARTS):
                    for c in range(PARTS):
                        r = (a * PARTS + c) * DK
                        sp.dma_start(Q[g][r:r + DK], heads(0, a)).then_inc(s_ld[g], 16)
                        sp.dma_start(K[g][r:r + DK], heads(1, c)).then_inc(s_ld[g], 16)
                sp.dma_start(Q[g][MROW:MROW + PARTS].rearrange("r j t -> r (j t)"), dram["zeros"]).then_inc(s_ld[g], 16)

            def maxima(b, g):
                gi = b * NG + g
                sp.wait_ge(s_mp, gi + 2)
                for a in range(PARTS):
                    sp.dma_start(dram["max"][g, a].rearrange("(r n) -> r n", n=P), mp[:, g % 2, a, :]).then_inc(s_ms[g], 16)
                sp.wait_ge(s_ms[g], b * 16 * PARTS + 16 * PARTS)
                sp.wait_ge(s_p1, gi * NI + NI)
                sp.dma_start(Q[g][MROW:MROW + PARTS].rearrange("r j t -> r (j t)"), dram["max"][g]).then_inc(s_ml[g], 16)

            sp.wait_ge(s_z, 2 * NG)
            for g in range(NG):
                load(0, g)
            maxima(0, 0)

            def body(b, last):
                for g in range(NG):
                    gi = b * NG + g
                    if not (last and g == NG - 1):
                        maxima(b + (g + 1) // NG, (g + 1) % NG)
                    if not last:
                        sp.wait_ge(s_st, gi * 2 * NB + 2 * NB)
                        sp.sem_inc(s_sp, 1)
                        sp.wait_ge(s_ml[g], b * 16 + 16)
                        load(b + 1, g)
            batches(sp, body)

        @block.gpsimd
        def _(pool):
            for g in range(NG):
                nc.gpsimd.memset(Q[g][:].rearrange("p j t -> p (j t)").bitcast(F32), 0.0).then_inc(s_z, 1)
                nc.gpsimd.memset(K[g][:].rearrange("p j t -> p (j t)"), 1.0).then_inc(s_z, 1)
            nc.gpsimd.memset(VG[:].rearrange("p k t n -> p (k t n)"), 0.0).then_inc(s_m, 1)
            nc.gpsimd.memset(maskf[:], 0.0).then_inc(s_m, 1)
            pool.wait_ge(s_m, 2)
            nc.gpsimd.affine_select(out=maskf[:], in_=maskf[:], compare_op=ALU.is_ge, fill=NEG, base=0,
                                    pattern=[[-1, P]], channel_multiplier=1).then_inc(s_m, 1)
            nc.gpsimd.memset(VG[:].rearrange("p k t (j n) -> p (k t j) n", n=VW)[:, :, DK:DK + 1], 1.0).then_inc(s_m, 1)
            pool.wait_ge(s_m, 4)

            def v_group(b, g):
                gi = b * NG + g
                if past(gi, 1):
                    pool.wait_ge(s_pv, gi * NB - NB + AHEAD)
                out = VG[:, g % 2].rearrange("p t (j n) -> p t j n", n=VW)[:, :, :, 0:DK]
                src = Vt[:, bass.ds(b * QT, QT), g * GH * DK:(g + 1) * GH * DK].rearrange("p t (j k) -> p t j k", k=DK)
                for t in range(QT):
                    ins = nc.gpsimd.tensor_copy(out[:, t], src[:, t])
                ins.then_inc(s_vg, 1)
            v_group(0, 0)

            def body(b, last):
                for g in range(NG):
                    gi = b * NG + g
                    d = 0
                    for n, (c, kt, r) in enumerate(BLOCKS):
                        if n == 2 and not (last and g == NG - 1):
                            v_group(b + (g + 1) // NG, (g + 1) % NG)
                        if kt < c * PER:
                            continue
                        pool.wait_ge(s_exp, gi * 2 * NB + 2 * n + 2 + AHEAD)
                        pool.sem_inc(s_pool, 1)
                        part = PT[:, n % 2, :, 0:P]
                        nc.gpsimd.affine_select(out=part, in_=part, compare_op=ALU.is_ge, fill=0.0, base=0,
                                                pattern=[[0, GH], [1, P]], channel_multiplier=-1).then_inc(s_mk, 1)
            batches(pool, body)

        @block.scalar
        def _(act):
            act.sem_inc(s_exp, AHEAD)

            def body(b, last):
                for g in range(NG):
                    gi = b * NG + g
                    for n, (c, kt, r) in enumerate(BLOCKS):
                        w = CH - r * P
                        for p in range(2):
                            act.wait_ge(s_st, gi * 2 * NB + 2 * n + p + 1)
                            act.wait_ge(s_pv, gi * NB + n - 1 + AHEAD)
                            src = ps_s[p][:].rearrange("p (j t) -> p j t", j=2)[:, :, 0:w]
                            nc.scalar.activation(PT[:, n % 2, 2 * p:2 * p + 2, 0:w], src, ACT.Exp, scale=DK ** -0.5).then_inc(s_exp, 1)
                        if n in (PER, NB - 1):
                            c = int(n == NB - 1)
                            act.wait_ge(s_pv, gi * NB + (NB if c else PER) + AHEAD)
                            act.wait_ge(s_ct, gi * 2 + c - 1 + AHEAD)
                            nc.scalar.activation(CT[:, c, :], ps_c[c][:], ACT.Copy).then_inc(s_ev, 1)
            batches(act, body)

        @block.vector
        def _(dve):
            dve.sem_inc(s_mx, AHEAD)
            dve.sem_inc(s_cx, AHEAD)
            dve.sem_inc(s_mp, 1)
            dve.wait_ge(s_m, 3)
            nc.vector.tensor_copy(mask[:], maskf[:]).then_inc(s_mb, 1)
            nc.vector.tensor_copy(identb[:], ident[:]).then_inc(s_mb, 1)

            def first_pass(b, g, n):
                gi = b * NG + g
                j, qt, c = ITEMS[n]
                width = min((qt + 1) * P - c * CH, CH)
                dve.wait_ge(s_p1, gi * NI + n + 1)
                out = (negm2[:, g % 2, j, qt - PER:qt - PER + 1] if c else negm[:, g % 2, j, qt:qt + 1])
                nc.vector.tensor_reduce(out, ps_1[n % 2][:, 0:width], AX.X, ALU.max, negate=True).then_inc(s_mx, 1)

            def join(b, g):
                gi = b * NG + g
                dve.wait_ge(s_mx, gi * NI + NI + AHEAD)
                nc.vector.tensor_tensor(negm[:, g % 2, :, PER:QT], negm[:, g % 2, :, PER:QT], negm2[:, g % 2], ALU.min).then_inc(s_cmb, 1)

            def parts(b, g):
                gi = b * NG + g
                dve.wait_ge(s_mt, gi + 1)
                dve.wait_ge(s_mp, gi + 1)
                nc.vector.tensor_copy(msb[:], ps_1[0][0:GH * QT, 0:P]).then_inc(s_mc, 1)
                dve.wait_ge(s_mc, gi + 1)
                nc.vector.tensor_copy(mp[:, g % 2, 0, :], msb[:]).then_inc(s_mq, 1)
                dve.wait_ge(s_mq, gi * 3 + 1)
                nc.vector.tensor_tensor(mrest[:], msb[:], mp[:, g % 2, 0, :], ALU.subtract).then_inc(s_mq, 1)
                dve.wait_ge(s_mq, gi * 3 + 2)
                nc.vector.tensor_copy(mp[:, g % 2, 1, :], mrest[:]).then_inc(s_mq, 1)
                dve.wait_ge(s_mq, gi * 3 + 3)
                nc.vector.tensor_tensor(mp[:, g % 2, 2, :], mrest[:], mp[:, g % 2, 1, :], ALU.subtract).then_inc(s_mp, 1)

            def divide(b, g, c):
                gi = b * NG + g
                dve.wait_ge(s_ct, gi * 2 + c + 1 + AHEAD)
                src = ps_c[c][:].rearrange("p (t j n) -> p t j n", t=PER, n=VW)
                nc.vector.reciprocal(den[:, c], src[:, :, :, DK]).then_inc(s_dr, 1)
                dve.wait_ge(s_dr, gi * 2 + c + 1)
                out = CX[:, bass.ds(b * QT + c * PER, PER), g * GH * DK:(g + 1) * GH * DK].rearrange("p t (j k) -> p t j k", k=DK)
                for t in range(PER):
                    ins = nc.vector.tensor_tensor(out[:, t], src[:, t, :, 0:DK], den[:, c, t].unsqueeze(2).broadcast_to([P, GH, DK]), ALU.mult)
                ins.then_inc(s_cx, 1)

            for n in range(NI):
                first_pass(0, 0, n)
            join(0, 0)
            parts(0, 0)
            for n in range(NI):
                first_pass(0, 1, n)
            join(0, 1)

            def body(b, last):
                for g in range(NG):
                    if not (last and g == NG - 1):
                        parts(b + (g + 1) // NG, (g + 1) % NG)
                    ahead = not (last and g >= NG - 2)
                    b2, g2 = b + (g + 2) // NG, (g + 2) % NG
                    if ahead:
                        for n in range(8 * PER):
                            first_pass(b2, g2, n)
                    divide(b, g, 0)
                    if ahead:
                        for n in range(8 * PER, NI):
                            first_pass(b2, g2, n)
                        join(b2, g2)
                    divide(b, g, 1)
            batches(dve, body)

        @block.tensor
        def _(pe):
            pe.sem_inc(s_pv, AHEAD)
            pe.sem_inc(s_ct, AHEAD)
            pe.wait_ge(s_mb, 2)

            def item(b, g, n):
                gi = b * NG + g
                j, qt, c = ITEMS[n]
                width = min((qt + 1) * P - c * CH, CH)
                diagonal = qt // PER == c
                if n == 0:
                    pe.wait_ge(s_ld[g], (b + 1) * 16 * (2 * PARTS * PARTS + 1))
                    if past(gi, 1):
                        pe.wait_ge(s_mc, gi)
                pe.wait_ge(s_mx, gi * NI + n - 1 + AHEAD)
                mm = nc.tensor.matmul(ps_1[n % 2][:, 0:width], Q[g][:, j, qt * P:(qt + 1) * P], K[g][:, j, c * CH:c * CH + width],
                                      start=True, stop=not diagonal, skip_group_check=True)
                if diagonal:
                    mm = nc.tensor.matmul(ps_1[n % 2][:, width - P:width], identb[:], mask[:], start=False, stop=True,
                                          skip_group_check=True)
                mm.then_inc(s_p1, 1)

            def turn_max(b, g):
                gi = b * NG + g
                pe.wait_ge(s_cmb, gi + 1)
                nc.tensor.transpose(ps_1[0][0:GH * QT, 0:P], negm[:, g % 2].rearrange("p j t -> p (j t)"), ident[:]).then_inc(s_mt, 1)

            def scores(b, g, n):
                gi = b * NG + g
                c, kt, r = BLOCKS[n]
                w = CH - r * P
                for p in range(2):
                    pe.wait_ge(s_exp, gi * 2 * NB + 2 * n + p - 1 + AHEAD)
                    for h in range(2):
                        mm = nc.tensor.matmul(ps_s[p][:, h * CH:h * CH + w], K[g][:, 2 * p + h, kt * P:(kt + 1) * P],
                                              Q[g][:, 2 * p + h, c * CH + r * P:(c + 1) * CH], start=True, stop=True)
                    mm.then_inc(s_st, 1)

            def product(b, g, n):
                gi = b * NG + g
                c, kt, r = BLOCKS[n]
                w = CH - r * P
                if kt >= c * PER:
                    pe.wait_ge(s_mk, gi * 2 * PER + c * PER + (kt - c * PER) + 1)
                else:
                    pe.wait_ge(s_exp, gi * 2 * NB + 2 * n + 2 + AHEAD)
                if kt == 0:
                    pe.wait_ge(s_cx, gi * 2 + c - 1 + AHEAD)
                for j in range(GH):
                    mm = nc.tensor.matmul(ps_c[c][j * VW:(j + 1) * VW, r * P:CH], VG[:, g % 2, kt, j * VW:(j + 1) * VW],
                                          PT[:, n % 2, j, 0:w], start=kt == 0, stop=kt == (c + 1) * PER - 1, skip_group_check=True)
                mm.then_inc(s_pv, 1)

            def turn_context(b, g, c):
                gi = b * NG + g
                pe.wait_ge(s_ev, gi * 2 + c + 1)
                for t in range(PER):
                    mm = nc.tensor.transpose(ps_c[c][:, t * P:(t + 1) * P], CT[:, c, t * P:(t + 1) * P], ident[:])
                mm.then_inc(s_ct, 1)

            for n in range(NI):
                item(0, 0, n)
            turn_max(0, 0)
            for n in range(NI):
                item(0, 1, n)

            def body(b, last):
                for g in range(NG):
                    ahead = not (last and g >= NG - 2)
                    b2, g2 = b + (g + 2) // NG, (g + 2) % NG
                    if not (last and g == NG - 1):
                        turn_max(b + (g + 1) // NG, (g + 1) % NG)
                    pe.wait_ge(s_ml[g], b * 16 + 16)
                    pe.wait_ge(s_vg, b * NG + g + 1)
                    for n in range(NB):
                        scores(b, g, n)
                        if n:
                            product(b, g, n - 1)
                        if n == 6:
                            turn_context(b, g, 0)
                        if ahead:
                            for m in range(PER * n, PER * n + PER - (2 if n == NB - 1 else 0)):
                                item(b2, g2, m)
                    product(b, g, NB - 1)
                    if ahead:
                        item(b2, g2, NI - 2)
                        item(b2, g2, NI - 1)
                    turn_context(b, g, 1)
            batches(pe, body)


def attn_out(nc, io, keep, slots):
    CX, X, LG, ident = keep["CX"], keep["X2t"], keep["LG"], keep["ident"]
    with ExitStack() as ctx:
        sb = lambda n, s, d=F32: ctx.enter_context(nc.sbuf_tensor("o_" + n, s, d))
        sem = lambda n: ctx.enter_context(nc.semaphore("o_" + n))
        bank = lambda n: ctx.enter_context(nc.psum_tensor("o_" + n, [P, CH], F32))
        w = sb("w", [P, P])
        bo = sb("bo", [1, PER, P])
        ones_row = sb("ones_row", [1, P])
        CXT = sb("CXT", [P, 2, CH])
        stats = sb("stats", [P, NT, 6])
        mv = sb("mv", [P, NT, 2])
        rstd = sb("rstd", [P, NT])
        router = sb("router", [P, E1])
        zero = sb("zero", [P, SLOTS // 4])
        ps_t = [bank(f"ps_t{k}") for k in range(2)]
        ps_o = [bank(f"ps_o{k}") for k in range(2)]
        ps_l = [bank(f"ps_l{k}") for k in range(2)]
        s_w, s_z, s_t, s_c, s_o, s_r, s_ln, s_sq, s_n, s_x, s_xc = (sem(n) for n in (
            "weights", "zeroed", "turned", "copied", "out", "residual", "norm", "sqrt", "normed", "x_turned", "x_copied"))
        s_l, s_lc, s_zb = sem("logits"), sem("logits_copied"), sem("slots_zeroed")

        ctx.enter_context(nc.allow_non_contiguous_dma(reason="rows of heads"))
        block = ctx.enter_context(nc.Block())

        @block.sync
        def _(sp):
            sp.dma_start(w[:], io["Wo"]).then_inc(s_w, 16)
            sp.dma_start(bo[:], io["bo"].rearrange("(a b n) -> a b n", a=1, b=1).broadcast_to([1, PER, P])).then_inc(s_w, 16)
            sp.dma_start(router[:], io["router_w"]).then_inc(s_w, 16)
            sp.wait_ge(s_z, 2)
            for q in range(4):
                rows = slots[q * (SLOTS // 4):(q + 1) * (SLOTS // 4), :].rearrange("(p a) n -> p (a n)", p=P)
                sp.dma_start(rows, zero[:]).then_inc(s_zb, 16)
            sp.wait_ge(s_zb, 64)

        @block.gpsimd
        def _(pool):
            nc.gpsimd.memset(ones_row[:], 1.0).then_inc(s_z, 1)
            nc.gpsimd.memset(zero[:], 0.0).then_inc(s_z, 1)

        @block.scalar
        def _(act):
            for i in range(NCH):
                act.wait_ge(s_t, i + 1)
                if i >= 2:
                    act.wait_ge(s_o, i - 1)
                nc.scalar.activation(CXT[:, i % 2, :], ps_t[i % 2][:], ACT.Copy).then_inc(s_c, 1)
            act.wait_ge(s_ln, 2 * NT + 1)
            nc.scalar.activation(rstd[:], rstd[:], ACT.Sqrt).then_inc(s_sq, 1)
            for i in range(NCH):
                act.wait_ge(s_x, i + 1)
                if i >= 2:
                    act.wait_ge(s_l, i - 1)
                nc.scalar.activation(CXT[:, i % 2, :], ps_t[i % 2][:], ACT.Copy).then_inc(s_xc, 1)

        @block.vector
        def _(dve):
            for i in range(NCH):
                dve.wait_ge(s_o, i + 1)
                rows = X[:, i * PER:(i + 1) * PER, :].rearrange("p t n -> p (t n)")
                nc.vector.tensor_tensor(rows, rows, ps_o[i % 2][:], ALU.add).then_inc(s_r, 1)
                dve.wait_ge(s_r, i + 1)
                for t in range(PER):
                    nc.vector.bn_stats(stats[:, i * PER + t, :], X[:, i * PER + t, :]).then_inc(s_ln, 1)
            for t in range(NT):
                dve.wait_ge(s_ln, t + 1)
                nc.vector.bn_aggr(mv[:, t, :], stats[:, t, :]).then_inc(s_ln, 1)
            dve.wait_ge(s_ln, 2 * NT)
            nc.vector.tensor_scalar(rstd[:], mv[:, :, 1], EPS, None, ALU.add).then_inc(s_ln, 1)
            dve.wait_ge(s_sq, 1)
            nc.vector.reciprocal(rstd[:], rstd[:]).then_inc(s_ln, 1)
            dve.wait_ge(s_ln, 2 * NT + 2)
            for t in range(NT):
                nc.vector.tensor_scalar(X[:, t, :], X[:, t, :], mv[:, t, 0:1], rstd[:, t:t + 1],
                                        ALU.subtract, ALU.mult).then_inc(s_n, 1)
            for i in range(NCH):
                dve.wait_ge(s_l, i + 1)
                nc.vector.tensor_copy(LG[:, i * PER:(i + 1) * PER, :].rearrange("p t e -> p (t e)"), ps_l[i % 2][:, 0:PER * E1]).then_inc(s_lc, 1)

        @block.tensor
        def _(pe):
            pe.wait_ge(s_w, 48)
            pe.wait_ge(s_z, 1)

            def turn(i):
                if i >= 2:
                    pe.wait_ge(s_c, i - 1)
                for t in range(PER):
                    mm = nc.tensor.transpose(ps_t[i % 2][:, t * P:(t + 1) * P], CX[:, i * PER + t, :], ident[:])
                mm.then_inc(s_t, 1)
            turn(0)
            for i in range(NCH):
                if i + 1 < NCH:
                    turn(i + 1)
                pe.wait_ge(s_c, i + 1)
                if i >= 2:
                    pe.wait_ge(s_r, i - 1)
                nc.tensor.matmul(ps_o[i % 2][:], ones_row[:], bo[:].rearrange("a t n -> a (t n)"), start=True, stop=False)
                for t in range(PER):
                    mm = nc.tensor.matmul(ps_o[i % 2][:, t * P:(t + 1) * P], CXT[:, i % 2, t * P:(t + 1) * P], w[:], start=False, stop=t == PER - 1)
                mm.then_inc(s_o, 1)
            pe.wait_ge(s_c, NCH)

            def turn_x(i):
                pe.wait_ge(s_n, (i + 1) * PER)
                if i >= 2:
                    pe.wait_ge(s_xc, i - 1)
                for t in range(PER):
                    mm = nc.tensor.transpose(ps_t[i % 2][:, t * P:(t + 1) * P], X[:, i * PER + t, :], ident[:])
                mm.then_inc(s_x, 1)
            turn_x(0)
            for i in range(NCH):
                if i + 1 < NCH:
                    turn_x(i + 1)
                pe.wait_ge(s_xc, i + 1)
                if i >= 2:
                    pe.wait_ge(s_lc, i - 1)
                for t in range(PER):
                    mm = nc.tensor.matmul(ps_l[i % 2][:, t * E1:(t + 1) * E1], CXT[:, i % 2, t * P:(t + 1) * P], router[:], start=True, stop=True)
                mm.then_inc(s_l, 1)


def attention(nc, io, keep, slots):
    dram = dict(
        qk=nc.dram_tensor("qk_parts", [2, PARTS, NH * DK, T], BF16).ap(),
        zeros=nc.dram_tensor("zero_rows", [PARTS, GH * SEQ], BF16).ap(),
        max=nc.dram_tensor("max_parts", [NG, PARTS, GH * SEQ], BF16).ap(),
    )
    with ExitStack() as ctx:
        sb = lambda n, s, d=F32: ctx.enter_context(nc.sbuf_tensor("c_" + n, s, d))
        own = dict(keep, Vt=sb("Vt", [P, NT, P]), CX=sb("CX", [P, NT, P]))
        attn_project(nc, io, own, dram)
        attn_scores(nc, io, own, dram)
        attn_out(nc, io, own, slots)


I1 = 64
GE = 4
NGE = E1 // GE
QTR = NT // BATCH
BEYOND = 1 << 17


def moe_route(nc, io, keep, slots):
    X, LG, prob, idx_g = keep["X2t"], keep["LG"], keep["prob"], keep["idx_g"]
    with ExitStack() as ctx:
        sb = lambda n, s, d=F32: ctx.enter_context(nc.sbuf_tensor("r_" + n, s, d))
        sem = lambda n: ctx.enter_context(nc.semaphore("r_" + n))
        bank = lambda n: ctx.enter_context(nc.psum_tensor("r_" + n, [P, CH], F32))
        top = sb("top", [P, NT, 8])
        idx = sb("idx", [P, NT, 8], U32)
        idxf = sb("idxf", [P, NT, 8])
        ex = sb("ex", [P, NT, E1])
        ex4 = sb("ex4", [P, NT, TOPK])
        den = sb("den", [P, NT])
        iota_i = sb("iota_i", [P, QTR, E1], I32)
        iota = sb("iota", [P, QTR, E1])
        oh = sb("oh", [P, TOPK, QTR, E1])
        pair = sb("pair", [P, 2, QTR, E1])
        M = sb("M", [P, 2, QTR, E1], BF16)
        trif = sb("trif", [P, P])
        tri = sb("tri", [P, P], BF16)
        ones = sb("ones", [P, P], BF16)
        base = sb("base", [P, NT + 1, E1])
        pos = sb("pos", [P, QTR, E1])
        posj = sb("posj", [P, TOPK, QTR])
        slot = sb("slot", [P, TOPK, QTR])
        over = sb("over", [P, TOPK, QTR])
        idx_s = sb("idx_s", [P, TOPK, NT], I32)
        ps_p = [bank(f"ps_p{k}") for k in range(2)]
        ps_n = [bank(f"ps_n{k}") for k in range(2)]
        s_z, s_c, s_t, s_i, s_e, s_pr = (sem(n) for n in ("shapes", "consts", "top", "index", "exp", "probs"))
        s_m, s_r, s_b, s_x, s_sc = (sem(n) for n in ("mask", "rank", "chain", "slots", "scattered"))

        block = ctx.enter_context(nc.Block())

        @block.gpsimd
        def _(pool):
            nc.gpsimd.iota(iota_i[:], pattern=[[0, QTR], [1, E1]], base=0, channel_multiplier=0).then_inc(s_z, 1)
            nc.gpsimd.memset(trif[:], 1.0).then_inc(s_z, 1)
            pool.wait_ge(s_z, 2)
            nc.gpsimd.affine_select(out=trif[:], in_=trif[:], compare_op=ALU.is_gt, fill=0.0, base=0,
                                    pattern=[[1, P]], channel_multiplier=-1).then_inc(s_z, 1)
            for q in range(BATCH):
                pool.wait_ge(s_x, q + 1)
                for t in range(q * QTR, (q + 1) * QTR):
                    for j in range(TOPK):
                        pool.indirect_dma_start(out=slots, out_offset=bass.IndirectOffsetOnAxis(ap=idx_s[:, j, t:t + 1].bitcast(U32), axis=0),
                                                in_=X[:, t, :], in_offset=None, bounds_check=SLOTS - 1,
                                                oob_is_err=False).then_inc(s_sc, 16)
            pool.wait_ge(s_sc, 16 * TOPK * NT)

        @block.scalar
        def _(act):
            act.wait_ge(s_e, 2)
            nc.scalar.activation(ex[:], ex[:], ACT.Exp).then_inc(s_pr, 1)
            nc.scalar.activation(ex4[:], ex4[:], ACT.Exp).then_inc(s_pr, 1)

        @block.vector
        def _(dve):
            dve.wait_ge(s_z, 3)
            nc.vector.tensor_copy(iota[:], iota_i[:]).then_inc(s_c, 1)
            nc.vector.tensor_copy(tri[:], trif[:]).then_inc(s_c, 1)
            nc.vector.memset(ones[:], 1.0).then_inc(s_c, 1)
            nc.vector.memset(base[:, 0, :], 0.0).then_inc(s_c, 1)
            for t in range(NT):
                nc.vector.max(top[:, t, :], LG[:, t, :]).then_inc(s_t, 1)
            for t in range(NT):
                dve.wait_ge(s_t, t + 1)
                nc.vector.max_index(idx[:, t, :], top[:, t, :], LG[:, t, :]).then_inc(s_i, 1)
            dve.wait_ge(s_i, NT)
            nc.vector.tensor_copy(idxf[:], idx[:]).then_inc(s_i, 1)
            nc.vector.tensor_tensor(ex[:], LG[:], wide(top[:, :, 0], E1), ALU.subtract).then_inc(s_e, 1)
            nc.vector.tensor_tensor(ex4[:], top[:, :, 0:TOPK], wide(top[:, :, 0], TOPK), ALU.subtract).then_inc(s_e, 1)
            dve.wait_ge(s_i, NT + 1)
            dve.wait_ge(s_c, 4)

            n = 0

            def link(ins):
                nonlocal n
                n += 1
                ins.then_inc(s_b, 1)
                dve.wait_ge(s_b, n)

            for q in range(BATCH):
                tiles = slice(q * QTR, (q + 1) * QTR)
                for j in range(TOPK):
                    ins = nc.vector.tensor_tensor(oh[:, j], iota[:], wide(idxf[:, tiles, j], E1), ALU.is_equal)
                    if j < TOPK - 1:
                        ins.then_inc(s_b, 1)
                        n += 1
                link(ins)
                for j in range(2):
                    ins = nc.vector.tensor_tensor(pair[:, j], oh[:, 2 * j], oh[:, 2 * j + 1], ALU.add)
                    if j == 0:
                        ins.then_inc(s_b, 1)
                        n += 1
                link(ins)
                nc.vector.tensor_tensor(M[:, q % 2], pair[:, 0], pair[:, 1], ALU.add).then_inc(s_m, 1)
                dve.wait_ge(s_r, 2 * q + 2)
                for t in range(QTR):
                    g = q * QTR + t
                    link(nc.vector.tensor_tensor(base[:, g + 1, :], base[:, g, :], ps_n[q % 2][:, t * E1:(t + 1) * E1], ALU.add))
                link(nc.vector.tensor_tensor(pos[:], ps_p[q % 2][:].rearrange("p (t e) -> p t e", e=E1), base[:, tiles, :], ALU.add))
                for j in range(TOPK):
                    ins = nc.vector.tensor_tensor(oh[:, j], oh[:, j], pos[:], ALU.mult)
                    if j < TOPK - 1:
                        ins.then_inc(s_b, 1)
                        n += 1
                link(ins)
                link(nc.vector.tensor_reduce(posj[:], oh[:], AX.X, ALU.add))
                experts = idxf[:, tiles, 0:TOPK].rearrange("p t j -> p j t")
                link(nc.vector.tensor_scalar(slot[:], posj[:], float(CAP - 1), None, ALU.min))
                link(nc.vector.scalar_tensor_tensor(out=slot[:], in0=experts, scalar=float(CAP), in1=slot[:], op0=ALU.mult, op1=ALU.add))
                link(nc.vector.tensor_copy(idx_g[:, :, tiles], slot[:]))
                link(nc.vector.tensor_scalar(over[:], posj[:], float(CAP), float(BEYOND), ALU.is_ge, ALU.mult))
                link(nc.vector.tensor_tensor(over[:], over[:], slot[:], ALU.add))
                nc.vector.tensor_copy(idx_s[:, :, tiles], over[:]).then_inc(s_x, 1)
            dve.wait_ge(s_pr, 2)
            link(nc.vector.tensor_reduce(den[:], ex[:], AX.X, ALU.add))
            link(nc.vector.reciprocal(den[:], den[:]))
            link(nc.vector.tensor_tensor(prob[:], ex4[:], wide(den[:], TOPK), ALU.mult))

        @block.tensor
        def _(pe):
            pe.wait_ge(s_c, 4)
            for q in range(BATCH):
                pe.wait_ge(s_m, q + 1)
                if q >= 2:
                    pe.wait_ge(s_x, q - 1)
                rows = M[:, q % 2].rearrange("p t e -> p (t e)")
                nc.tensor.matmul(ps_n[q % 2][:], ones[:], rows, start=True, stop=True).then_inc(s_r, 1)
                nc.tensor.matmul(ps_p[q % 2][:], tri[:], rows, start=True, stop=True).then_inc(s_r, 1)


def moe_experts(nc, io, keep, slots, outs):
    ident = keep["ident"]
    with ExitStack() as ctx:
        sb = lambda n, s, d=F32: ctx.enter_context(nc.sbuf_tensor("e_" + n, s, d))
        sem = lambda n: ctx.enter_context(nc.semaphore("e_" + n))
        bank = lambda n: ctx.enter_context(nc.psum_tensor("e_" + n, [P, CH], F32))
        x = sb("x", [P, 2, GE, P])
        xT = sb("xT", [P, 2, CH])
        w1 = sb("w1", [P, 2, GE, 2 * I1])
        w2 = sb("w2", [I1, 2, GE, P])
        S = sb("S", [I1, 2, CH])
        H = sb("H", [I1, 2, CH])
        Y = sb("Y", [P, 2, GE, P])
        ps_x = [bank(f"ps_x{k}") for k in range(2)]
        ps_a = [bank(f"ps_a{k}") for k in range(2)]
        ps_b = [bank(f"ps_b{k}") for k in range(2)]
        ps_y = [bank(f"ps_y{k}") for k in range(2)]
        s_ld = [sem(f"loaded{k}") for k in range(2)]
        s_st = [sem(f"stored{k}") for k in range(2)]
        s_x, s_xc, s_u, s_s, s_h, s_y, s_yc = (sem(n) for n in ("turned", "copied", "up", "silu", "gated", "out", "out_copied"))

        block = ctx.enter_context(nc.Block())

        @block.sync
        def _(sp):
            def load(i, k):
                if past(i):
                    sp.wait_ge(s_y, i - 1)
                sp.dma_start(x[:, k], slots[bass.ds(i * (GE * CAP), GE * CAP), :].rearrange("(e s) n -> s e n", e=GE)).then_inc(s_ld[k], 16)
                sp.dma_start(w1[:, k], io["w1"][bass.ds(i * GE, GE)].rearrange("e d f -> d e f")).then_inc(s_ld[k], 16)
                sp.dma_start(w2[:, k], io["w2"][bass.ds(i * GE, GE)].rearrange("e i n -> i e n")).then_inc(s_ld[k], 16)
            twos(sp, NGE, load)

        @block.gpsimd
        def _(pool):
            def store(i, k):
                pool.wait_ge(s_yc, i + 1)
                pool.dma_start(outs[bass.ds(i * (GE * CAP), GE * CAP), :].rearrange("(e s) n -> s e n", e=GE), Y[:, k]).then_inc(s_st[k], 16)
            twos(pool, NGE, store)
            for k in range(2):
                pool.wait_ge(s_st[k], 16 * NGE // 2)

        @block.scalar
        def _(act):
            def step(i, k):
                act.wait_ge(s_x, i + 1)
                if past(i):
                    act.wait_ge(s_u, i - 1)
                nc.scalar.activation(xT[:, k, :], ps_x[k][:], ACT.Copy).then_inc(s_xc, 1)
                act.wait_ge(s_u, i + 1)
                if past(i):
                    act.wait_ge(s_h, i - 1)
                nc.scalar.activation(S[:, k, :], ps_a[k][0:I1, :], ACT.Silu).then_inc(s_s, 1)
            twos(act, NGE, step)

        @block.vector
        def _(dve):
            def step(i, k):
                dve.wait_ge(s_s, i + 1)
                if past(i):
                    dve.wait_ge(s_y, i - 1)
                nc.vector.tensor_tensor(H[:, k, :], S[:, k, :], ps_b[k][0:I1, :], ALU.mult).then_inc(s_h, 1)
                dve.wait_ge(s_y, i + 1)
                if past(i):
                    dve.wait_ge(s_st[k], (i - k) * 8)
                nc.vector.tensor_copy(Y[:, k].rearrange("p e n -> p (e n)"), ps_y[k][:]).then_inc(s_yc, 1)
            twos(dve, NGE, step)

        @block.tensor
        def _(pe):
            def turn(i, k):
                pe.wait_ge(s_ld[k], (i - k) * 24 + 48)
                if past(i):
                    pe.wait_ge(s_xc, i - 1)
                for e in range(GE):
                    mm = nc.tensor.transpose(ps_x[k][:, e * P:(e + 1) * P], x[:, k, e, :], ident[:])
                mm.then_inc(s_x, 1)

            def step(i, k):
                pe.wait_ge(s_xc, i + 1)
                if past(i):
                    pe.wait_ge(s_h, i - 1)
                for part, ps in enumerate((ps_a, ps_b)):
                    for e in range(GE):
                        mm = nc.tensor.matmul(ps[k][0:I1, e * P:(e + 1) * P], w1[:, k, e, part * I1:(part + 1) * I1],
                                              xT[:, k, e * P:(e + 1) * P], start=True, stop=True)
                mm.then_inc(s_u, 1)

            def down(i, k):
                pe.wait_ge(s_h, i + 1)
                if past(i):
                    pe.wait_ge(s_yc, i - 1)
                for e in range(GE):
                    mm = nc.tensor.matmul(ps_y[k][:, e * P:(e + 1) * P], H[:, k, e * P:(e + 1) * P], w2[:, k, e, :], start=True, stop=True)
                mm.then_inc(s_y, 1)

            turn(0, 0)
            turn(1, 1)
            step(0, 0)
            step(1, 1)
            down(0, 0)
            with pe.Fori(1, NGE // 2) as j:
                turn(j * 2, 0)
                step(j * 2, 0)
                down(j * 2 - 1, 1)
                turn(j * 2 + 1, 1)
                step(j * 2 + 1, 1)
                down(j * 2, 0)
            down(NGE - 1, 1)


def moe_combine(nc, io, keep, outs, out):
    X, prob, idx_g = keep["X2t"], keep["prob"], keep["idx_g"]
    RING = 4
    with ExitStack() as ctx:
        sb = lambda n, s, d=F32: ctx.enter_context(nc.sbuf_tensor("y_" + n, s, d))
        sem = lambda n: ctx.enter_context(nc.semaphore("y_" + n))
        Yg = sb("Yg", [P, RING, TOPK, P])
        stats = sb("stats", [P, NT, 6])
        mv = sb("mv", [P, NT, 2])
        rstd = sb("rstd", [P, NT])
        s_g = [sem(f"gathered{k}") for k in range(RING)]
        s_a, s_b, s_v, s_q, s_r, s_n, s_o = (sem(n) for n in ("added", "stats", "variance", "sqrt", "rstd", "normed", "stored"))

        block = ctx.enter_context(nc.Block())
        rows = out.rearrange("b (t p) n -> p (b t) n", p=P)

        @block.gpsimd
        def _(pool):
            for t in range(NT):
                if t >= RING:
                    pool.wait_ge(s_a, TOPK * (t - RING + 1))
                for j in range(TOPK):
                    pool.indirect_dma_start(out=Yg[:, t % RING, j, :], out_offset=None, in_=outs,
                                            in_offset=bass.IndirectOffsetOnAxis(ap=idx_g[:, j, t:t + 1].bitcast(U32), axis=0),
                                            bounds_check=SLOTS - 1, oob_is_err=False).then_inc(s_g[t % RING], 16)

        @block.scalar
        def _(act):
            with act.Fori(0, BATCH) as q:
                act.wait_ge(s_v, q + 1)
                part = rstd[:, bass.ds(q * QTR, QTR)]
                nc.scalar.activation(part, part, ACT.Sqrt).then_inc(s_q, 1)

        @block.vector
        def _(dve):
            for t in range(NT):
                dve.wait_ge(s_g[t % RING], 16 * TOPK * (t // RING + 1))
                for j in range(TOPK):
                    nc.vector.scalar_tensor_tensor(out=X[:, t, :], in0=Yg[:, t % RING, j, :], scalar=prob[:, t, j:j + 1], in1=X[:, t, :],
                                                   op0=ALU.mult, op1=ALU.add).then_inc(s_a, 1)
                    dve.wait_ge(s_a, TOPK * t + j + 1)
                nc.vector.bn_stats(stats[:, t, :], X[:, t, :]).then_inc(s_b, 1)
                dve.wait_ge(s_b, 2 * t + 1)
                nc.vector.bn_aggr(mv[:, t, :], stats[:, t, :]).then_inc(s_b, 1)
                if t % QTR == QTR - 1:
                    q = t // QTR
                    tiles = slice(q * QTR, (q + 1) * QTR)
                    dve.wait_ge(s_b, 2 * t + 2)
                    nc.vector.tensor_scalar(rstd[:, tiles], mv[:, tiles, 1], EPS, None, ALU.add).then_inc(s_v, 1)
                    dve.wait_ge(s_q, q + 1)
                    nc.vector.reciprocal(rstd[:, tiles], rstd[:, tiles]).then_inc(s_r, 1)
                    dve.wait_ge(s_r, q + 1)
                    for u in range(q * QTR, (q + 1) * QTR):
                        nc.vector.tensor_scalar(X[:, u, :], X[:, u, :], mv[:, u, 0:1], rstd[:, u:u + 1],
                                                ALU.subtract, ALU.mult).then_inc(s_n, 1)

        @block.sync
        def _(sp):
            with sp.Fori(0, BATCH) as q:
                sp.wait_ge(s_n, q * QTR + QTR)
                sp.dma_start(rows[:, bass.ds(q * QTR, QTR), :], X[:, bass.ds(q * QTR, QTR), :]).then_inc(s_o, 16)
            sp.wait_ge(s_o, 16 * BATCH)


def moe(nc, io, keep, slots, out):
    outs = nc.dram_tensor("slot_outputs", [SLOTS, P], F32).ap()
    moe_route(nc, io, keep, slots)
    moe_experts(nc, io, keep, slots, outs)
    moe_combine(nc, io, keep, outs, out)


def build(nc, io, out):
    slots = nc.dram_tensor("slots", [SLOTS, P], F32).ap()
    with ExitStack() as ctx:
        sb = lambda n, s, d=F32: ctx.enter_context(nc.sbuf_tensor(n, s, d))
        keep = dict(ones=sb("mean_ones", [P, P]), eps=sb("eps", [P, 1]), one=sb("one", [P, 1]), ident=sb("ident", [P, P]))
        keep["X1"] = sb("X1", [P, T])
        mamba(nc, io, keep)
        keep["X2"] = sb("X2", [P, T])
        keep["X2t"] = sb("X2t", [P, NT, P])
        ffn(nc, io, keep)
        keep["LG"] = sb("LG", [P, NT, E1])
        attention(nc, io, keep, slots)
        keep["prob"] = sb("prob", [P, NT, TOPK])
        keep["idx_g"] = sb("idx_g", [P, TOPK, NT], I32)
        moe(nc, io, keep, slots, out)


def kernel(**inputs):
    import concourse.bacc as _bacc
    from concourse.bass_utils import run_bass_kernel_spmd as _run

    mixer = lambda n: inputs["L0_attn_" + n]
    gated = lambda n: inputs["L0_ffn_" + n]
    laid = dict(
        xT=mixer("x").reshape(T, P).T, norm_w=mixer("norm_w"), in_wT=mixer("in_proj_w").T,
        conv_w=mixer("conv_w"), conv_b=mixer("conv_b"), xp_wT=mixer("x_proj_w").T, dt_wT=mixer("dt_proj_w").T,
        dt_b=mixer("dt_proj_b"), A_log=mixer("A_log"), D=mixer("D"), out_wT=mixer("out_proj_w").T, norm_f_w=mixer("norm_f_w"),
        gate_w=gated("gate_W"), sh_w=gated("shared_W"), sh_b=gated("shared_b"), gamma=gated("gamma"), beta=gated("beta"),
        b2=gated("b2"), W1=gated("W1"), W2=gated("W2"), b1T=gated("b1").reshape(E0, HM, P).transpose(0, 2, 1),
        router_w=inputs["L1_ffn_router_w"], w1=inputs["L1_ffn_w1"], w2=inputs["L1_ffn_w2"],
        **{n: inputs["L1_attn_" + n] for n in ("Wq", "Wk", "Wv", "Wo", "bq", "bk", "bv", "bo")},
    )
    nc = _bacc.Bacc("TRN2", target_bir_lowering=False, num_devices=1)
    arrays, io = {}, {}
    for name, a in laid.items():
        a = np.ascontiguousarray(a)
        arrays[f"in_{name}_dram"] = a
        io[name] = nc.dram_tensor(f"in_{name}_dram", a.shape, mybir.dt.from_np(a.dtype), kind="ExternalInput").ap()
    out = nc.dram_tensor("out_0_dram", (BATCH, SEQ, P), F32, kind="ExternalOutput").ap()
    build(nc, io, out)
    r = _run(nc, [arrays], core_ids=[0])
    return r.results[0]["out_0_dram"]
```

```python
from contextlib import ExitStack

import numpy as np

import concourse.bass as bass
from concourse import mybir

F32 = mybir.dt.float32
F32R = mybir.dt.float32r
BF16 = mybir.dt.bfloat16
I32 = mybir.dt.int32
U32 = mybir.dt.uint32
ALU = mybir.AluOpType
ACT = mybir.ActivationFunctionType
AX = mybir.AxisListType

P = 128
T = 4096
BATCH = 4
SEQ = T // BATCH
CH = 512
NCH = T // CH
EPS = 1e-5
LN_EXP = "natural_log_exp_and_others"


def chunk(tile, i, n=CH):
    return tile[:, bass.ds(i * n, n)]


def chunk2(tile, c, i, n=CH):
    return tile[:, c, bass.ds(i * n, n)]


def twos(eng, n, step):
    step(0, 0)
    step(1, 1)
    with eng.Fori(1, n // 2) as j:
        for k in range(2):
            step(j * 2 + k, k)


def past(i, n=2):
    return not (isinstance(i, int) and i < n)


D_IN = 256
NST = 16
RANK = 16
TAPS = 4
RING = 4


def mamba_front(nc, io, keep):
    XN, U, DT, G, XT = keep["XN"], keep["U"], keep["DT"], keep["G"], keep["XT"]
    with ExitStack() as ctx:
        sb = lambda n, s, d=F32: ctx.enter_context(nc.sbuf_tensor("a_" + n, s, d))
        sem = lambda n: ctx.enter_context(nc.semaphore(n))
        bank = lambda n: ctx.enter_context(nc.psum_tensor(n, [P, CH], F32))
        pad = SEQ + TAPS - 1
        XB = sb("XB", [P, 2, BATCH * pad])
        SQ = sb("SQ", [P, 2, CH])
        R = sb("R", [P, 2, CH])
        E = sb("E", [P, 2, 2, CH])
        L = sb("L", [P, 2, 2, CH])
        W = sb("W", [P, 2, 2, CH])
        ones = keep["ones"]
        in_w = sb("in_w", [P, D_IN])
        conv_w = sb("conv_w", [P, 2, TAPS])
        conv_b = sb("conv_b", [P, 2])
        norm_w = sb("norm_w", [P, 1])
        xp_bc = sb("xp_bc", [P, 2, P])
        low = sb("low", [P, 1])
        xp_dt = sb("xp_dt", [RANK, D_IN])
        dt_w = sb("dt_w", [RANK, D_IN])
        dt_full = sb("dt_full", [P, 2, D_IN])
        dt_b = sb("dt_b", [P, 2])
        eps, one, ident = keep["eps"], keep["one"], keep["ident"]
        ps_rms = [bank(f"ps_rms{k}") for k in range(2)]
        ps_x = [bank(f"ps_x{c}") for c in range(2)]
        ps_bc = [bank(f"ps_bc{k}") for k in range(2)]
        ps_dt = [[bank(f"ps_dt{c}") for c in range(2)], ps_x]
        s_w = sem("a_weights")
        s_zero = sem("a_zeroed")
        s_id = sem("a_identity")
        s_xp = sem("a_xp_loaded")
        s_x = [sem(f"a_x_loaded{b}") for b in range(BATCH)]
        s_sq = sem("a_squares")
        s_ms = sem("a_mean_square")
        s_lnr = sem("a_ln_rms")
        s_r = sem("a_inv_rms")
        s_xn = sem("a_normed")
        s_xps = sem("a_x_proj_psum")
        s_xb = sem("a_x_branch")
        s_tap = sem("a_tap")
        s_cv = sem("a_conv")
        s_u = sem("a_silu")
        s_wp = sem("a_dt_weight_psum")
        s_wc = sem("a_dt_weight")
        s_bcps = sem("a_bc_psum")
        s_hi = sem("a_bc_high")
        s_g = sem("a_bc_split")
        s_dtps = sem("a_dt_psum")
        s_abs = sem("a_abs_dt")
        s_rel = sem("a_relu_dt")
        s_e = sem("a_exp_dt")
        s_l = sem("a_ln_dt")
        s_t = sem("a_one_plus_exp")
        s_t1 = sem("a_rounded_off")
        s_t2 = sem("a_relu_and_rounded_off")
        s_c = sem("a_softplus")
        s_low = sem("a_low_rows")
        s_own = sem("a_own_step")
        keep["used"] += [s_w, s_zero, s_id, s_xp, *s_x, s_sq, s_ms, s_lnr, s_r, s_xn, s_xps, s_xb, s_tap, s_cv, s_u,
                         s_wp, s_wc, s_bcps, s_hi, s_g, s_dtps, s_abs, s_rel, s_e, s_l, s_t, s_t1, s_t2, s_c, s_low, s_own]

        ctx.enter_context(nc.allow_non_contiguous_dma(reason="small per-feature vectors"))
        block = ctx.enter_context(nc.Block())

        @block.sync
        def _(sp):
            for b in range(BATCH):
                cols = slice(b * SEQ, (b + 1) * SEQ)
                sp.dma_start(XT[:, cols], io["xT"][:, cols]).then_inc(s_x[b], 16)
                if b == 0:
                    for dst, src in (
                        (norm_w[:], io["norm_w"].rearrange("(p a) -> p a", a=1)),
                        (in_w[:], io["in_wT"][:, 0:D_IN]),
                        (conv_w[:], io["conv_w"].rearrange("(c p) k -> p c k", p=P)),
                        (conv_b[:], io["conv_b"].rearrange("(c p) -> p c", p=P)),
                        (xp_dt[:], io["xp_w"][0:RANK, :]),
                        (dt_w[:], io["dt_wT"]),
                        (dt_b[:], io["dt_b"].rearrange("(c p) -> p c", p=P)),
                    ):
                        sp.dma_start(dst, src).then_inc(s_w, 16)
            sp.wait_ge(s_zero, 2)
            for col, src in ((0, RANK), (32, RANK), (64, RANK + NST), (96, RANK + NST)):
                sp.dma_start(xp_bc[:, :, col:col + NST],
                             io["xp_wT"].rearrange("(c p) n -> p c n", p=P)[:, :, src:src + NST]).then_inc(s_xp, 16)

        @block.gpsimd
        def _(pool):
            nc.gpsimd.memset(ones[:], 1.0 / P).then_inc(s_zero, 1)
            nc.gpsimd.memset(xp_bc[:], 0.0).then_inc(s_zero, 1)
            nc.gpsimd.memset(eps[:], EPS).then_inc(s_zero, 1)
            nc.gpsimd.memset(one[:], 1.0).then_inc(s_zero, 1)
            for c in range(2):
                for b in range(BATCH):
                    nc.gpsimd.memset(XB[:, c, b * pad:b * pad + TAPS - 1], 0.0).then_inc(s_zero, 1)
            nc.gpsimd.memset(ident[:], 0.0).then_inc(s_id, 1)
            pool.wait_ge(s_id, 1)
            nc.gpsimd.affine_select(out=ident[:], in_=ident[:], compare_op=ALU.not_equal, fill=1.0, base=0,
                                    pattern=[[-1, P]], channel_multiplier=1).then_inc(s_id, 1)

            def rounded_off(i, k):
                for c in range(2):
                    pool.wait_ge(s_t, i * 2 + c + 1)
                    nc.gpsimd.tensor_tensor(W[:, k, c, :], E[:, k, c, :], W[:, k, c, :], ALU.subtract).then_inc(s_t1, 1)
                for c in range(2):
                    pool.wait_ge(s_t1, i * 2 + c + 1)
                    pool.wait_ge(s_rel, i * 2 + c + 1)
                    pool.sem_inc(s_own, 1)
                    nc.gpsimd.tensor_tensor(chunk2(DT, c, i), chunk2(DT, c, i), W[:, k, c, :], ALU.add).then_inc(s_t2, 1)
            twos(pool, NCH, rounded_off)

        @block.scalar
        def _(act):
            nc.scalar.preload_act_table_set(LN_EXP)
            act.wait_ge(s_zero, 4)

            def square(i, k):
                if past(i):
                    act.wait_ge(s_ms, i - 1)
                nc.scalar.activation(SQ[:, k, :], chunk(XT, i), ACT.Square).then_inc(s_sq, 1)

            def inverse(i, k):
                act.wait_ge(s_ms, i + 1)
                if past(i):
                    act.wait_ge(s_xn, i - 1)
                nc.scalar.activation(R[:, k, :], ps_rms[k][:], ACT.Ln, bias=eps[:, 0:1]).then_inc(s_lnr, 1)
                act.wait_ge(s_lnr, i + 1)
                nc.scalar.activation(R[:, k, :], R[:, k, :], ACT.Exp, scale=-0.5).then_inc(s_r, 1)

            def branch(b, h):
                for c in range(2):
                    act.wait_ge(s_xps, b * 4 + h * 2 + c + 1)
                    nc.scalar.activation(XB[:, c, bass.ds(b * pad + TAPS - 1 + h * CH, CH)], ps_x[c][:],
                                         ACT.Copy).then_inc(s_xb, 1)

            for h in range(2):
                act.wait_ge(s_x[0], 16)
                square(h, h)
                if h == 1:
                    inverse(0, 0)
            for b in range(1, BATCH):
                act.wait_ge(s_x[b], 16)
                for h in range(2):
                    square(b * 2 + h, h)
                    inverse(b * 2 + h - 1, 1 - h)
                    branch(b - 1, h)
            inverse(NCH - 1, 1)
            for h in range(2):
                branch(BATCH - 1, h)
            act.wait_ge(s_wp, 1)
            nc.scalar.activation(dt_full[:].rearrange("p c n -> p (c n)"), ps_bc[0][:], ACT.Copy).then_inc(s_wc, 1)
            nc.scalar.preload_act_table(ACT.Silu)
            with act.Fori(0, NCH) as i:
                for c in range(2):
                    act.wait_ge(s_cv, i * 2 + c + 1)
                    act.sem_inc(s_own, 1)
                    nc.scalar.activation(chunk2(U, c, i), chunk2(U, c, i), ACT.Silu).then_inc(s_u, 1)
            nc.scalar.preload_act_table_set(LN_EXP)

            def exps(i, k):
                act.wait_ge(s_bcps, i + 1)
                nc.scalar.activation(chunk(G, i), ps_bc[k][:], ACT.Copy).then_inc(s_hi, 1)
                for c in range(2):
                    act.wait_ge(s_dtps, i * 2 + c + 1)
                    if past(i):
                        act.wait_ge(s_t1, i * 2 + c - 3)
                    nc.scalar.activation(E[:, k, c, :], ps_dt[k][c][:], ACT.Abs, bias=dt_b[:, c:c + 1]).then_inc(s_abs, 1)
                for c in range(2):
                    act.wait_ge(s_abs, i * 2 + c + 1)
                    nc.scalar.activation(E[:, k, c, :], E[:, k, c, :], ACT.Exp, scale=-1.0).then_inc(s_e, 1)
                for c in range(2):
                    act.wait_ge(s_e, i * 2 + c + 1)
                    if past(i):
                        act.wait_ge(s_c, i * 2 + c - 3)
                    nc.scalar.activation(L[:, k, c, :], E[:, k, c, :], ACT.Ln, bias=one[:, 0:1]).then_inc(s_l, 1)
            twos(act, NCH, exps)

        @block.vector
        def _(dve):
            for q in range(4):
                nc.vector.memset(low[q * 32:(q + 1) * 32], -float(q % 2)).then_inc(s_low, 1)
            dve.wait_ge(s_w, 16 * 7)

            def normed(i, k):
                dve.wait_ge(s_r, i + 1)
                nc.vector.scalar_tensor_tensor(out=chunk(XN, i), in0=chunk(XT, i), scalar=norm_w[:, 0:1],
                                               in1=R[:, k, :], op0=ALU.mult, op1=ALU.mult).then_inc(s_xn, 1)

            def conv(b, h):
                i = b * 2 + h
                for c in range(2):
                    dve.wait_ge(s_xb, i * 2 + c + 1)
                for k in range(TAPS):
                    for c in range(2):
                        src = XB[:, c, bass.ds(b * pad + h * CH + k, CH)]
                        out = chunk2(U, c, i)
                        if k == 0:
                            ins = nc.vector.tensor_scalar(out, src, conv_w[:, c, 0:1], conv_b[:, c:c + 1], ALU.mult, ALU.add)
                        else:
                            dve.wait_ge(s_tap, i * (2 * TAPS - 2) + 2 * (k - 1) + c + 1)
                            ins = nc.vector.scalar_tensor_tensor(out=out, in0=src, scalar=conv_w[:, c, k:k + 1],
                                                                 in1=out, op0=ALU.mult, op1=ALU.add)
                        ins.then_inc(s_cv if k == TAPS - 1 else s_tap, 1)
            dve.wait_ge(s_x[0], 16)
            normed(0, 0)
            normed(1, 1)
            dve.wait_ge(s_zero, 4 + 2 * BATCH)
            for b in range(1, BATCH):
                dve.wait_ge(s_x[b], 16)
                for h in range(2):
                    normed(b * 2 + h, h)
                    conv(b - 1, h)
            for h in range(2):
                conv(BATCH - 1, h)

            def add_ln(i, k):
                for c in range(2):
                    dve.wait_ge(s_l, i * 2 + c + 1)
                    dve.wait_ge(s_t2, i * 2 + c + 1)
                    nc.vector.tensor_tensor(chunk2(DT, c, i), chunk2(DT, c, i), L[:, k, c, :], ALU.add).then_inc(s_c, 1)

            def softplus(i, k):
                dve.wait_ge(s_hi, i + 1)
                nc.vector.scalar_tensor_tensor(out=chunk(G, i), in0=chunk(G, i).bitcast(F32), scalar=low[:, 0:1],
                                               in1=ps_bc[k][:], op0=ALU.mult, op1=ALU.add).then_inc(s_g, 1)
                for c in range(2):
                    dve.wait_ge(s_abs, i * 2 + c + 1)
                    nc.vector.tensor_scalar(chunk2(DT, c, i), ps_dt[k][c][:], dt_b[:, c:c + 1], 0.0,
                                            ALU.add, ALU.max).then_inc(s_rel, 1)
                for c in range(2):
                    dve.wait_ge(s_e, i * 2 + c + 1)
                    if past(i):
                        dve.wait_ge(s_t2, i * 2 + c - 3)
                    nc.vector.tensor_scalar(W[:, k, c, :], E[:, k, c, :], 1.0, -1.0, ALU.add, ALU.add).then_inc(s_t, 1)
                if past(i, 1):
                    add_ln(i - 1, 1 - k)
            dve.wait_ge(s_low, 4)
            twos(dve, NCH, softplus)
            add_ln(NCH - 1, 1)

        @block.tensor
        def _(pe):
            pe.wait_ge(s_zero, 3)

            def mean_square(i, k):
                pe.wait_ge(s_sq, i + 1)
                if past(i):
                    pe.wait_ge(s_lnr, i - 1)
                nc.tensor.matmul(ps_rms[k][:], ones[:], SQ[:, k, :], start=True, stop=True).then_inc(s_ms, 1)

            def x_branch(i):
                pe.wait_ge(s_xn, i + 1)
                for c in range(2):
                    if past(i, 1):
                        pe.wait_ge(s_xb, i * 2 + c - 1)
                    nc.tensor.matmul(ps_x[c][:], in_w[:, c * P:(c + 1) * P], chunk(XN, i),
                                     start=True, stop=True).then_inc(s_xps, 1)
            mean_square(0, 0)
            mean_square(1, 1)
            pe.wait_ge(s_w, 16 * 7)
            x_branch(0)
            with pe.Fori(1, NCH // 2) as j:
                for k in range(2):
                    mean_square(j * 2 + k, k)
                    x_branch(j * 2 + k - 1)
            x_branch(NCH - 1)
            for c in range(2):
                mm = nc.tensor.matmul(ps_bc[0][:, c * D_IN:(c + 1) * D_IN], xp_dt[:, c * P:(c + 1) * P], dt_w[:], start=True, stop=True)
            mm.then_inc(s_wp, 1)
            pe.wait_ge(s_wc, 1)
            pe.wait_ge(s_xp, 16 * 4)
            pe.wait_ge(s_xb, 2 * NCH)

            def x_proj(i, k):
                pe.wait_ge(s_u, i * 2 + 2)
                if past(i):
                    pe.wait_ge(s_g, i - 1)
                for c in range(2):
                    mm = nc.tensor.matmul(ps_bc[k][:], xp_bc[:, c, :], chunk2(U, c, i), start=c == 0, stop=c == 1)
                mm.then_inc(s_bcps, 1)
                for c in range(2):
                    if past(i):
                        pe.wait_ge(s_rel, i * 2 + c - 3)
                    for d in range(2):
                        mm = nc.tensor.matmul(ps_dt[k][c][:], dt_full[:, d, c * P:(c + 1) * P], chunk2(U, d, i), start=d == 0, stop=d == 1)
                    mm.then_inc(s_dtps, 1)
            twos(pe, NCH, x_proj)


def mamba_scan(nc, io, keep):
    U, DT, G = keep["U"], keep["DT"], keep["G"]
    with ExitStack() as ctx:
        sb = lambda n, s, d=F32: ctx.enter_context(nc.sbuf_tensor("s_" + n, s, d))
        sem = lambda n: ctx.enter_context(nc.semaphore(n))
        bank = lambda n: ctx.enter_context(nc.psum_tensor(n, [P, CH], F32))
        sel = sb("sel", [P, 2 * NST, P], F32R)
        selw = sb("selw", [P, 2 * NST, P // 4])
        ident = keep["ident"]
        A = sb("A", [P, 2, NST])
        Dw = sb("D", [P, 2])
        DU = sb("DU", [P, 2, 2, CH])
        dA = sb("dA", [P, 2, 2, CH])
        H = sb("H", [P, 2, 2, CH])
        HC = sb("HC", [P, RING, 2, CH])
        diag = sb("diag", [P, 2, P])
        C_sb = sb("C_sb", [P, 2, CH])
        last = sb("last", [P, 2, NST])
        ps_b = [bank(f"ps_b{k}") for k in range(2)]
        ps_d = [bank(f"ps_d{k}") for k in range(2)]
        ps_c = [bank(f"ps_c{k}") for k in range(2)]
        ps_y = [bank(f"ps_y{c}") for c in range(2)]
        s_w = sem("s_weights")
        s_sel0 = sem("s_sel_shape")
        s_sel = sem("s_sel")
        s_a = sem("s_A")
        s_b = sem("s_b_spread")
        s_c = sem("s_c_spread")
        s_da = sem("s_decay")
        s_cs = sem("s_c_copied")
        s_du = sem("s_dt_u")
        s_in = sem("s_input")
        s_h = sem("s_state")
        s_hl = sem("s_state_saved")
        s_hc = sem("s_c_times_state")
        s_y = sem("s_y_added")
        s_out = sem("s_y_out")
        s_own = sem("s_own_step")
        keep["used"] += [s_w, s_sel0, s_sel, s_a, s_b, s_c, s_da, s_cs, s_du, s_in, s_h, s_hl, s_hc, s_y, s_out, s_own]

        ctx.enter_context(nc.allow_non_contiguous_dma(reason="small per-feature vectors"))
        block = ctx.enter_context(nc.Block())
        N = NST

        @block.sync
        def _(sp):
            sp.dma_start(A[:], io["A_log"].rearrange("(c p) n -> p c n", p=P)).then_inc(s_w, 16)
            sp.dma_start(Dw[:], io["D"].rearrange("(c p) -> p c", p=P)).then_inc(s_w, 16)

        @block.gpsimd
        def _(pool):
            nc.gpsimd.memset(selw[:], 0.0).then_inc(s_sel0, 1)
            for q in range(4):
                pool.wait_ge(s_sel0, q + 1)
                half = selw[:, (q // 2) * N:(q // 2 + 1) * N, :]
                nc.gpsimd.affine_select(out=half, in_=half, compare_op=ALU.not_equal, fill=1.0, base=-32 * q,
                                        pattern=[[-1, N], [0, P // 4]], channel_multiplier=1).then_inc(s_sel0, 1)

            def times_c(i, g):
                k = g % 2
                pool.wait_ge(s_cs, i * N + g + 1)
                for c in range(2):
                    pool.wait_ge(s_h, i * 2 * N + 2 * g + c + 1)
                    if past(i, 1) or g >= RING:
                        pool.wait_ge(s_y, i * 2 * N + 2 * (g - RING) + c + 1)
                    nc.gpsimd.tensor_tensor(HC[:, g % RING, c, :], H[:, k, c, :], C_sb[:, k, :], ALU.mult).then_inc(s_hc, 1)
            for g in range(N):
                times_c(0, g)
            with pool.Fori(1, NCH) as i:
                for g in range(N):
                    times_c(i, g)

        @block.scalar
        def _(act):
            nc.scalar.preload_act_table_set(LN_EXP)
            act.wait_ge(s_w, 32)
            nc.scalar.activation(A[:], A[:], ACT.Exp).then_inc(s_a, 1)
            act.wait_ge(s_a, 2)

            def save(g):
                nc.scalar.activation(last[:, :, g], H[:, g % 2, :, CH - 1], ACT.Copy).then_inc(s_hl, 1)

            def y_out(i):
                for c in range(2):
                    act.wait_ge(s_y, i * 2 * N + 2 * N - 1 + c)
                    act.sem_inc(s_own, 1)
                    nc.scalar.activation(chunk2(U, c, i), ps_y[c][:], ACT.Copy).then_inc(s_out, 1)

            def chunk_of(b, h):
                i = b * 2 + h
                for g in range(N):
                    k = g % 2
                    if past(i, 1) or g >= 2:
                        act.wait_ge(s_h, i * 2 * N + 2 * (g - 1))
                        if h == 0 and g >= 2:
                            save(g - 2)
                        elif h == 1 and g < 2:
                            save(N - 2 + g)
                        else:
                            act.sem_inc(s_own, 1)
                    for c in range(2):
                        nc.scalar.activation(dA[:, k, c, :], chunk2(DT, c, i), ACT.Exp,
                                             scale=A[:, c, g:g + 1]).then_inc(s_da, 1)
                    act.wait_ge(s_c, i * N + g + 1)
                    if past(i, 1) or g >= 2:
                        act.wait_ge(s_hc, i * 2 * N + 2 * (g - 1))
                    nc.scalar.activation(C_sb[:, k, :], ps_c[k][:], ACT.Copy).then_inc(s_cs, 1)
                    if g == 2 and past(i, 1):
                        y_out(i - 1)
            chunk_of(0, 0)
            chunk_of(0, 1)
            with act.Fori(1, BATCH) as b:
                for h in range(2):
                    chunk_of(b, h)
            y_out(NCH - 1)

        @block.vector
        def _(dve):
            dve.wait_ge(s_sel0, 5)
            for q in range(4):
                nc.vector.tensor_copy(sel[:, :, q * 32:(q + 1) * 32], selw[:]).then_inc(s_sel, 1)
            dve.wait_ge(s_a, 1)
            nc.vector.tensor_scalar(A[:], A[:], -1.0, None, ALU.mult).then_inc(s_a, 1)
            dve.wait_ge(s_w, 32)
            for c in range(2):
                nc.vector.tensor_scalar(diag[:, c, :], ident[:], Dw[:, c:c + 1], None, ALU.mult).then_inc(s_sel, 1)

            def chunk_of(b, h):
                i = b * 2 + h
                for c in range(2):
                    nc.vector.tensor_tensor(DU[:, h, c, :], chunk2(DT, c, i), chunk2(U, c, i), ALU.mult).then_inc(s_du, 1)
                for g in range(N):
                    k = g % 2
                    dve.wait_ge(s_b, i * N + g + 1)
                    for c in range(2):
                        if g == 0:
                            dve.wait_ge(s_du, i * 2 + c + 1)
                        if past(i, 1) or g >= 2:
                            dve.wait_ge(s_h, i * 2 * N + 2 * (g - 2) + c + 1)
                        nc.vector.tensor_tensor((ps_d[k] if c == 0 else ps_b[k])[:], DU[:, h, c, :], ps_b[k][:],
                                                ALU.mult).then_inc(s_in, 1)
                    for c in range(2):
                        n = i * 2 * N + 2 * g + c
                        dve.wait_ge(s_in, n + 1)
                        dve.wait_ge(s_da, n + 1)
                        if past(i, 1) or g >= 2:
                            dve.wait_ge(s_hc, n - 3)
                        if h == 0 and g >= 2:
                            dve.wait_ge(s_hl, b * N + g - 1)
                        elif h == 1 and g < 2:
                            dve.wait_ge(s_hl, b * N + N - 1 + g)
                        nc.vector.tensor_tensor_scan(H[:, k, c, :], dA[:, k, c, :], (ps_d[k] if c == 0 else ps_b[k])[:],
                                                     last[:, c, g:g + 1] if h else 0.0, ALU.mult, ALU.add).then_inc(s_h, 1)
            chunk_of(0, 0)
            chunk_of(0, 1)
            with dve.Fori(1, BATCH) as b:
                for h in range(2):
                    chunk_of(b, h)

        @block.tensor
        def _(pe):
            pe.wait_ge(s_sel, 6)

            def spread(i, g):
                k = g % 2
                if past(i, 1) or g >= 2:
                    pe.wait_ge(s_h, i * 2 * N + 2 * (g - 1))
                nc.tensor.matmul(ps_b[k][:], sel[:, g, :], chunk(G, i), start=True, stop=True).then_inc(s_b, 1)
                if past(i, 1) or g >= 2:
                    pe.wait_ge(s_cs, i * N + g - 1)
                nc.tensor.matmul(ps_c[k][:], sel[:, N + g, :], chunk(G, i), start=True, stop=True).then_inc(s_c, 1)

            def add(i, g):
                if g == N // 2:
                    for c in range(2):
                        nc.tensor.matmul(ps_y[c][:], diag[:, c, :], chunk2(U, c, i), start=False, stop=False, skip_group_check=True)
                for c in range(2):
                    pe.wait_ge(s_hc, i * 2 * N + 2 * g + c + 1)
                    if g == 0 and past(i, 1):
                        pe.wait_ge(s_out, i * 2 - 1 + c)
                    nc.tensor.matmul(ps_y[c][:], ident[:], HC[:, g % RING, c, :], start=g == 0, stop=g == N - 1,
                                     skip_group_check=True).then_inc(s_y, 1)

            def chunk_of(i, last):
                for g in range(N):
                    if g + 2 < N:
                        spread(i, g + 2)
                    elif not last:
                        spread(i + 1, g + 2 - N)
                    if g > 0:
                        add(i, g - 1)
                    elif past(i, 1):
                        add(i - 1, N - 1)
            spread(0, 0)
            spread(0, 1)
            chunk_of(0, False)
            with pe.Fori(1, NCH - 1) as i:
                chunk_of(i, False)
            chunk_of(NCH - 1, True)
            add(NCH - 1, N - 1)


def mamba_back(nc, io, keep):
    XN, U, XT, X1 = keep["XN"], keep["U"], keep["XT"], keep["X1"]
    ones, ident, eps = keep["ones"], keep["ident"], keep["eps"]
    with ExitStack() as ctx:
        sb = lambda n, s, d=F32: ctx.enter_context(nc.sbuf_tensor("k_" + n, s, d))
        sem = lambda n: ctx.enter_context(nc.semaphore("k_" + n))
        banks = lambda n: [ctx.enter_context(nc.psum_tensor(f"k_{n}{k}", [P, CH], F32)) for k in range(2)]
        z_w = sb("z_w", [P, D_IN])
        out_w = sb("out_w", [P, 2, P])
        norm_w = sb("norm_w", [P, 1])
        centre = sb("centre", [P, P])
        SZ = sb("SZ", [P, 2, T])
        SQ = sb("SQ", [P, 2, CH])
        R = sb("R", [P, 2, CH])
        SQ2 = sb("SQ2", [P, 2, CH])
        R2 = sb("R2", [P, 2, CH])
        ps_o, ps_m, ps_c, ps_v = banks("ps_o"), banks("ps_m"), banks("ps_c"), banks("ps_v")
        ps_z = (ps_c, ps_v)
        s_w, s_z, s_sz, s_g, s_ce, s_o, s_t, s_sq, s_m = (sem(n) for n in (
            "weights", "z_psum", "silu_z", "gated", "centring", "out_psum", "out", "squares", "mean_square"))
        s_ln, s_r, s_n, s_x, s_c, s_q2, s_v, s_l2, s_r2, s_f = (sem(n) for n in (
            "ln", "inv_rms", "rms_normed", "x_added", "centred", "squares2", "variance", "ln2", "inv_std", "x1"))

        ctx.enter_context(nc.allow_non_contiguous_dma(reason="small per-feature vectors"))
        block = ctx.enter_context(nc.Block())

        def pipeline(*stages):
            for step in range(NCH + 3):
                for lag, stage in stages:
                    if 0 <= step - lag < NCH:
                        stage(step - lag, (step - lag) % 2)

        @block.sync
        def _(sp):
            sp.dma_start(z_w[:], io["in_wT"][:, D_IN:2 * D_IN]).then_inc(s_w, 16)
            sp.dma_start(out_w[:], io["out_wT"].rearrange("(c p) n -> p c n", p=P)).then_inc(s_w, 16)
            sp.dma_start(norm_w[:], io["norm_f_w"].rearrange("(p a) -> p a", a=1)).then_inc(s_w, 16)

        @block.gpsimd
        def _(pool):
            for used in keep["used"]:
                pool.sem_clear(used)

        @block.scalar
        def _(act):
            nc.scalar.preload_act_table(ACT.Silu)

            def silu(i, k):
                for c in range(2):
                    act.wait_ge(s_z, i * 2 + c + 1)
                    nc.scalar.activation(chunk2(SZ, c, i), ps_z[k][c][:], ACT.Silu).then_inc(s_sz, 1)
            twos(act, NCH, silu)
            nc.scalar.preload_act_table_set(LN_EXP)

            def squares(i, k):
                act.wait_ge(s_t, i + 1)
                if i >= 2:
                    act.wait_ge(s_m, i - 1)
                nc.scalar.activation(SQ[:, k, :], chunk(X1, i), ACT.Square).then_inc(s_sq, 1)

            def inv_rms(i, k):
                act.wait_ge(s_m, i + 1)
                if i >= 2:
                    act.wait_ge(s_n, i - 1)
                nc.scalar.activation(R[:, k, :], ps_m[k][:], ACT.Ln, bias=eps[:, 0:1]).then_inc(s_ln, 1)
                act.wait_ge(s_ln, i + 1)
                nc.scalar.activation(R[:, k, :], R[:, k, :], ACT.Exp, scale=-0.5).then_inc(s_r, 1)

            def squares2(i, k):
                act.wait_ge(s_c, i + 1)
                if i >= 2:
                    act.wait_ge(s_v, i - 1)
                nc.scalar.activation(SQ2[:, k, :], ps_c[k][:], ACT.Square).then_inc(s_q2, 1)

            def inv_std(i, k):
                act.wait_ge(s_v, i + 1)
                if i >= 2:
                    act.wait_ge(s_f, i - 1)
                nc.scalar.activation(R2[:, k, :], ps_v[k][:], ACT.Ln, bias=eps[:, 0:1]).then_inc(s_l2, 1)
                act.wait_ge(s_l2, i + 1)
                nc.scalar.activation(R2[:, k, :], R2[:, k, :], ACT.Exp, scale=-0.5).then_inc(s_r2, 1)
            pipeline((0, squares), (1, inv_rms), (2, squares2), (3, inv_std))

        @block.vector
        def _(dve):
            nc.vector.tensor_tensor(centre[:], ident[:], ones[:], ALU.subtract).then_inc(s_ce, 1)
            with dve.Fori(0, NCH) as i:
                for c in range(2):
                    dve.wait_ge(s_sz, i * 2 + c + 1)
                    nc.vector.tensor_tensor(chunk2(U, c, i), chunk2(U, c, i), chunk2(SZ, c, i), ALU.mult).then_inc(s_g, 1)
            dve.wait_ge(s_w, 48)

            def residual(i, k):
                dve.wait_ge(s_o, i + 1)
                nc.vector.tensor_tensor(chunk(X1, i), ps_o[k][:], chunk(XT, i), ALU.add).then_inc(s_t, 1)

            def rms_norm(i, k):
                dve.wait_ge(s_r, i + 1)
                dve.wait_ge(s_sq, i + 1)
                nc.vector.scalar_tensor_tensor(out=chunk(X1, i), in0=chunk(X1, i), scalar=norm_w[:, 0:1],
                                               in1=R[:, k, :], op0=ALU.mult, op1=ALU.mult).then_inc(s_n, 1)
                dve.wait_ge(s_n, i + 1)
                nc.vector.tensor_tensor(chunk(X1, i), chunk(X1, i), chunk(XT, i), ALU.add).then_inc(s_x, 1)

            def layer_norm(i, k):
                dve.wait_ge(s_r2, i + 1)
                nc.vector.tensor_tensor(chunk(X1, i), ps_c[k][:], R2[:, k, :], ALU.mult).then_inc(s_f, 1)
            pipeline((0, residual), (1, rms_norm), (3, layer_norm))

        @block.tensor
        def _(pe):
            pe.wait_ge(s_w, 48)

            def z_proj(i, k):
                for c in range(2):
                    if past(i):
                        pe.wait_ge(s_sz, i * 2 + c - 3)
                    nc.tensor.matmul(ps_z[k][c][:], z_w[:, c * P:(c + 1) * P], chunk(XN, i), start=True, stop=True).then_inc(s_z, 1)
            twos(pe, NCH, z_proj)
            pe.wait_ge(s_ce, 1)

            def out_proj(i, k):
                pe.wait_ge(s_g, i * 2 + 2)
                if i >= 2:
                    pe.wait_ge(s_t, i - 1)
                for c in range(2):
                    mm = nc.tensor.matmul(ps_o[k][:], out_w[:, c, :], chunk2(U, c, i), start=c == 0, stop=c == 1)
                mm.then_inc(s_o, 1)

            def mean_square(i, k):
                pe.wait_ge(s_sq, i + 1)
                if i >= 2:
                    pe.wait_ge(s_ln, i - 1)
                nc.tensor.matmul(ps_m[k][:], ones[:], SQ[:, k, :], start=True, stop=True).then_inc(s_m, 1)

            def centred(i, k):
                pe.wait_ge(s_x, i + 1)
                if i >= 2:
                    pe.wait_ge(s_f, i - 1)
                nc.tensor.matmul(ps_c[k][:], centre[:], chunk(X1, i), start=True, stop=True).then_inc(s_c, 1)

            def variance(i, k):
                pe.wait_ge(s_q2, i + 1)
                if i >= 2:
                    pe.wait_ge(s_l2, i - 1)
                nc.tensor.matmul(ps_v[k][:], ones[:], SQ2[:, k, :], start=True, stop=True).then_inc(s_v, 1)
            pipeline((0, out_proj), (1, mean_square), (2, centred), (3, variance))


def mamba(nc, io, keep):
    with ExitStack() as ctx:
        sb = lambda n, s, d=F32: ctx.enter_context(nc.sbuf_tensor("m_" + n, s, d))
        own = dict(keep, used=[], XT=sb("XT", [P, T]), XN=sb("XN", [P, T]), U=sb("U", [P, 2, T]))
        with ExitStack() as inner:
            sb = lambda n, s, d=F32: inner.enter_context(nc.sbuf_tensor("m_" + n, s, d))
            own.update(DT=sb("DT", [P, 2, T]), G=sb("G", [P, T], F32R))
            mamba_front(nc, io, own)
            mamba_scan(nc, io, own)
        mamba_back(nc, io, own)


NT = T // P
PER = CH // P


E0 = 8
HID = 512
HM = HID // P
BIG = 1e30


def wide(ap, n):
    return ap.unsqueeze(2).broadcast_to([ap.shape[0], ap.shape[1], n])


def row_wide(ap, n):
    return ap.unsqueeze(1).broadcast_to([ap.shape[0], n, ap.shape[1]])


def ffn(nc, io, keep):
    X1, X2, X2t, ident, eps = keep["X1"], keep["X2"], keep["X2t"], keep["ident"], keep["eps"]
    with ExitStack() as ctx:
        sb = lambda n, s, d=F32: ctx.enter_context(nc.sbuf_tensor("f_" + n, s, d))
        sem = lambda n: ctx.enter_context(nc.semaphore("f_" + n))
        bank = lambda n: ctx.enter_context(nc.psum_tensor("f_" + n, [P, CH], F32))
        ACC = X2t
        X1t = sb("X1t", [P, NT, P])
        stage = sb("stage", [P, 2, CH])
        gate_w = sb("gate_w", [P, E0])
        sh_w = sb("sh_w", [P, P])
        sh_b = sb("sh_b", [1, PER, P])
        ones_row = sb("ones_row", [1, P])
        b2big = sb("b2big", [P, NT // 2, P])
        gamma = sb("gamma", [P, P])
        beta = sb("beta", [P, P])
        L = sb("L", [P, NT, E0])
        iota_i = sb("iota_i", [P, NT, E0], I32)
        iota = sb("iota", [P, NT, E0])
        oh = sb("oh", [P, 2, NT, E0])
        eq = sb("eq", [P, NT, E0])
        top = sb("top", [P, 2, NT])
        idx = sb("idx", [P, 2, NT])
        wt = sb("wt", [P, 3, NT])
        comb = sb("comb", [P, NT, E0])
        combE = sb("combE", [P, E0 * NT])
        combT = sb("combT", [P, 2, P])
        w1 = sb("w1", [P, 2, HID])
        w2 = sb("w2", [P, 2, HM, P])
        b1 = sb("b1", [P, 2, HM])
        HT = sb("HT", [P, 2, HM, CH])
        stats = sb("stats", [P, NT, 6])
        mv = sb("mv", [P, NT, 2])
        rstd = sb("rstd", [P, NT])
        ps_h = [bank(f"ps_h{m}") for m in range(HM)]
        ps_y = [bank(f"ps_y{k}") for k in range(2)]
        ps_t = [bank(f"ps_t{k}") for k in range(2)]
        s_w, s_b2, s_z, s_st, s_g, s_sh, s_tr = (sem(n) for n in ("weights", "b2_loaded", "zeroed", "staged", "logits", "shared", "transposed"))
        s_l, s_gelu, s_x1t, s_rt, s_exp, s_ct, s_ctc, s_b2m = (sem(n) for n in ("logits_copied", "shared_gelu", "x_token_major", "route", "gate_exp", "comb_t", "comb_t_copied", "b2_sum"))
        s_acc = sem("acc")
        s_ew = [sem(f"expert_weights{k}") for k in range(2)]
        s_h, s_ht, s_y = sem("hidden"), sem("hidden_gelu"), sem("expert_out")
        s_ln, s_sq, s_fin, s_x2 = sem("norm"), sem("norm_sqrt"), sem("x2_token_major"), sem("x2_transposed")

        ctx.enter_context(nc.allow_non_contiguous_dma(reason="small per-feature vectors"))
        block = ctx.enter_context(nc.Block())

        @block.sync
        def _(sp):
            for dst, src in (
                (gate_w[:], io["gate_w"]), (sh_w[:], io["sh_w"]),
                (sh_b[:], io["sh_b"].rearrange("(a b n) -> a b n", a=1, b=1).broadcast_to([1, PER, P])),
                (gamma[:], io["gamma"].rearrange("(a n) -> a n", a=1).broadcast_to([P, P])),
                (beta[:], io["beta"].rearrange("(a n) -> a n", a=1).broadcast_to([P, P])),
            ):
                sp.dma_start(dst, src).then_inc(s_w, 16)
            sp.wait_ge(s_z, 1)
            for t in range(NT // 2):
                sp.dma_start(b2big[t * E0:(t + 1) * E0, t, :], io["b2"]).then_inc(s_b2, 16)

            def weights(e, k):
                if past(e):
                    sp.wait_ge(s_y, (e - 1) * NCH)
                one_e = bass.ds(e, 1)
                sp.dma_start(w1[:, k, :], io["W1"][one_e].rearrange("a p n -> p (a n)")).then_inc(s_ew[k], 16)
                sp.dma_start(w2[:, k, :, :], io["W2"][one_e].rearrange("a (m p) n -> p (a m) n", p=P)).then_inc(s_ew[k], 16)
                sp.dma_start(b1[:, k, :], io["b1T"][one_e].rearrange("a p m -> p (a m)")).then_inc(s_ew[k], 16)
            twos(sp, E0, weights)

        @block.gpsimd
        def _(pool):
            nc.gpsimd.memset(b2big[:], 0.0).then_inc(s_z, 1)
            nc.gpsimd.memset(ones_row[:], 1.0).then_inc(s_z, 1)
            nc.gpsimd.iota(iota_i[:], pattern=[[0, NT], [1, E0]], base=0, channel_multiplier=0).then_inc(s_z, 1)

            def stage_in(i, k):
                if past(i):
                    pool.wait_ge(s_tr, i - 1)
                nc.gpsimd.tensor_copy(stage[:, k, :], chunk(X1, i)).then_inc(s_st, 1)
            twos(pool, NCH, stage_in)

        @block.scalar
        def _(act):
            nc.scalar.preload_act_table(ACT.Gelu)

            def shared(i, k):
                act.wait_ge(s_sh, i + 1)
                nc.scalar.activation(ACC[:, bass.ds(i * PER, PER), :].rearrange("p t n -> p (t n)"), ps_y[k][:], ACT.Gelu).then_inc(s_gelu, 1)
                act.wait_ge(s_tr, i + 1)
                nc.scalar.activation(X1t[:, bass.ds(i * PER, PER), :].rearrange("p t n -> p (t n)"), ps_t[k][:], ACT.Copy).then_inc(s_x1t, 1)
            twos(act, NCH, shared)
            act.wait_ge(s_rt, 15)
            nc.scalar.activation(wt[:, 2, :], wt[:, 0, :], ACT.Exp).then_inc(s_exp, 1)

            def hidden(e, i, ke, k):
                g = e * NCH + i
                for m in range(HM):
                    act.wait_ge(s_h, g * HM + m + 1)
                    if past(e, 1) or past(i):
                        act.wait_ge(s_y, g - 1)
                    nc.scalar.activation(HT[:, k, m, :], ps_h[m][:], ACT.Gelu, bias=b1[:, ke, m:m + 1]).then_inc(s_ht, 1)
            nc.scalar.preload_act_table(ACT.Gelu)
            twos(act, NCH, lambda i, k: hidden(0, i, 0, k))
            with act.Fori(0, NCH // 2) as j:
                for k in range(2):
                    hidden(1, j * 2 + k, 1, k)
            with act.Fori(1, E0 // 2) as ep:
                for ke in range(2):
                    with act.Fori(0, NCH // 2) as j:
                        for k in range(2):
                            hidden(ep * 2 + ke, j * 2 + k, ke, k)
            for r in range(2):
                act.wait_ge(s_ln, r * (3 * NT + 2 + 3) + 2 * NT + 1)
                nc.scalar.activation(rstd[:], rstd[:], ACT.Sqrt).then_inc(s_sq, 1)

            def x2_copy(i, k):
                act.wait_ge(s_x2, i + 1)
                nc.scalar.activation(chunk(X2, i), ps_t[k][:], ACT.Copy).then_inc(s_fin, 1)
            twos(act, NCH, x2_copy)

        @block.vector
        def _(dve):
            def logits(i, k):
                dve.wait_ge(s_g, i + 1)
                nc.vector.tensor_copy(L[:, bass.ds(i * PER, PER), :].rearrange("p t e -> p (t e)"), ps_h[k][:, 0:PER * E0]).then_inc(s_l, 1)
            twos(dve, NCH, logits)
            dve.wait_ge(s_z, 3)
            nc.vector.tensor_copy(iota[:], iota_i[:]).then_inc(s_rt, 1)
            dve.wait_ge(s_l, NCH)
            dve.wait_ge(s_rt, 1)
            n = 1
            for r in range(2):
                nc.vector.tensor_reduce(top[:, r, :], L[:], AX.X, ALU.max).then_inc(s_rt, 1)
                dve.wait_ge(s_rt, n + 1)
                nc.vector.tensor_tensor(eq[:], L[:], wide(top[:, r, :], E0), ALU.is_equal).then_inc(s_rt, 1)
                dve.wait_ge(s_rt, n + 2)
                nc.vector.scalar_tensor_tensor(out=eq[:], in0=eq[:], scalar=-float(E0), in1=iota[:], op0=ALU.mult, op1=ALU.add).then_inc(s_rt, 1)
                dve.wait_ge(s_rt, n + 3)
                nc.vector.tensor_reduce(idx[:, r, :], eq[:], AX.X, ALU.min).then_inc(s_rt, 1)
                dve.wait_ge(s_rt, n + 4)
                nc.vector.tensor_scalar(idx[:, r, :], idx[:, r, :], float(E0), None, ALU.add).then_inc(s_rt, 1)
                dve.wait_ge(s_rt, n + 5)
                nc.vector.tensor_tensor(oh[:, r], iota[:], wide(idx[:, r, :], E0), ALU.is_equal).then_inc(s_rt, 1)
                n += 6
                dve.wait_ge(s_rt, n)
                if r == 0:
                    nc.vector.scalar_tensor_tensor(out=L[:], in0=oh[:, 0], scalar=-BIG, in1=L[:], op0=ALU.mult, op1=ALU.add).then_inc(s_rt, 1)
                    n += 1
                    dve.wait_ge(s_rt, n)
            nc.vector.tensor_tensor(wt[:, 0, :], top[:, 1, :], top[:, 0, :], ALU.subtract).then_inc(s_rt, 1)
            dve.wait_ge(s_exp, 1)
            nc.vector.tensor_scalar(wt[:, 0, :], wt[:, 2, :], 1.0, None, ALU.add).then_inc(s_rt, 1)
            dve.wait_ge(s_rt, 16)
            nc.vector.reciprocal(wt[:, 1, :], wt[:, 0, :]).then_inc(s_rt, 1)
            dve.wait_ge(s_rt, 17)
            nc.vector.tensor_tensor(wt[:, 2, :], wt[:, 2, :], wt[:, 1, :], ALU.mult).then_inc(s_rt, 1)
            dve.wait_ge(s_rt, 18)
            for r in range(2):
                nc.vector.tensor_tensor(oh[:, r], oh[:, r], wide(wt[:, 1 + r, :], E0), ALU.mult).then_inc(s_rt, 1)
            dve.wait_ge(s_rt, 20)
            nc.vector.tensor_tensor(comb[:], oh[:, 0], oh[:, 1], ALU.add).then_inc(s_rt, 1)
            dve.wait_ge(s_rt, 21)
            nc.vector.tensor_copy(combE[:].rearrange("p (e t) -> p e t", e=E0), comb[:].rearrange("p t e -> p e t")).then_inc(s_rt, 1)
            for h in range(2):
                dve.wait_ge(s_ct, h + 1)
                nc.vector.tensor_copy(combT[:, h, :], ps_t[h][:, 0:P]).then_inc(s_ctc, 1)
            dve.wait_ge(s_gelu, NCH)

            def start_acc(i, k):
                dve.wait_ge(s_b2m, i + 1)
                part = ACC[:, bass.ds(i * PER, PER), :].rearrange("p t n -> p (t n)")
                nc.vector.scalar_tensor_tensor(out=part, in0=part, scalar=0.5, in1=ps_y[k][:], op0=ALU.mult, op1=ALU.add).then_inc(s_acc, PER)
            twos(dve, NCH, start_acc)
            dve.wait_ge(s_rt, 22)

            def add_expert(e, i, k):
                g = e * NCH + i
                dve.wait_ge(s_y, g + 1)
                for t in range(PER):
                    dve.wait_ge(s_acc, g * PER + t + 1)
                    tile = ACC[:, bass.ds(i * PER + t, 1), :].rearrange("p a n -> p (a n)")
                    nc.vector.scalar_tensor_tensor(out=tile, in0=ps_y[k][:, t * P:(t + 1) * P],
                                                   scalar=combE[:, bass.ds(e * NT + i * PER + t, 1)], in1=tile,
                                                   op0=ALU.mult, op1=ALU.add).then_inc(s_acc, 1)
            with dve.Fori(0, E0) as e:
                with dve.Fori(0, NCH // 2) as j:
                    for k in range(2):
                        add_expert(e, j * 2 + k, k)
            dve.wait_ge(s_w, 16 * 5)
            dve.wait_ge(s_acc, NT * (E0 + 1))

            def norm(n):
                for t in range(NT):
                    nc.vector.bn_stats(stats[:, t, :], ACC[:, t, :]).then_inc(s_ln, 1)
                for t in range(NT):
                    dve.wait_ge(s_ln, n + t + 1)
                    nc.vector.bn_aggr(mv[:, t, :], stats[:, t, :]).then_inc(s_ln, 1)
                dve.wait_ge(s_ln, n + 2 * NT)
                nc.vector.tensor_scalar(rstd[:], mv[:, :, 1], EPS, None, ALU.add).then_inc(s_ln, 1)
                dve.wait_ge(s_sq, 1 if n == 0 else 2)
                nc.vector.reciprocal(rstd[:], rstd[:]).then_inc(s_ln, 1)
                dve.wait_ge(s_ln, n + 2 * NT + 2)
                for t in range(NT):
                    nc.vector.tensor_scalar(ACC[:, t, :], ACC[:, t, :], mv[:, t, 0:1], rstd[:, t:t + 1],
                                            ALU.subtract, ALU.mult).then_inc(s_ln, 1)
                dve.wait_ge(s_ln, n + 3 * NT + 2)
                return n + 3 * NT + 2
            n = norm(0)
            dve.wait_ge(s_x1t, NCH)
            for other, op in ((row_wide(gamma[:], NT), ALU.mult), (row_wide(beta[:], NT), ALU.add), (X1t[:], ALU.add)):
                nc.vector.tensor_tensor(ACC[:], ACC[:], other, op).then_inc(s_ln, 1)
                n += 1
                dve.wait_ge(s_ln, n)
            norm(n)

        @block.tensor
        def _(pe):
            pe.wait_ge(s_w, 16 * 5)
            pe.wait_ge(s_z, 2)

            def token_major(i, k):
                pe.wait_ge(s_st, i + 1)
                tiles = [stage[:, k, t * P:(t + 1) * P] for t in range(PER)]
                if past(i):
                    pe.wait_ge(s_l, i - 1)
                for t in range(PER):
                    mm = nc.tensor.matmul(ps_h[k][:, t * E0:(t + 1) * E0], tiles[t], gate_w[:], start=True, stop=True)
                mm.then_inc(s_g, 1)
                if past(i):
                    pe.wait_ge(s_gelu, i - 1)
                nc.tensor.matmul(ps_y[k][:], ones_row[:], sh_b[:].rearrange("a t n -> a (t n)"), start=True, stop=False)
                for t in range(PER):
                    mm = nc.tensor.matmul(ps_y[k][:, t * P:(t + 1) * P], tiles[t], sh_w[:], start=False, stop=t == PER - 1)
                mm.then_inc(s_sh, 1)
                if past(i):
                    pe.wait_ge(s_x1t, i - 1)
                for t in range(PER):
                    mm = nc.tensor.transpose(ps_t[k][:, t * P:(t + 1) * P], tiles[t], ident[:])
                mm.then_inc(s_tr, 1)
            twos(pe, NCH, token_major)
            pe.wait_ge(s_rt, 21)
            pe.wait_ge(s_x1t, NCH)
            for h in range(2):
                nc.tensor.transpose(ps_t[h][:, 0:P], comb[:, h * 16:(h + 1) * 16, :].rearrange("p t e -> p (t e)"), ident[:]).then_inc(s_ct, 1)
            pe.wait_ge(s_b2, 16 * NT // 2)
            pe.wait_ge(s_ctc, 2)
            pe.wait_ge(s_gelu, NCH)

            for i in range(NCH):
                if i >= 2:
                    pe.wait_ge(s_acc, PER * (i - 1))
                cols = b2big[:, (i % 4) * PER:(i % 4 + 1) * PER, :].rearrange("p t n -> p (t n)")
                nc.tensor.matmul(ps_y[i % 2][:], combT[:, i // 4, :], cols, start=True, stop=True).then_inc(s_b2m, 1)

            def up(e, i, ke):
                g = e * NCH + i
                for m in range(HM):
                    if past(e, 1) or past(i, 1):
                        pe.wait_ge(s_ht, g * HM + m - HM + 1)
                    nc.tensor.matmul(ps_h[m][:], w1[:, ke, m * P:(m + 1) * P], chunk(X1, i), start=True, stop=True).then_inc(s_h, 1)

            def down(e, i, ke, k):
                g = e * NCH + i
                pe.wait_ge(s_ht, g * HM + HM)
                pe.wait_ge(s_acc, g * PER + NT - PER)
                for t in range(PER):
                    for m in range(HM):
                        mm = nc.tensor.matmul(ps_y[k][:, t * P:(t + 1) * P], HT[:, k, m, t * P:(t + 1) * P], w2[:, ke, m, :],
                                              start=m == 0, stop=m == HM - 1)
                mm.then_inc(s_y, 1)

            def expert(e, ke, first, last):
                if first:
                    up(e, 1, ke)
                    down(e, 0, ke, 0)
                    up(e, 2, ke)
                    down(e, 1, ke, 1)
                with pe.Fori(1 if first else 0, NCH // 2 - 1) as j:
                    for k in range(2):
                        up(e, j * 2 + k + 1, ke)
                        down(e, j * 2 + k, ke, k)
                up(e, NCH - 1, ke)
                down(e, NCH - 2, ke, 0)
                if not last:
                    pe.wait_ge(s_ew[1 - ke], (e + 1 - (1 - ke)) * 24 + 48)
                    up(e + 1, 0, 1 - ke)
                down(e, NCH - 1, ke, 1)
            pe.wait_ge(s_ew[0], 48)
            up(0, 0, 0)
            expert(0, 0, True, False)
            expert(1, 1, False, False)
            with pe.Fori(1, E0 // 2 - 1) as ep:
                for ke in range(2):
                    expert(ep * 2 + ke, ke, False, False)
            expert(E0 - 2, 0, False, False)
            expert(E0 - 1, 1, False, True)

            for i in range(NCH):
                pe.wait_ge(s_ln, (3 * NT + 2 + 3) + 2 * NT + 2 + (i + 1) * PER)
                if i >= 2:
                    pe.wait_ge(s_fin, i - 1)
                for t in range(PER):
                    mm = nc.tensor.transpose(ps_t[i % 2][:, t * P:(t + 1) * P], ACC[:, i * PER + t, :], ident[:])
                mm.then_inc(s_x2, 1)


NH = 16
DK = 8
PARTS = 3
GH = 4
NG = NH // GH
QT = SEQ // P
ROWS = PARTS * PARTS * DK
MROW = ROWS
VW = 32
NEG = -1e30
BLOCKS = [(c, kt, max(kt - c * PER, 0)) for c in range(2) for kt in range((c + 1) * PER)]
ITEMS = [(j, qt, c) for j in range(GH) for c in range(2) for qt in range(c * PER, QT)]
NB, NI = len(BLOCKS), len(ITEMS)
LOADS = 16 * (2 * PARTS + 1)
RP = 3


E1 = 64
TOPK = 4
CAP = P
SLOTS = E1 * CAP


def load_heads(sp, dram, keep, b, g, zeros):
    Q, K, s_ld = keep["Q"][g], keep["K"][g], keep["s_ld"][g]
    heads = lambda x: dram["qk"][x, :, bass.ds(b, 1), :, g * GH:(g + 1) * GH, :].rearrange("c b d j t -> c (b d) (j t)")
    for a in range(PARTS):
        rows = slice(a * PARTS * DK, (a + 1) * PARTS * DK)
        for buf, src in ((Q, heads(0)[a:a + 1].broadcast_to([PARTS, DK, GH * SEQ])), (K, heads(1))):
            sp.dma_start(buf[rows].rearrange("r j t -> r (j t)"), src).then_inc(s_ld, 16)
    sp.dma_start(Q[MROW:MROW + PARTS].rearrange("r j t -> r (j t)"), zeros).then_inc(s_ld, 16)


def attn_project(nc, io, keep, dram):
    X2, Vt, Q, K = keep["X2"], keep["Vt"], keep["Q"], keep["K"]
    with ExitStack() as ctx:
        sb = lambda n, s, d=F32: ctx.enter_context(nc.sbuf_tensor("p_" + n, s, d))
        sem = lambda n: ctx.enter_context(nc.semaphore("p_" + n))
        bank = lambda n: ctx.enter_context(nc.psum_tensor("p_" + n, [P, CH], F32))
        w = [sb(f"w{j}", [P, P]) for j in range(3)]
        bias = sb("bias", [P, 2])
        v_b = sb("v_b", [P, P])
        stage = sb("stage", [P, 2, CH])
        zero = sb("zero", [P, 2 * CH], BF16)
        parts = sb("parts", [P, 2, 2, PARTS, CH], BF16)
        rest = sb("rest", [P, 2, 2, CH])
        ps = [[bank(f"ps{k}{x}") for x in range(2)] for k in range(2)]
        ps_v = [bank(f"ps_v{k}") for k in range(2)]
        s_w, s_z, s_zd, s_ps, s_p0, s_r, s_p1, s_p2 = (sem(n) for n in ("weights", "zeroed", "zeros_stored", "qk_psum", "part0", "rest", "part1", "part2"))
        s_st, s_v, s_vt, s_q = sem("staged"), sem("v_psum"), sem("v"), sem("head_buffers")
        s_d = [sem(f"stored{k}") for k in range(2)]

        ctx.enter_context(nc.allow_non_contiguous_dma(reason="small per-feature vectors"))
        block = ctx.enter_context(nc.Block())

        @block.sync
        def _(sp):
            for dst, src in (
                [(w[j][:], io[n]) for j, n in enumerate(("Wq", "Wk", "Wv"))]
                + [(bias[:, j:j + 1], io[n].rearrange("h (k a) -> (h k) a", a=1)) for j, n in enumerate(("bq", "bk"))]
                + [(v_b[:], io["bv"].rearrange("(a h) k -> a (h k)", a=1).broadcast_to([P, P]))]
            ):
                sp.dma_start(dst, src).then_inc(s_w, 16)
            sp.wait_ge(s_z, 1)
            sp.dma_start(dram["zeros"].rearrange("r (a n) -> (r a) n", a=GH), zero[0:PARTS * GH, :]).then_inc(s_zd, 16)

            def store(i, k):
                for x in range(2):
                    sp.wait_ge(s_p2, i * 2 + x + 1)
                    for a in range(PARTS):
                        rows = dram["qk"][x, a, i // 2, :, :, k * CH:(k + 1) * CH].rearrange("d h t -> h d t")
                        sp.dma_start(rows, parts[:, k, x, a, :]).then_inc(s_d[k], 16)
            store(0, 0)
            store(1, 1)
            sp.wait_ge(s_zd, 16)
            for k in range(2):
                sp.wait_ge(s_d[k], 16 * 2 * PARTS)
            sp.wait_ge(s_q, 2)
            load_heads(sp, dram, keep, 0, 0, dram["zeros"])
            for i in range(2, NCH):
                store(i, i % 2)
            for k in range(2):
                sp.wait_ge(s_d[k], 16 * 2 * PARTS * NCH // 2)

        @block.gpsimd
        def _(pool):
            nc.gpsimd.memset(zero[:], 0.0).then_inc(s_z, 1)
            for i in range(NCH):
                if i >= 2:
                    pool.wait_ge(s_v, i - 1)
                nc.gpsimd.tensor_copy(stage[:, i % 2, :], chunk(X2, i)).then_inc(s_st, 1)
                if i % 2 == 0:
                    nc.gpsimd.memset(Q[i // 2][:].rearrange("p j t -> p (j t)").bitcast(F32), 0.0).then_inc(s_q, 1)
                else:
                    nc.gpsimd.memset(K[i // 2][:].rearrange("p j t -> p (j t)"), 1.0).then_inc(s_q, 1)

        @block.scalar
        def _(act):
            act.wait_ge(s_w, 16 * 6)

            def split(i, k):
                if past(i):
                    act.wait_ge(s_d[k], (i - k) * 16 * PARTS)
                for x in range(2):
                    act.wait_ge(s_ps, i * 2 + x + 1)
                    nc.scalar.activation(parts[:, k, x, 0, :], ps[k][x][:], ACT.Identity, bias=bias[:, x:x + 1]).then_inc(s_p0, 1)
                for x in range(2):
                    act.wait_ge(s_r, i * 2 + x + 1)
                    nc.scalar.activation(parts[:, k, x, 1, :], rest[:, k, x, :], ACT.Copy).then_inc(s_p1, 1)
            twos(act, NCH, split)

        @block.vector
        def _(dve):
            dve.wait_ge(s_w, 16 * 6)

            def third(i, k):
                for x in range(2):
                    dve.wait_ge(s_p1, i * 2 + x + 1)
                    nc.vector.tensor_tensor(parts[:, k, x, 2, :], rest[:, k, x, :], parts[:, k, x, 1, :], ALU.subtract).then_inc(s_p2, 1)

            def split(i, k):
                for x in range(2):
                    dve.wait_ge(s_p0, i * 2 + x + 1)
                    nc.vector.scalar_tensor_tensor(out=rest[:, k, x, :], in0=ps[k][x][:], scalar=bias[:, x:x + 1], in1=parts[:, k, x, 0, :],
                                                   op0=ALU.add, op1=ALU.subtract).then_inc(s_r, 1)
                dve.wait_ge(s_v, i + 1)
                nc.vector.tensor_tensor(Vt[:, bass.ds(i * PER, PER), :], ps_v[k][:].rearrange("p (t n) -> p t n", n=P),
                                        row_wide(v_b[:], PER), ALU.add).then_inc(s_vt, 1)
                third(i, k)
            twos(dve, NCH, split)

        @block.tensor
        def _(pe):
            pe.wait_ge(s_w, 16 * 6)

            def project(i, k):
                for x in range(2):
                    if past(i):
                        pe.wait_ge(s_r, i * 2 + x - 3)
                    nc.tensor.matmul(ps[k][x][:], w[x][:], chunk(X2, i), start=True, stop=True).then_inc(s_ps, 1)
                pe.wait_ge(s_st, i + 1)
                if past(i):
                    pe.wait_ge(s_vt, i - 1)
                for t in range(PER):
                    mm = nc.tensor.matmul(ps_v[k][:, t * P:(t + 1) * P], stage[:, k, t * P:(t + 1) * P], w[2][:], start=True, stop=True)
                mm.then_inc(s_v, 1)
            twos(pe, NCH, project)


def attn_scores(nc, io, keep, dram):
    Vt, CX, ident, Q, K, s_ld = keep["Vt"], keep["CX"], keep["ident"], keep["Q"], keep["K"], keep["s_ld"]
    with ExitStack() as ctx:
        sb = lambda n, s, d=F32: ctx.enter_context(nc.sbuf_tensor("t_" + n, s, d))
        sem = lambda n: ctx.enter_context(nc.semaphore("t_" + n))
        bank = lambda n, m=1: ctx.enter_context(nc.psum_tensor("t_" + n, [P, m * CH], F32))
        VG = sb("VG", [P, 2, QT, GH * VW])
        PT = sb("PT", [P, RP, GH, CH])
        CT = sb("CT", [P, 2, CH])
        den = sb("den", [P, 2, PER, GH])
        negm = sb("negm", [P, 2, GH, QT])
        negm2 = sb("negm2", [P, 2, GH, PER])
        msb = sb("msb", [GH * QT, P])
        mrest = sb("mrest", [GH * QT, P])
        mp = sb("mp", [GH * QT, 2, PARTS, P], BF16)
        maskf = sb("maskf", [P, P])
        mask = sb("mask", [P, P], BF16)
        identb = sb("identb", [P, P], BF16)
        ps_1 = [bank(f"ps_1{k}") for k in range(2)]
        ps_s = [bank(f"ps_s{p}", 2) for p in range(2)]
        ps_c = [bank(f"ps_c{c}") for c in range(2)]
        s_m, s_mb = sem("mask_f32"), sem("mask")
        s_ms = [sem(f"max_stored{g}") for g in range(NG)]
        s_ml = [sem(f"max_loaded{g}") for g in range(NG)]
        s_p1, s_mx, s_cmb, s_mt, s_mc, s_mp = (sem(n) for n in ("scores1", "maxed", "max_joined", "max_transposed", "max_copied", "max_parts"))
        s_st, s_exp, s_mk, s_pv, s_vg = (sem(n) for n in ("scores2", "exped", "masked", "context", "v_group"))
        s_ev, s_ct, s_cx = sem("context_copied"), sem("context_transposed"), sem("normed")
        s_pool, s_sp = sem("pool_step"), sem("sync_step")
        s_dr, s_mq = sem("reciprocal"), sem("max_chain")
        AHEAD = 2
        assert NB % RP == 0

        ctx.enter_context(nc.allow_non_contiguous_dma(reason="rows of heads"))
        block = ctx.enter_context(nc.Block())

        def batches(eng, body):
            with eng.Fori(0, BATCH - 1) as b:
                body(b, False)
            body(BATCH - 1, True)

        @block.sync
        def _(sp):
            def maxima(b, g):
                gi = b * NG + g
                sp.wait_ge(s_mp, gi + 2)
                for a in range(PARTS):
                    sp.dma_start(dram["max"][g, a].rearrange("(r n) -> r n", n=P), mp[:, g % 2, a, :]).then_inc(s_ms[g], 16)
                sp.wait_ge(s_ms[g], b * 16 * PARTS + 16 * PARTS)
                sp.wait_ge(s_p1, gi * NI + NI)
                sp.dma_start(Q[g][MROW:MROW + PARTS].rearrange("r j t -> r (j t)"), dram["max"][g]).then_inc(s_ml[g], 16)

            for g in range(1, NG):
                load_heads(sp, dram, keep, 0, g, dram["zeros"])
            maxima(0, 0)

            def body(b, last):
                for g in range(NG):
                    gi = b * NG + g
                    if not (last and g == NG - 1):
                        maxima(b + (g + 1) // NG, (g + 1) % NG)
                    if not last:
                        sp.wait_ge(s_st, gi * 2 * NB + 2 * NB)
                        sp.sem_inc(s_sp, 1)
                        sp.wait_ge(s_ml[g], b * 16 + 16)
                        load_heads(sp, dram, keep, b + 1, g, dram["zeros"])
            batches(sp, body)

        @block.gpsimd
        def _(pool):
            nc.gpsimd.memset(VG[:].rearrange("p k t n -> p (k t n)"), 0.0).then_inc(s_m, 1)
            nc.gpsimd.memset(maskf[:], 0.0).then_inc(s_m, 1)
            pool.wait_ge(s_m, 2)
            nc.gpsimd.affine_select(out=maskf[:], in_=maskf[:], compare_op=ALU.is_ge, fill=NEG, base=0,
                                    pattern=[[-1, P]], channel_multiplier=1).then_inc(s_m, 1)
            nc.gpsimd.memset(VG[:].rearrange("p k t (j n) -> p (k t j) n", n=VW)[:, :, DK:DK + 1], 1.0).then_inc(s_m, 1)
            pool.wait_ge(s_m, 4)

            def v_group(b, g):
                gi = b * NG + g
                if past(gi, 1):
                    pool.wait_ge(s_pv, gi * NB - NB + RP)
                out = VG[:, g % 2].rearrange("p t (j n) -> p t j n", n=VW)[:, :, :, 0:DK]
                src = Vt[:, bass.ds(b * QT, QT), g * GH * DK:(g + 1) * GH * DK].rearrange("p t (j k) -> p t j k", k=DK)
                for t in range(QT):
                    ins = nc.gpsimd.tensor_copy(out[:, t], src[:, t])
                ins.then_inc(s_vg, 1)
            v_group(0, 0)

            def body(b, last):
                for g in range(NG):
                    gi = b * NG + g
                    d = 0
                    for n, (c, kt, r) in enumerate(BLOCKS):
                        if n == 2 and not (last and g == NG - 1):
                            v_group(b + (g + 1) // NG, (g + 1) % NG)
                        if kt < c * PER:
                            continue
                        pool.wait_ge(s_exp, gi * 2 * NB + 2 * n + 2 + AHEAD)
                        pool.sem_inc(s_pool, 1)
                        part = PT[:, n % RP, :, 0:P]
                        nc.gpsimd.affine_select(out=part, in_=part, compare_op=ALU.is_ge, fill=0.0, base=0,
                                                pattern=[[0, GH], [1, P]], channel_multiplier=-1).then_inc(s_mk, 1)
            batches(pool, body)

        @block.scalar
        def _(act):
            act.sem_inc(s_exp, AHEAD)

            def context(b, g, c):
                gi = b * NG + g
                act.wait_ge(s_pv, gi * NB + (NB if c else PER) + RP)
                act.wait_ge(s_ct, gi * 2 + c - 1 + AHEAD)
                nc.scalar.activation(CT[:, c, :], ps_c[c][:], ACT.Copy).then_inc(s_ev, 1)

            def body(b, last):
                for g in range(NG):
                    gi = b * NG + g
                    for n, (c, kt, r) in enumerate(BLOCKS):
                        w = CH - r * P
                        for p in range(2):
                            act.wait_ge(s_st, gi * 2 * NB + 2 * n + p + 1)
                            act.wait_ge(s_pv, gi * NB + n + 1)
                            src = ps_s[p][:].rearrange("p (j t) -> p j t", j=2)[:, :, 0:w]
                            nc.scalar.activation(PT[:, n % RP, 2 * p:2 * p + 2, 0:w], src, ACT.Exp, scale=DK ** -0.5).then_inc(s_exp, 1)
                        if n == 1 and g > 0:
                            context(b, g - 1, 1)
                        if n == PER + 1:
                            context(b, g, 0)
                context(b, NG - 1, 1)
            batches(act, body)

        @block.vector
        def _(dve):
            dve.sem_inc(s_mx, AHEAD)
            dve.sem_inc(s_cx, AHEAD)
            dve.sem_inc(s_mp, 1)
            dve.wait_ge(s_m, 3)
            nc.vector.tensor_copy(mask[:], maskf[:]).then_inc(s_mb, 1)
            nc.vector.tensor_copy(identb[:], ident[:]).then_inc(s_mb, 1)

            def first_pass(b, g, n):
                gi = b * NG + g
                j, qt, c = ITEMS[n]
                width = min((qt + 1) * P - c * CH, CH)
                dve.wait_ge(s_p1, gi * NI + n + 1)
                out = (negm2[:, g % 2, j, qt - PER:qt - PER + 1] if c else negm[:, g % 2, j, qt:qt + 1])
                nc.vector.tensor_reduce(out, ps_1[n % 2][:, 0:width], AX.X, ALU.max, negate=True).then_inc(s_mx, 1)

            def join(b, g):
                gi = b * NG + g
                dve.wait_ge(s_mx, gi * NI + NI + AHEAD)
                nc.vector.tensor_tensor(negm[:, g % 2, :, PER:QT], negm[:, g % 2, :, PER:QT], negm2[:, g % 2], ALU.min).then_inc(s_cmb, 1)

            def parts(b, g):
                gi = b * NG + g
                dve.wait_ge(s_mt, gi + 1)
                dve.wait_ge(s_mp, gi + 1)
                nc.vector.tensor_copy(msb[:], ps_1[0][0:GH * QT, 0:P]).then_inc(s_mc, 1)
                dve.wait_ge(s_mc, gi + 1)
                nc.vector.tensor_copy(mp[:, g % 2, 0, :], msb[:]).then_inc(s_mq, 1)
                dve.wait_ge(s_mq, gi * 3 + 1)
                nc.vector.tensor_tensor(mrest[:], msb[:], mp[:, g % 2, 0, :], ALU.subtract).then_inc(s_mq, 1)
                dve.wait_ge(s_mq, gi * 3 + 2)
                nc.vector.tensor_copy(mp[:, g % 2, 1, :], mrest[:]).then_inc(s_mq, 1)
                dve.wait_ge(s_mq, gi * 3 + 3)
                nc.vector.tensor_tensor(mp[:, g % 2, 2, :], mrest[:], mp[:, g % 2, 1, :], ALU.subtract).then_inc(s_mp, 1)

            def divide(b, g, c):
                gi = b * NG + g
                dve.wait_ge(s_ct, gi * 2 + c + 1 + AHEAD)
                src = ps_c[c][:].rearrange("p (t j n) -> p t j n", t=PER, n=VW)
                nc.vector.reciprocal(den[:, c], src[:, :, :, DK]).then_inc(s_dr, 1)
                dve.wait_ge(s_dr, gi * 2 + c + 1)
                out = CX[:, bass.ds(b * QT + c * PER, PER), g * GH * DK:(g + 1) * GH * DK].rearrange("p t (j k) -> p t j k", k=DK)
                for t in range(PER):
                    ins = nc.vector.tensor_tensor(out[:, t], src[:, t, :, 0:DK], den[:, c, t].unsqueeze(2).broadcast_to([P, GH, DK]), ALU.mult)
                ins.then_inc(s_cx, 1)

            for n in range(NI):
                first_pass(0, 0, n)
            join(0, 0)
            parts(0, 0)
            for n in range(NI):
                first_pass(0, 1, n)
            join(0, 1)

            def body(b, last):
                for g in range(NG):
                    if not (last and g == NG - 1):
                        parts(b + (g + 1) // NG, (g + 1) % NG)
                    ahead = not (last and g >= NG - 2)
                    b2, g2 = b + (g + 2) // NG, (g + 2) % NG
                    if ahead:
                        for n in range(4 * PER):
                            first_pass(b2, g2, n)
                    if g > 0:
                        divide(b, g - 1, 1)
                    if ahead:
                        for n in range(4 * PER, 9 * PER):
                            first_pass(b2, g2, n)
                    divide(b, g, 0)
                    if ahead:
                        for n in range(9 * PER, NI):
                            first_pass(b2, g2, n)
                        join(b2, g2)
                divide(b, NG - 1, 1)
            batches(dve, body)

        @block.tensor
        def _(pe):
            pe.sem_inc(s_pv, RP)
            pe.sem_inc(s_ct, AHEAD)
            pe.wait_ge(s_mb, 2)

            def item(b, g, n):
                gi = b * NG + g
                j, qt, c = ITEMS[n]
                width = min((qt + 1) * P - c * CH, CH)
                diagonal = qt // PER == c
                if n == 0:
                    pe.wait_ge(s_ld[g], (b + 1) * LOADS)
                    if past(gi, 1):
                        pe.wait_ge(s_mc, gi)
                pe.wait_ge(s_mx, gi * NI + n - 1 + AHEAD)
                mm = nc.tensor.matmul(ps_1[n % 2][:, 0:width], Q[g][:, j, qt * P:(qt + 1) * P], K[g][:, j, c * CH:c * CH + width],
                                      start=True, stop=not diagonal, skip_group_check=True)
                if diagonal:
                    mm = nc.tensor.matmul(ps_1[n % 2][:, width - P:width], identb[:], mask[:], start=False, stop=True,
                                          skip_group_check=True)
                mm.then_inc(s_p1, 1)

            def turn_max(b, g):
                gi = b * NG + g
                pe.wait_ge(s_cmb, gi + 1)
                nc.tensor.transpose(ps_1[0][0:GH * QT, 0:P], negm[:, g % 2].rearrange("p j t -> p (j t)"), ident[:]).then_inc(s_mt, 1)

            def scores(b, g, n, p):
                gi = b * NG + g
                c, kt, r = BLOCKS[n]
                w = CH - r * P
                pe.wait_ge(s_exp, gi * 2 * NB + 2 * n + p - 1 + AHEAD)
                for h in range(2):
                    mm = nc.tensor.matmul(ps_s[p][:, h * CH:h * CH + w], K[g][:, 2 * p + h, kt * P:(kt + 1) * P],
                                          Q[g][:, 2 * p + h, c * CH + r * P:(c + 1) * CH], start=True, stop=True)
                mm.then_inc(s_st, 1)

            def product(b, g, n):
                gi = b * NG + g
                c, kt, r = BLOCKS[n]
                w = CH - r * P
                if kt >= c * PER:
                    pe.wait_ge(s_mk, gi * 2 * PER + c * PER + (kt - c * PER) + 1)
                else:
                    pe.wait_ge(s_exp, gi * 2 * NB + 2 * n + 2 + AHEAD)
                if kt == 0:
                    pe.wait_ge(s_cx, gi * 2 + c - 1 + AHEAD)
                for j in range(GH):
                    mm = nc.tensor.matmul(ps_c[c][j * VW:(j + 1) * VW, r * P:CH], VG[:, g % 2, kt, j * VW:(j + 1) * VW],
                                          PT[:, n % RP, j, 0:w], start=kt == 0, stop=kt == (c + 1) * PER - 1, skip_group_check=True)
                mm.then_inc(s_pv, 1)

            def turn_context(b, g, c):
                gi = b * NG + g
                pe.wait_ge(s_ev, gi * 2 + c + 1)
                for t in range(PER):
                    mm = nc.tensor.transpose(ps_c[c][:, t * P:(t + 1) * P], CT[:, c, t * P:(t + 1) * P], ident[:])
                mm.then_inc(s_ct, 1)

            for n in range(NI):
                item(0, 0, n)
            turn_max(0, 0)
            for n in range(NI):
                item(0, 1, n)

            def body(b, last):
                for g in range(NG):
                    ahead = not (last and g >= NG - 2)
                    b2, g2 = b + (g + 2) // NG, (g + 2) % NG
                    if not (last and g == NG - 1):
                        turn_max(b + (g + 1) // NG, (g + 1) % NG)
                    pe.wait_ge(s_ml[g], b * 16 + 16)
                    pe.wait_ge(s_vg, b * NG + g + 1)
                    for n in range(NB):
                        for p in range(2):
                            scores(b, g, n, p)
                            if ahead:
                                item(b2, g2, PER * n + p)
                        if n >= 2:
                            product(b, g, n - 2)
                        elif g > 0:
                            product(b, g - 1, NB - 2 + n)
                        if n == 3 and g > 0:
                            turn_context(b, g - 1, 1)
                        if n == 7:
                            turn_context(b, g, 0)
                        if ahead:
                            item(b2, g2, PER * n + 2)
                            item(b2, g2, PER * n + 3)
                product(b, NG - 1, NB - 2)
                product(b, NG - 1, NB - 1)
                turn_context(b, NG - 1, 1)
            batches(pe, body)


def attn_out(nc, io, keep, slots):
    CX, X, LG, ident = keep["CX"], keep["X2t"], keep["LG"], keep["ident"]
    with ExitStack() as ctx:
        sb = lambda n, s, d=F32: ctx.enter_context(nc.sbuf_tensor("o_" + n, s, d))
        sem = lambda n: ctx.enter_context(nc.semaphore("o_" + n))
        bank = lambda n: ctx.enter_context(nc.psum_tensor("o_" + n, [P, CH], F32))
        w = sb("w", [P, P])
        bo = sb("bo", [1, PER, P])
        ones_row = sb("ones_row", [1, P])
        CXT = sb("CXT", [P, 2, CH])
        stats = sb("stats", [P, NT, 6])
        mv = sb("mv", [P, NT, 2])
        rstd = sb("rstd", [P, NT])
        router = sb("router", [P, E1])
        zero = sb("zero", [P, SLOTS // 4])
        ps_t = [bank(f"ps_t{k}") for k in range(2)]
        ps_o = [bank(f"ps_o{k}") for k in range(2)]
        ps_l = [bank(f"ps_l{k}") for k in range(2)]
        s_w, s_z, s_t, s_c, s_o, s_r, s_ln, s_sq, s_n, s_x, s_xc = (sem(n) for n in (
            "weights", "zeroed", "turned", "copied", "out", "residual", "norm", "sqrt", "normed", "x_turned", "x_copied"))
        s_l, s_lc, s_zb = sem("logits"), sem("logits_copied"), sem("slots_zeroed")

        ctx.enter_context(nc.allow_non_contiguous_dma(reason="rows of heads"))
        block = ctx.enter_context(nc.Block())

        @block.sync
        def _(sp):
            sp.dma_start(w[:], io["Wo"]).then_inc(s_w, 16)
            sp.dma_start(bo[:], io["bo"].rearrange("(a b n) -> a b n", a=1, b=1).broadcast_to([1, PER, P])).then_inc(s_w, 16)
            sp.dma_start(router[:], io["router_w"]).then_inc(s_w, 16)
            sp.wait_ge(s_z, 2)
            for q in range(4):
                rows = slots[q * (SLOTS // 4):(q + 1) * (SLOTS // 4), :].rearrange("(p a) n -> p (a n)", p=P)
                sp.dma_start(rows, zero[:]).then_inc(s_zb, 16)
            sp.wait_ge(s_zb, 64)

        @block.gpsimd
        def _(pool):
            nc.gpsimd.memset(ones_row[:], 1.0).then_inc(s_z, 1)
            nc.gpsimd.memset(zero[:], 0.0).then_inc(s_z, 1)

        @block.scalar
        def _(act):
            for i in range(NCH):
                act.wait_ge(s_t, i + 1)
                if i >= 2:
                    act.wait_ge(s_o, i - 1)
                nc.scalar.activation(CXT[:, i % 2, :], ps_t[i % 2][:], ACT.Copy).then_inc(s_c, 1)
            act.wait_ge(s_ln, 2 * NT + 1)
            nc.scalar.activation(rstd[:], rstd[:], ACT.Sqrt).then_inc(s_sq, 1)
            for i in range(NCH):
                act.wait_ge(s_x, i + 1)
                if i >= 2:
                    act.wait_ge(s_l, i - 1)
                nc.scalar.activation(CXT[:, i % 2, :], ps_t[i % 2][:], ACT.Copy).then_inc(s_xc, 1)

        @block.vector
        def _(dve):
            for i in range(NCH):
                dve.wait_ge(s_o, i + 1)
                rows = X[:, i * PER:(i + 1) * PER, :].rearrange("p t n -> p (t n)")
                nc.vector.tensor_tensor(rows, rows, ps_o[i % 2][:], ALU.add).then_inc(s_r, 1)
                dve.wait_ge(s_r, i + 1)
                for t in range(PER):
                    nc.vector.bn_stats(stats[:, i * PER + t, :], X[:, i * PER + t, :]).then_inc(s_ln, 1)
            for t in range(NT):
                dve.wait_ge(s_ln, t + 1)
                nc.vector.bn_aggr(mv[:, t, :], stats[:, t, :]).then_inc(s_ln, 1)
            dve.wait_ge(s_ln, 2 * NT)
            nc.vector.tensor_scalar(rstd[:], mv[:, :, 1], EPS, None, ALU.add).then_inc(s_ln, 1)
            dve.wait_ge(s_sq, 1)
            nc.vector.reciprocal(rstd[:], rstd[:]).then_inc(s_ln, 1)
            dve.wait_ge(s_ln, 2 * NT + 2)
            for t in range(NT):
                nc.vector.tensor_scalar(X[:, t, :], X[:, t, :], mv[:, t, 0:1], rstd[:, t:t + 1],
                                        ALU.subtract, ALU.mult).then_inc(s_n, 1)
            for i in range(NCH):
                dve.wait_ge(s_l, i + 1)
                nc.vector.tensor_copy(LG[:, i * PER:(i + 1) * PER, :].rearrange("p t e -> p (t e)"), ps_l[i % 2][:, 0:PER * E1]).then_inc(s_lc, 1)

        @block.tensor
        def _(pe):
            pe.wait_ge(s_w, 48)
            pe.wait_ge(s_z, 1)

            def turn(i):
                if i >= 2:
                    pe.wait_ge(s_c, i - 1)
                for t in range(PER):
                    mm = nc.tensor.transpose(ps_t[i % 2][:, t * P:(t + 1) * P], CX[:, i * PER + t, :], ident[:])
                mm.then_inc(s_t, 1)
            turn(0)
            for i in range(NCH):
                if i + 1 < NCH:
                    turn(i + 1)
                pe.wait_ge(s_c, i + 1)
                if i >= 2:
                    pe.wait_ge(s_r, i - 1)
                nc.tensor.matmul(ps_o[i % 2][:], ones_row[:], bo[:].rearrange("a t n -> a (t n)"), start=True, stop=False)
                for t in range(PER):
                    mm = nc.tensor.matmul(ps_o[i % 2][:, t * P:(t + 1) * P], CXT[:, i % 2, t * P:(t + 1) * P], w[:], start=False, stop=t == PER - 1)
                mm.then_inc(s_o, 1)
            pe.wait_ge(s_c, NCH)

            def turn_x(i):
                pe.wait_ge(s_n, (i + 1) * PER)
                if i >= 2:
                    pe.wait_ge(s_xc, i - 1)
                for t in range(PER):
                    mm = nc.tensor.transpose(ps_t[i % 2][:, t * P:(t + 1) * P], X[:, i * PER + t, :], ident[:])
                mm.then_inc(s_x, 1)
            turn_x(0)
            for i in range(NCH):
                if i + 1 < NCH:
                    turn_x(i + 1)
                pe.wait_ge(s_xc, i + 1)
                if i >= 2:
                    pe.wait_ge(s_lc, i - 1)
                for t in range(PER):
                    mm = nc.tensor.matmul(ps_l[i % 2][:, t * E1:(t + 1) * E1], CXT[:, i % 2, t * P:(t + 1) * P], router[:], start=True, stop=True)
                mm.then_inc(s_l, 1)


def attention(nc, io, keep, slots):
    dram = dict(
        qk=nc.dram_tensor("qk_parts", [2, PARTS, BATCH, DK, NH, SEQ], BF16).ap(),
        zeros=nc.dram_tensor("zero_rows", [PARTS, GH * SEQ], BF16).ap(),
        max=nc.dram_tensor("max_parts", [NG, PARTS, GH * SEQ], BF16).ap(),
    )
    with ExitStack() as ctx:
        sb = lambda n, s, d=F32: ctx.enter_context(nc.sbuf_tensor("c_" + n, s, d))
        own = dict(keep, Vt=sb("Vt", [P, NT, P]), CX=sb("CX", [P, NT, P]),
                   Q=[sb(f"Q{g}", [P, GH, SEQ], BF16) for g in range(NG)], K=[sb(f"K{g}", [P, GH, SEQ], BF16) for g in range(NG)],
                   s_ld=[ctx.enter_context(nc.semaphore(f"heads_loaded{g}")) for g in range(NG)])
        attn_project(nc, io, own, dram)
        attn_scores(nc, io, own, dram)
        attn_out(nc, io, own, slots)


I1 = 64
GE = 4
NGE = E1 // GE
QTR = NT // BATCH
BEYOND = 1 << 17


def moe_route(nc, io, keep, slots):
    X, LG, prob, idx_g = keep["X2t"], keep["LG"], keep["prob"], keep["idx_g"]
    with ExitStack() as ctx:
        sb = lambda n, s, d=F32: ctx.enter_context(nc.sbuf_tensor("r_" + n, s, d))
        sem = lambda n: ctx.enter_context(nc.semaphore("r_" + n))
        bank = lambda n: ctx.enter_context(nc.psum_tensor("r_" + n, [P, CH], F32))
        top = sb("top", [P, NT, 8])
        idx = sb("idx", [P, NT, 8], U32)
        idxf = sb("idxf", [P, NT, 8])
        ex = sb("ex", [P, NT, E1])
        ex4 = sb("ex4", [P, NT, TOPK])
        den = sb("den", [P, NT])
        iota_i = sb("iota_i", [P, QTR, E1], I32)
        iota = sb("iota", [P, QTR, E1])
        oh = sb("oh", [P, TOPK, QTR, E1])
        pair = sb("pair", [P, 2, QTR, E1])
        M = sb("M", [P, 2, QTR, E1], BF16)
        trif = sb("trif", [P, P])
        tri = sb("tri", [P, P], BF16)
        ones = sb("ones", [P, P], BF16)
        base = sb("base", [P, NT + 1, E1])
        pos = sb("pos", [P, QTR, E1])
        posj = sb("posj", [P, TOPK, QTR])
        slot = sb("slot", [P, TOPK, QTR])
        over = sb("over", [P, TOPK, QTR])
        idx_s = sb("idx_s", [P, TOPK, NT], I32)
        ps_p = [bank(f"ps_p{k}") for k in range(2)]
        ps_n = [bank(f"ps_n{k}") for k in range(2)]
        s_z, s_c, s_t, s_i, s_e, s_pr = (sem(n) for n in ("shapes", "consts", "top", "index", "exp", "probs"))
        s_m, s_r, s_b, s_x, s_sc, s_zw = (sem(n) for n in ("mask", "rank", "chain", "slots", "scattered", "w2_zeroed"))

        block = ctx.enter_context(nc.Block())

        @block.sync
        def _(sp):
            for e in range(0, E1, GE):
                sp.dma_start(keep["w1"][:, e:e + GE, :], io["w1"][e:e + GE].rearrange("e d f -> d e f")).then_inc(keep["s_ew"], 16)
            sp.wait_ge(s_zw, 1)
            for q in range(2):
                src = io["w2"].rearrange("(c q) i n -> q i c n", q=2)[q]
                dst = keep["w2"][q * I1:(q + 1) * I1, q:E1:2, :]
                sp.dma_start(dst, src).then_inc(keep["s_ew"], 16)

        @block.gpsimd
        def _(pool):
            nc.gpsimd.iota(iota_i[:], pattern=[[0, QTR], [1, E1]], base=0, channel_multiplier=0).then_inc(s_z, 1)
            nc.gpsimd.memset(trif[:], 1.0).then_inc(s_z, 1)
            pool.wait_ge(s_z, 2)
            nc.gpsimd.affine_select(out=trif[:], in_=trif[:], compare_op=ALU.is_gt, fill=0.0, base=0,
                                    pattern=[[1, P]], channel_multiplier=-1).then_inc(s_z, 1)
            nc.gpsimd.memset(keep["w2"][:].rearrange("p e n -> p (e n)"), 0.0).then_inc(s_zw, 1)
            for q in range(BATCH):
                pool.wait_ge(s_x, q + 1)
                for t in range(q * QTR, (q + 1) * QTR):
                    for j in range(TOPK):
                        pool.indirect_dma_start(out=slots, out_offset=bass.IndirectOffsetOnAxis(ap=idx_s[:, j, t:t + 1].bitcast(U32), axis=0),
                                                in_=X[:, t, :], in_offset=None, bounds_check=SLOTS - 1,
                                                oob_is_err=False).then_inc(s_sc, 16)
            pool.wait_ge(s_sc, 16 * TOPK * NT)

        @block.scalar
        def _(act):
            act.wait_ge(s_e, 2)
            nc.scalar.activation(ex[:], ex[:], ACT.Exp).then_inc(s_pr, 1)
            nc.scalar.activation(ex4[:], ex4[:], ACT.Exp).then_inc(s_pr, 1)

        @block.vector
        def _(dve):
            dve.wait_ge(s_z, 3)
            nc.vector.tensor_copy(iota[:], iota_i[:]).then_inc(s_c, 1)
            nc.vector.tensor_copy(tri[:], trif[:]).then_inc(s_c, 1)
            nc.vector.memset(ones[:], 1.0).then_inc(s_c, 1)
            nc.vector.memset(base[:, 0, :], 0.0).then_inc(s_c, 1)
            for t in range(NT):
                nc.vector.max(top[:, t, :], LG[:, t, :]).then_inc(s_t, 1)
            for t in range(NT):
                dve.wait_ge(s_t, t + 1)
                nc.vector.max_index(idx[:, t, :], top[:, t, :], LG[:, t, :]).then_inc(s_i, 1)
            dve.wait_ge(s_i, NT)
            nc.vector.tensor_copy(idxf[:], idx[:]).then_inc(s_i, 1)
            nc.vector.tensor_tensor(ex[:], LG[:], wide(top[:, :, 0], E1), ALU.subtract).then_inc(s_e, 1)
            nc.vector.tensor_tensor(ex4[:], top[:, :, 0:TOPK], wide(top[:, :, 0], TOPK), ALU.subtract).then_inc(s_e, 1)
            dve.wait_ge(s_i, NT + 1)
            dve.wait_ge(s_c, 4)

            n = 0

            def link(ins):
                nonlocal n
                n += 1
                ins.then_inc(s_b, 1)
                dve.wait_ge(s_b, n)

            for q in range(BATCH):
                tiles = slice(q * QTR, (q + 1) * QTR)
                for j in range(TOPK):
                    ins = nc.vector.tensor_tensor(oh[:, j], iota[:], wide(idxf[:, tiles, j], E1), ALU.is_equal)
                    if j < TOPK - 1:
                        ins.then_inc(s_b, 1)
                        n += 1
                link(ins)
                for j in range(2):
                    ins = nc.vector.tensor_tensor(pair[:, j], oh[:, 2 * j], oh[:, 2 * j + 1], ALU.add)
                    if j == 0:
                        ins.then_inc(s_b, 1)
                        n += 1
                link(ins)
                nc.vector.tensor_tensor(M[:, q % 2], pair[:, 0], pair[:, 1], ALU.add).then_inc(s_m, 1)
                dve.wait_ge(s_r, 2 * q + 2)
                for t in range(QTR):
                    g = q * QTR + t
                    link(nc.vector.tensor_tensor(base[:, g + 1, :], base[:, g, :], ps_n[q % 2][:, t * E1:(t + 1) * E1], ALU.add))
                link(nc.vector.tensor_tensor(pos[:], ps_p[q % 2][:].rearrange("p (t e) -> p t e", e=E1), base[:, tiles, :], ALU.add))
                for j in range(TOPK):
                    ins = nc.vector.tensor_tensor(oh[:, j], oh[:, j], pos[:], ALU.mult)
                    if j < TOPK - 1:
                        ins.then_inc(s_b, 1)
                        n += 1
                link(ins)
                link(nc.vector.tensor_reduce(posj[:], oh[:], AX.X, ALU.add))
                experts = idxf[:, tiles, 0:TOPK].rearrange("p t j -> p j t")
                link(nc.vector.tensor_scalar(slot[:], posj[:], float(CAP - 1), None, ALU.min))
                link(nc.vector.scalar_tensor_tensor(out=slot[:], in0=experts, scalar=float(CAP), in1=slot[:], op0=ALU.mult, op1=ALU.add))
                link(nc.vector.tensor_copy(idx_g[:, :, tiles], slot[:]))
                link(nc.vector.tensor_scalar(over[:], posj[:], float(CAP), float(BEYOND), ALU.is_ge, ALU.mult))
                link(nc.vector.tensor_tensor(over[:], over[:], slot[:], ALU.add))
                nc.vector.tensor_copy(idx_s[:, :, tiles], over[:]).then_inc(s_x, 1)
            dve.wait_ge(s_pr, 2)
            link(nc.vector.tensor_reduce(den[:], ex[:], AX.X, ALU.add))
            link(nc.vector.reciprocal(den[:], den[:]))
            link(nc.vector.tensor_tensor(prob[:], ex4[:], wide(den[:], TOPK), ALU.mult))

        @block.tensor
        def _(pe):
            pe.wait_ge(s_c, 4)
            for q in range(BATCH):
                pe.wait_ge(s_m, q + 1)
                if q >= 2:
                    pe.wait_ge(s_x, q - 1)
                rows = M[:, q % 2].rearrange("p t e -> p (t e)")
                nc.tensor.matmul(ps_n[q % 2][:], ones[:], rows, start=True, stop=True).then_inc(s_r, 1)
                nc.tensor.matmul(ps_p[q % 2][:], tri[:], rows, start=True, stop=True).then_inc(s_r, 1)


def moe_experts(nc, io, keep, slots, outs):
    ident, w1, w2 = keep["ident"], keep["w1"], keep["w2"]
    RX = 4
    with ExitStack() as ctx:
        sb = lambda n, s, d=F32: ctx.enter_context(nc.sbuf_tensor("e_" + n, s, d))
        sem = lambda n: ctx.enter_context(nc.semaphore("e_" + n))
        bank = lambda n: ctx.enter_context(nc.psum_tensor("e_" + n, [P, CH], F32))
        x = sb("x", [P, RX, GE, P])
        xT = sb("xT", [P, 2, CH])
        S = sb("S", [P, 2, GE, I1])
        H = sb("H", [P, 2, GE, I1])
        HT = sb("HT", [P, 2, GE // 2, P])
        Y = sb("Y", [P, 2, GE, P])
        ps_x = [bank(f"ps_x{k}") for k in range(2)]
        ps_h = [bank(f"ps_h{k}") for k in range(2)]
        ps_t = [bank(f"ps_t{k}") for k in range(2)]
        ps_y = [bank(f"ps_y{k}") for k in range(2)]
        s_ld = [sem(f"loaded{r}") for r in range(RX)]
        s_st = [sem(f"stored{k}") for k in range(2)]
        s_x, s_xc, s_u, s_s, s_h, s_t, s_tc, s_y, s_yc = (sem(n) for n in (
            "turned", "copied", "up", "silu", "gated", "h_turned", "h_copied", "out", "out_copied"))

        block = ctx.enter_context(nc.Block())

        def ring(eng, step):
            for r in range(RX):
                step(r, r)
            with eng.Fori(1, NGE // RX) as j:
                for r in range(RX):
                    step(j * RX + r, r)

        @block.sync
        def _(sp):
            def load(i, r):
                if past(i, RX):
                    sp.wait_ge(s_x, i - (RX - 1))
                sp.dma_start(x[:, r], slots[bass.ds(i * (GE * CAP), GE * CAP), :].rearrange("(e s) n -> s e n", e=GE)).then_inc(s_ld[r], 16)
            ring(sp, load)

        @block.gpsimd
        def _(pool):
            def store(i, k):
                pool.wait_ge(s_yc, i + 1)
                pool.dma_start(outs[bass.ds(i * (GE * CAP), GE * CAP), :].rearrange("(e s) n -> s e n", e=GE), Y[:, k]).then_inc(s_st[k], 16)
            twos(pool, NGE, store)
            for k in range(2):
                pool.wait_ge(s_st[k], 16 * NGE // 2)

        @block.scalar
        def _(act):
            nc.scalar.preload_act_table(ACT.Silu)

            def x_copy(i, k):
                act.wait_ge(s_x, i + 1)
                if past(i):
                    act.wait_ge(s_u, i - 1)
                nc.scalar.activation(xT[:, k, :], ps_x[k][:], ACT.Copy).then_inc(s_xc, 1)

            def silu(i, k):
                act.wait_ge(s_u, i + 1)
                if past(i):
                    act.wait_ge(s_h, i - 1)
                half = ps_h[k][:].rearrange("p (e n) -> p e n", e=GE)[:, :, 0:I1]
                nc.scalar.activation(S[:, k], half, ACT.Silu).then_inc(s_s, 1)

            def h_copy(i, k):
                act.wait_ge(s_t, i + 1)
                if past(i):
                    act.wait_ge(s_y, i - 1)
                nc.scalar.activation(HT[:, k].rearrange("p c n -> p (c n)"), ps_t[k][:, 0:GE // 2 * P], ACT.Copy).then_inc(s_tc, 1)
            x_copy(0, 0)

            def step(i, k):
                if not (isinstance(i, int) and i == NGE - 1):
                    x_copy(i + 1, 1 - k)
                silu(i, k)
                h_copy(i, k)
            step(0, 0)
            step(1, 1)
            with act.Fori(1, NGE // 2 - 1) as j:
                for k in range(2):
                    step(j * 2 + k, k)
            step(NGE - 2, 0)
            step(NGE - 1, 1)

        @block.vector
        def _(dve):
            def step(i, k):
                dve.wait_ge(s_s, i + 1)
                if past(i):
                    dve.wait_ge(s_t, i - 1)
                half = ps_h[k][:].rearrange("p (e n) -> p e n", e=GE)[:, :, I1:2 * I1]
                nc.vector.tensor_tensor(H[:, k], S[:, k], half, ALU.mult).then_inc(s_h, 1)
                dve.wait_ge(s_y, i + 1)
                if past(i):
                    dve.wait_ge(s_st[k], (i - k) * 8)
                nc.vector.tensor_copy(Y[:, k].rearrange("p e n -> p (e n)"), ps_y[k][:]).then_inc(s_yc, 1)
            twos(dve, NGE, step)

        @block.tensor
        def _(pe):
            pe.wait_ge(keep["s_ew"], 16 * (NGE + 2))

            def turn(i, k, r):
                pe.wait_ge(s_ld[r], (i - r) * (16 // RX) + 16)
                if past(i):
                    pe.wait_ge(s_xc, i - 1)
                for e in range(GE):
                    mm = nc.tensor.transpose(ps_x[k][:, e * P:(e + 1) * P], x[:, r, e, :], ident[:])
                mm.then_inc(s_x, 1)

            def up(i, k):
                pe.wait_ge(s_xc, i + 1)
                if past(i):
                    pe.wait_ge(s_h, i - 1)
                for e in range(GE):
                    w = w1[:, bass.ds(i * GE + e, 1), :].rearrange("p a n -> p (a n)")
                    mm = nc.tensor.matmul(ps_h[k][:, e * P:(e + 1) * P], xT[:, k, e * P:(e + 1) * P], w, start=True, stop=True)
                mm.then_inc(s_u, 1)

            def turn_hidden(i, k):
                pe.wait_ge(s_h, i + 1)
                if past(i):
                    pe.wait_ge(s_tc, i - 1)
                for c in range(GE // 2):
                    mm = nc.tensor.transpose(ps_t[k][:, c * P:(c + 1) * P], H[:, k, 2 * c:2 * c + 2, :].rearrange("p e n -> p (e n)"), ident[:])
                mm.then_inc(s_t, 1)

            def down(i, k):
                pe.wait_ge(s_tc, i + 1)
                if past(i):
                    pe.wait_ge(s_yc, i - 1)
                for e in range(GE):
                    w = w2[:, bass.ds(i * GE + e, 1), :].rearrange("p a n -> p (a n)")
                    mm = nc.tensor.matmul(ps_y[k][:, e * P:(e + 1) * P], HT[:, k, e // 2, :], w, start=True, stop=True)
                mm.then_inc(s_y, 1)

            def step(i, k, r):
                turn(i + 1, 1 - k, (r + 1) % RX)
                up(i, k)
                if past(i, 1):
                    down(i - 1, 1 - k)
                turn_hidden(i, k)

            turn(0, 0, 0)
            for r in range(RX):
                step(r, r % 2, r)
            with pe.Fori(1, NGE // RX - 1) as j:
                for r in range(RX):
                    step(j * RX + r, r % 2, r)
            for i in range(NGE - RX, NGE - 1):
                step(i, i % 2, i % RX)
            up(NGE - 1, 1)
            down(NGE - 2, 0)
            turn_hidden(NGE - 1, 1)
            down(NGE - 1, 1)


def moe_combine(nc, io, keep, outs, out):
    X, prob, idx_g = keep["X2t"], keep["prob"], keep["idx_g"]
    RING = 4
    with ExitStack() as ctx:
        sb = lambda n, s, d=F32: ctx.enter_context(nc.sbuf_tensor("y_" + n, s, d))
        sem = lambda n: ctx.enter_context(nc.semaphore("y_" + n))
        Yg = sb("Yg", [P, RING, TOPK, P])
        stats = sb("stats", [P, NT, 6])
        mv = sb("mv", [P, NT, 2])
        rstd = sb("rstd", [P, NT])
        s_g = [sem(f"gathered{k}") for k in range(RING)]
        s_a, s_b, s_v, s_q, s_r, s_n, s_o = (sem(n) for n in ("added", "stats", "variance", "sqrt", "rstd", "normed", "stored"))

        block = ctx.enter_context(nc.Block())
        rows = out.rearrange("b (t p) n -> p (b t) n", p=P)

        @block.gpsimd
        def _(pool):
            for t in range(NT):
                if t >= RING:
                    pool.wait_ge(s_a, TOPK * (t - RING + 1))
                for j in range(TOPK):
                    pool.indirect_dma_start(out=Yg[:, t % RING, j, :], out_offset=None, in_=outs,
                                            in_offset=bass.IndirectOffsetOnAxis(ap=idx_g[:, j, t:t + 1].bitcast(U32), axis=0),
                                            bounds_check=SLOTS - 1, oob_is_err=False).then_inc(s_g[t % RING], 16)

        @block.scalar
        def _(act):
            with act.Fori(0, BATCH) as q:
                act.wait_ge(s_v, q + 1)
                part = rstd[:, bass.ds(q * QTR, QTR)]
                nc.scalar.activation(part, part, ACT.Sqrt).then_inc(s_q, 1)

        @block.vector
        def _(dve):
            for t in range(NT):
                dve.wait_ge(s_g[t % RING], 16 * TOPK * (t // RING + 1))
                for j in range(TOPK):
                    nc.vector.scalar_tensor_tensor(out=X[:, t, :], in0=Yg[:, t % RING, j, :], scalar=prob[:, t, j:j + 1], in1=X[:, t, :],
                                                   op0=ALU.mult, op1=ALU.add).then_inc(s_a, 1)
                    dve.wait_ge(s_a, TOPK * t + j + 1)
                nc.vector.bn_stats(stats[:, t, :], X[:, t, :]).then_inc(s_b, 1)
                dve.wait_ge(s_b, 2 * t + 1)
                nc.vector.bn_aggr(mv[:, t, :], stats[:, t, :]).then_inc(s_b, 1)
                if t % QTR == QTR - 1:
                    q = t // QTR
                    tiles = slice(q * QTR, (q + 1) * QTR)
                    dve.wait_ge(s_b, 2 * t + 2)
                    nc.vector.tensor_scalar(rstd[:, tiles], mv[:, tiles, 1], EPS, None, ALU.add).then_inc(s_v, 1)
                    dve.wait_ge(s_q, q + 1)
                    nc.vector.reciprocal(rstd[:, tiles], rstd[:, tiles]).then_inc(s_r, 1)
                    dve.wait_ge(s_r, q + 1)
                    for u in range(q * QTR, (q + 1) * QTR):
                        nc.vector.tensor_scalar(X[:, u, :], X[:, u, :], mv[:, u, 0:1], rstd[:, u:u + 1],
                                                ALU.subtract, ALU.mult).then_inc(s_n, 1)

        @block.sync
        def _(sp):
            with sp.Fori(0, BATCH) as q:
                sp.wait_ge(s_n, q * QTR + QTR)
                sp.dma_start(rows[:, bass.ds(q * QTR, QTR), :], X[:, bass.ds(q * QTR, QTR), :]).then_inc(s_o, 16)
            sp.wait_ge(s_o, 16 * BATCH)


def moe(nc, io, keep, slots, out):
    outs = nc.dram_tensor("slot_outputs", [SLOTS, P], F32).ap()
    with ExitStack() as ctx:
        own = dict(keep, w1=ctx.enter_context(nc.sbuf_tensor("experts_w1", [P, E1, 2 * I1], F32)),
                   w2=ctx.enter_context(nc.sbuf_tensor("experts_w2", [P, E1, P], F32)),
                   s_ew=ctx.enter_context(nc.semaphore("expert_weights")))
        moe_route(nc, io, own, slots)
        moe_experts(nc, io, own, slots, outs)
    moe_combine(nc, io, keep, outs, out)


def build(nc, io, out):
    slots = nc.dram_tensor("slots", [SLOTS, P], F32).ap()
    with ExitStack() as ctx:
        sb = lambda n, s, d=F32: ctx.enter_context(nc.sbuf_tensor(n, s, d))
        keep = dict(ones=sb("mean_ones", [P, P]), eps=sb("eps", [P, 1]), one=sb("one", [P, 1]), ident=sb("ident", [P, P]))
        keep["X1"] = sb("X1", [P, T])
        mamba(nc, io, keep)
        keep["X2"] = sb("X2", [P, T])
        keep["X2t"] = sb("X2t", [P, NT, P])
        ffn(nc, io, keep)
        keep["LG"] = sb("LG", [P, NT, E1])
        attention(nc, io, keep, slots)
        keep["prob"] = sb("prob", [P, NT, TOPK])
        keep["idx_g"] = sb("idx_g", [P, TOPK, NT], I32)
        moe(nc, io, keep, slots, out)


def kernel(**inputs):
    import concourse.bacc as _bacc
    from concourse.bass_utils import run_bass_kernel_spmd as _run

    mixer = lambda n: inputs["L0_attn_" + n]
    gated = lambda n: inputs["L0_ffn_" + n]
    laid = dict(
        xT=mixer("x").reshape(T, P).T, norm_w=mixer("norm_w"), in_wT=mixer("in_proj_w").T,
        conv_w=mixer("conv_w"), conv_b=mixer("conv_b"), xp_w=mixer("x_proj_w"), xp_wT=mixer("x_proj_w").T, dt_wT=mixer("dt_proj_w").T,
        dt_b=mixer("dt_proj_b"), A_log=mixer("A_log"), D=mixer("D"), out_wT=mixer("out_proj_w").T, norm_f_w=mixer("norm_f_w"),
        gate_w=gated("gate_W"), sh_w=gated("shared_W"), sh_b=gated("shared_b"), gamma=gated("gamma"), beta=gated("beta"),
        b2=gated("b2"), W1=gated("W1"), W2=gated("W2"), b1T=gated("b1").reshape(E0, HM, P).transpose(0, 2, 1),
        router_w=inputs["L1_ffn_router_w"], w1=inputs["L1_ffn_w1"], w2=inputs["L1_ffn_w2"],
        **{n: inputs["L1_attn_" + n].transpose(1, 0, 2).reshape(P, P) for n in ("Wq", "Wk", "Wv")},
        **{n: inputs["L1_attn_" + n] for n in ("Wo", "bq", "bk", "bv", "bo")},
    )
    nc = _bacc.Bacc("TRN2", target_bir_lowering=False, num_devices=1)
    arrays, io = {}, {}
    for name, a in laid.items():
        a = np.ascontiguousarray(a)
        arrays[f"in_{name}_dram"] = a
        io[name] = nc.dram_tensor(f"in_{name}_dram", a.shape, mybir.dt.from_np(a.dtype), kind="ExternalInput").ap()
    out = nc.dram_tensor("out_0_dram", (BATCH, SEQ, P), F32, kind="ExternalOutput").ap()
    build(nc, io, out)
    r = _run(nc, [arrays], core_ids=[0])
    return r.results[0]["out_0_dram"]
```

```python
from contextlib import ExitStack

import numpy as np

import concourse.bass as bass
from concourse import mybir

F32 = mybir.dt.float32
F32R = mybir.dt.float32r
BF16 = mybir.dt.bfloat16
I32 = mybir.dt.int32
U32 = mybir.dt.uint32
ALU = mybir.AluOpType
ACT = mybir.ActivationFunctionType
AX = mybir.AxisListType

P = 128
T = 4096
BATCH = 4
SEQ = T // BATCH
CH = 512
NCH = T // CH
EPS = 1e-5
LN_EXP = "natural_log_exp_and_others"


def chunk(tile, i, n=CH):
    return tile[:, bass.ds(i * n, n)]


def chunk2(tile, c, i, n=CH):
    return tile[:, c, bass.ds(i * n, n)]


def twos(eng, n, step):
    step(0, 0)
    step(1, 1)
    with eng.Fori(1, n // 2) as j:
        for k in range(2):
            step(j * 2 + k, k)


def past(i, n=2):
    return not (isinstance(i, int) and i < n)


D_IN = 256
NST = 16
RANK = 16
TAPS = 4
RING = 4


def mamba_front(nc, io, keep):
    XN, U, DT, G, XT = keep["XN"], keep["U"], keep["DT"], keep["G"], keep["XT"]
    with ExitStack() as ctx:
        sb = lambda n, s, d=F32: ctx.enter_context(nc.sbuf_tensor("a_" + n, s, d))
        sem = lambda n: ctx.enter_context(nc.semaphore(n))
        bank = lambda n: ctx.enter_context(nc.psum_tensor(n, [P, CH], F32))
        pad = SEQ + TAPS - 1
        XB = sb("XB", [P, 2, BATCH * pad])
        SQ = sb("SQ", [P, 2, CH])
        R = sb("R", [P, 2, CH])
        E = sb("E", [P, 2, 2, CH])
        L = sb("L", [P, 2, 2, CH])
        W = sb("W", [P, 2, 2, CH])
        ones = keep["ones"]
        in_w = sb("in_w", [P, D_IN])
        conv_w = sb("conv_w", [P, 2, TAPS])
        conv_b = sb("conv_b", [P, 2])
        norm_w = sb("norm_w", [P, 1])
        xp_bc = sb("xp_bc", [P, 2, P])
        low = sb("low", [P, 1])
        xp_dt = sb("xp_dt", [RANK, D_IN])
        dt_w = sb("dt_w", [RANK, D_IN])
        dt_full = sb("dt_full", [P, 2, D_IN])
        dt_b = sb("dt_b", [P, 2])
        eps, one, ident, selw = keep["eps"], keep["one"], keep["ident"], keep["selw"]
        ps_rms = [bank(f"ps_rms{k}") for k in range(2)]
        ps_x = [bank(f"ps_x{c}") for c in range(2)]
        ps_bc = [bank(f"ps_bc{k}") for k in range(2)]
        ps_dt = [[bank(f"ps_dt{c}") for c in range(2)], ps_x]
        s_w = sem("a_weights")
        s_zero = sem("a_zeroed")
        s_id = sem("a_identity")
        s_xp = sem("a_xp_loaded")
        s_x = [sem(f"a_x_loaded{b}") for b in range(BATCH)]
        s_sq = sem("a_squares")
        s_ms = sem("a_mean_square")
        s_lnr = sem("a_ln_rms")
        s_r = sem("a_inv_rms")
        s_xn = sem("a_normed")
        s_xps = sem("a_x_proj_psum")
        s_xb = sem("a_x_branch")
        s_tap = sem("a_tap")
        s_cv = sem("a_conv")
        s_u = sem("a_silu")
        s_wp = sem("a_dt_weight_psum")
        s_wc = sem("a_dt_weight")
        s_bcps = sem("a_bc_psum")
        s_hi = sem("a_bc_high")
        s_g = sem("a_bc_split")
        s_dtps = sem("a_dt_psum")
        s_abs = sem("a_abs_dt")
        s_rel = sem("a_relu_dt")
        s_e = sem("a_exp_dt")
        s_l = sem("a_ln_dt")
        s_t = sem("a_one_plus_exp")
        s_t1 = sem("a_rounded_off")
        s_t2 = sem("a_relu_and_rounded_off")
        s_c = sem("a_softplus")
        s_low = sem("a_low_rows")
        s_sel = sem("a_selector_column")
        s_own = sem("a_own_step")
        keep["used"] += [s_w, s_zero, s_id, s_xp, *s_x, s_sq, s_ms, s_lnr, s_r, s_xn, s_xps, s_xb, s_tap, s_cv, s_u,
                         s_wp, s_wc, s_bcps, s_hi, s_g, s_dtps, s_abs, s_rel, s_e, s_l, s_t, s_t1, s_t2, s_c, s_low, s_sel, s_own]

        ctx.enter_context(nc.allow_non_contiguous_dma(reason="small per-feature vectors"))
        block = ctx.enter_context(nc.Block())

        @block.sync
        def _(sp):
            for b in range(BATCH):
                cols = slice(b * SEQ, (b + 1) * SEQ)
                sp.dma_start(XT[:, cols], io["xT"][:, cols]).then_inc(s_x[b], 16)
                if b == 0:
                    for dst, src in (
                        (norm_w[:], io["norm_w"].rearrange("(p a) -> p a", a=1)),
                        (in_w[:], io["in_wT"][:, 0:D_IN]),
                        (conv_w[:], io["conv_w"].rearrange("(c p) k -> p c k", p=P)),
                        (conv_b[:], io["conv_b"].rearrange("(c p) -> p c", p=P)),
                        (xp_dt[:], io["xp_w"][0:RANK, :]),
                        (dt_w[:], io["dt_wT"]),
                        (dt_b[:], io["dt_b"].rearrange("(c p) -> p c", p=P)),
                    ):
                        sp.dma_start(dst, src).then_inc(s_w, 16)
            sp.wait_ge(s_zero, 2)
            for col, src in ((0, RANK), (32, RANK), (64, RANK + NST), (96, RANK + NST)):
                sp.dma_start(xp_bc[:, :, col:col + NST],
                             io["xp_wT"].rearrange("(c p) n -> p c n", p=P)[:, :, src:src + NST]).then_inc(s_xp, 16)

        @block.gpsimd
        def _(pool):
            nc.gpsimd.memset(ones[:], 1.0 / P).then_inc(s_zero, 1)
            nc.gpsimd.memset(xp_bc[:], 0.0).then_inc(s_zero, 1)
            nc.gpsimd.memset(eps[:], EPS).then_inc(s_zero, 1)
            nc.gpsimd.memset(one[:], 1.0).then_inc(s_zero, 1)
            for c in range(2):
                for b in range(BATCH):
                    nc.gpsimd.memset(XB[:, c, b * pad:b * pad + TAPS - 1], 0.0).then_inc(s_zero, 1)
            nc.gpsimd.memset(ident[:], 0.0).then_inc(s_id, 1)
            pool.wait_ge(s_id, 1)
            nc.gpsimd.affine_select(out=ident[:], in_=ident[:], compare_op=ALU.not_equal, fill=1.0, base=0,
                                    pattern=[[-1, P]], channel_multiplier=1).then_inc(s_id, 1)
            nc.gpsimd.memset(selw[:], 0.0).then_inc(s_sel, 1)
            for q in range(4):
                pool.wait_ge(s_sel, q + 1)
                half = selw[:, (q // 2) * NST:(q // 2 + 1) * NST, :]
                nc.gpsimd.affine_select(out=half, in_=half, compare_op=ALU.not_equal, fill=1.0, base=-32 * q,
                                        pattern=[[-1, NST], [0, P // 4]], channel_multiplier=1).then_inc(s_sel, 1)

            def rounded_off(i, k):
                for c in range(2):
                    pool.wait_ge(s_t, i * 2 + c + 1)
                    nc.gpsimd.tensor_tensor(W[:, k, c, :], E[:, k, c, :], W[:, k, c, :], ALU.subtract).then_inc(s_t1, 1)
                for c in range(2):
                    pool.wait_ge(s_t1, i * 2 + c + 1)
                    pool.wait_ge(s_rel, i * 2 + c + 1)
                    pool.sem_inc(s_own, 1)
                    nc.gpsimd.tensor_tensor(chunk2(DT, c, i), chunk2(DT, c, i), W[:, k, c, :], ALU.add).then_inc(s_t2, 1)
            twos(pool, NCH, rounded_off)

        @block.scalar
        def _(act):
            nc.scalar.preload_act_table_set(LN_EXP)
            act.wait_ge(s_zero, 4)

            def square(i, k):
                if past(i):
                    act.wait_ge(s_ms, i - 1)
                nc.scalar.activation(SQ[:, k, :], chunk(XT, i), ACT.Square).then_inc(s_sq, 1)

            def inverse(i, k):
                act.wait_ge(s_ms, i + 1)
                if past(i):
                    act.wait_ge(s_xn, i - 1)
                nc.scalar.activation(R[:, k, :], ps_rms[k][:], ACT.Ln, bias=eps[:, 0:1]).then_inc(s_lnr, 1)
                act.wait_ge(s_lnr, i + 1)
                nc.scalar.activation(R[:, k, :], R[:, k, :], ACT.Exp, scale=-0.5).then_inc(s_r, 1)

            def branch(b, h):
                for c in range(2):
                    act.wait_ge(s_xps, b * 4 + h * 2 + c + 1)
                    nc.scalar.activation(XB[:, c, bass.ds(b * pad + TAPS - 1 + h * CH, CH)], ps_x[c][:],
                                         ACT.Copy).then_inc(s_xb, 1)

            for h in range(2):
                act.wait_ge(s_x[0], 16)
                square(h, h)
                if h == 1:
                    inverse(0, 0)
            for b in range(1, BATCH):
                act.wait_ge(s_x[b], 16)
                for h in range(2):
                    square(b * 2 + h, h)
                    inverse(b * 2 + h - 1, 1 - h)
                    branch(b - 1, h)
            inverse(NCH - 1, 1)
            for h in range(2):
                branch(BATCH - 1, h)
            act.wait_ge(s_wp, 1)
            nc.scalar.activation(dt_full[:].rearrange("p c n -> p (c n)"), ps_bc[0][:], ACT.Copy).then_inc(s_wc, 1)
            nc.scalar.preload_act_table(ACT.Silu)
            with act.Fori(0, NCH) as i:
                for c in range(2):
                    act.wait_ge(s_cv, i * 2 + c + 1)
                    act.sem_inc(s_own, 1)
                    nc.scalar.activation(chunk2(U, c, i), chunk2(U, c, i), ACT.Silu).then_inc(s_u, 1)
            nc.scalar.preload_act_table_set(LN_EXP)

            def exps(i, k):
                act.wait_ge(s_bcps, i + 1)
                nc.scalar.activation(chunk(G, i), ps_bc[k][:], ACT.Copy).then_inc(s_hi, 1)
                for c in range(2):
                    act.wait_ge(s_dtps, i * 2 + c + 1)
                    if past(i):
                        act.wait_ge(s_t1, i * 2 + c - 3)
                    nc.scalar.activation(E[:, k, c, :], ps_dt[k][c][:], ACT.Abs, bias=dt_b[:, c:c + 1]).then_inc(s_abs, 1)
                for c in range(2):
                    act.wait_ge(s_abs, i * 2 + c + 1)
                    nc.scalar.activation(E[:, k, c, :], E[:, k, c, :], ACT.Exp, scale=-1.0).then_inc(s_e, 1)
                for c in range(2):
                    act.wait_ge(s_e, i * 2 + c + 1)
                    if past(i):
                        act.wait_ge(s_c, i * 2 + c - 3)
                    nc.scalar.activation(L[:, k, c, :], E[:, k, c, :], ACT.Ln, bias=one[:, 0:1]).then_inc(s_l, 1)
            twos(act, NCH, exps)

        @block.vector
        def _(dve):
            for q in range(4):
                nc.vector.memset(low[q * 32:(q + 1) * 32], -float(q % 2)).then_inc(s_low, 1)
            dve.wait_ge(s_w, 16 * 7)

            def normed(i, k):
                dve.wait_ge(s_r, i + 1)
                nc.vector.scalar_tensor_tensor(out=chunk(XN, i), in0=chunk(XT, i), scalar=norm_w[:, 0:1],
                                               in1=R[:, k, :], op0=ALU.mult, op1=ALU.mult).then_inc(s_xn, 1)

            def conv(b, h):
                i = b * 2 + h
                for c in range(2):
                    dve.wait_ge(s_xb, i * 2 + c + 1)
                for k in range(TAPS):
                    for c in range(2):
                        src = XB[:, c, bass.ds(b * pad + h * CH + k, CH)]
                        out = chunk2(U, c, i)
                        if k == 0:
                            ins = nc.vector.tensor_scalar(out, src, conv_w[:, c, 0:1], conv_b[:, c:c + 1], ALU.mult, ALU.add)
                        else:
                            dve.wait_ge(s_tap, i * (2 * TAPS - 2) + 2 * (k - 1) + c + 1)
                            ins = nc.vector.scalar_tensor_tensor(out=out, in0=src, scalar=conv_w[:, c, k:k + 1],
                                                                 in1=out, op0=ALU.mult, op1=ALU.add)
                        ins.then_inc(s_cv if k == TAPS - 1 else s_tap, 1)
            dve.wait_ge(s_x[0], 16)
            normed(0, 0)
            normed(1, 1)
            dve.wait_ge(s_zero, 4 + 2 * BATCH)
            for b in range(1, BATCH):
                dve.wait_ge(s_x[b], 16)
                for h in range(2):
                    normed(b * 2 + h, h)
                    conv(b - 1, h)
            for h in range(2):
                conv(BATCH - 1, h)

            def add_ln(i, k):
                for c in range(2):
                    dve.wait_ge(s_l, i * 2 + c + 1)
                    dve.wait_ge(s_t2, i * 2 + c + 1)
                    nc.vector.tensor_tensor(chunk2(DT, c, i), chunk2(DT, c, i), L[:, k, c, :], ALU.add).then_inc(s_c, 1)

            def softplus(i, k):
                dve.wait_ge(s_hi, i + 1)
                nc.vector.scalar_tensor_tensor(out=chunk(G, i), in0=chunk(G, i).bitcast(F32), scalar=low[:, 0:1],
                                               in1=ps_bc[k][:], op0=ALU.mult, op1=ALU.add).then_inc(s_g, 1)
                for c in range(2):
                    dve.wait_ge(s_abs, i * 2 + c + 1)
                    nc.vector.tensor_scalar(chunk2(DT, c, i), ps_dt[k][c][:], dt_b[:, c:c + 1], 0.0,
                                            ALU.add, ALU.max).then_inc(s_rel, 1)
                for c in range(2):
                    dve.wait_ge(s_e, i * 2 + c + 1)
                    if past(i):
                        dve.wait_ge(s_t2, i * 2 + c - 3)
                    nc.vector.tensor_scalar(W[:, k, c, :], E[:, k, c, :], 1.0, -1.0, ALU.add, ALU.add).then_inc(s_t, 1)
                if past(i, 1):
                    add_ln(i - 1, 1 - k)
            dve.wait_ge(s_low, 4)
            twos(dve, NCH, softplus)
            add_ln(NCH - 1, 1)

        @block.tensor
        def _(pe):
            pe.wait_ge(s_zero, 3)

            def mean_square(i, k):
                pe.wait_ge(s_sq, i + 1)
                if past(i):
                    pe.wait_ge(s_lnr, i - 1)
                nc.tensor.matmul(ps_rms[k][:], ones[:], SQ[:, k, :], start=True, stop=True).then_inc(s_ms, 1)

            def x_branch(i):
                pe.wait_ge(s_xn, i + 1)
                for c in range(2):
                    if past(i, 1):
                        pe.wait_ge(s_xb, i * 2 + c - 1)
                    nc.tensor.matmul(ps_x[c][:], in_w[:, c * P:(c + 1) * P], chunk(XN, i),
                                     start=True, stop=True).then_inc(s_xps, 1)
            mean_square(0, 0)
            mean_square(1, 1)
            pe.wait_ge(s_w, 16 * 7)
            x_branch(0)
            with pe.Fori(1, NCH // 2) as j:
                for k in range(2):
                    mean_square(j * 2 + k, k)
                    x_branch(j * 2 + k - 1)
            x_branch(NCH - 1)
            for c in range(2):
                mm = nc.tensor.matmul(ps_bc[0][:, c * D_IN:(c + 1) * D_IN], xp_dt[:, c * P:(c + 1) * P], dt_w[:], start=True, stop=True)
            mm.then_inc(s_wp, 1)
            pe.wait_ge(s_wc, 1)
            pe.wait_ge(s_xp, 16 * 4)
            pe.wait_ge(s_xb, 2 * NCH)

            def x_proj(i, k):
                pe.wait_ge(s_u, i * 2 + 2)
                if past(i):
                    pe.wait_ge(s_g, i - 1)
                for c in range(2):
                    mm = nc.tensor.matmul(ps_bc[k][:], xp_bc[:, c, :], chunk2(U, c, i), start=c == 0, stop=c == 1)
                mm.then_inc(s_bcps, 1)
                for c in range(2):
                    if past(i):
                        pe.wait_ge(s_rel, i * 2 + c - 3)
                    for d in range(2):
                        mm = nc.tensor.matmul(ps_dt[k][c][:], dt_full[:, d, c * P:(c + 1) * P], chunk2(U, d, i), start=d == 0, stop=d == 1)
                    mm.then_inc(s_dtps, 1)
            twos(pe, NCH, x_proj)


def mamba_scan(nc, io, keep):
    U, DT, G = keep["U"], keep["DT"], keep["G"]
    with ExitStack() as ctx:
        sb = lambda n, s, d=F32: ctx.enter_context(nc.sbuf_tensor("s_" + n, s, d))
        sem = lambda n: ctx.enter_context(nc.semaphore(n))
        bank = lambda n: ctx.enter_context(nc.psum_tensor(n, [P, CH], F32))
        sel = sb("sel", [P, 2 * NST, P], F32R)
        ident, selw = keep["ident"], keep["selw"]
        A = sb("A", [P, 2, NST])
        Dw = sb("D", [P, 2])
        DU = sb("DU", [P, 2, 2, CH])
        dA = sb("dA", [P, 2, 2, CH])
        H = sb("H", [P, 2, 2, CH])
        HC = sb("HC", [P, RING, 2, CH])
        diag = sb("diag", [P, 2, P])
        C_sb = sb("C_sb", [P, 2, CH])
        last = sb("last", [P, 2, NST])
        ps_b = [bank(f"ps_b{k}") for k in range(2)]
        ps_d = [bank(f"ps_d{k}") for k in range(2)]
        ps_c = [bank(f"ps_c{k}") for k in range(2)]
        ps_y = [bank(f"ps_y{c}") for c in range(2)]
        s_w = sem("s_weights")
        s_sel = sem("s_sel")
        s_a = sem("s_A")
        s_b = sem("s_b_spread")
        s_c = sem("s_c_spread")
        s_da = sem("s_decay")
        s_cs = sem("s_c_copied")
        s_du = sem("s_dt_u")
        s_in = sem("s_input")
        s_h = sem("s_state")
        s_hl = sem("s_state_saved")
        s_hc = sem("s_c_times_state")
        s_y = sem("s_y_added")
        s_out = sem("s_y_out")
        s_own = sem("s_own_step")
        keep["used"] += [s_w, s_sel, s_a, s_b, s_c, s_da, s_cs, s_du, s_in, s_h, s_hl, s_hc, s_y, s_out, s_own]

        ctx.enter_context(nc.allow_non_contiguous_dma(reason="small per-feature vectors"))
        block = ctx.enter_context(nc.Block())
        N = NST

        @block.sync
        def _(sp):
            sp.dma_start(A[:], io["A_log"].rearrange("(c p) n -> p c n", p=P)).then_inc(s_w, 16)
            sp.dma_start(Dw[:], io["D"].rearrange("(c p) -> p c", p=P)).then_inc(s_w, 16)

        @block.gpsimd
        def _(pool):
            def times_c(i, g):
                k = g % 2
                pool.wait_ge(s_cs, i * N + g + 1)
                for c in range(2):
                    pool.wait_ge(s_h, i * 2 * N + 2 * g + c + 1)
                    if past(i, 1) or g >= RING:
                        pool.wait_ge(s_y, i * 2 * N + 2 * (g - RING) + c + 1)
                    nc.gpsimd.tensor_tensor(HC[:, g % RING, c, :], H[:, k, c, :], C_sb[:, k, :], ALU.mult).then_inc(s_hc, 1)
            for g in range(N):
                times_c(0, g)
            with pool.Fori(1, NCH) as i:
                for g in range(N):
                    times_c(i, g)

        @block.scalar
        def _(act):
            nc.scalar.preload_act_table_set(LN_EXP)
            act.wait_ge(s_w, 32)
            nc.scalar.activation(A[:], A[:], ACT.Exp).then_inc(s_a, 1)
            act.wait_ge(s_a, 2)

            def save(g):
                nc.scalar.activation(last[:, :, g], H[:, g % 2, :, CH - 1], ACT.Copy).then_inc(s_hl, 1)

            def y_out(i):
                for c in range(2):
                    act.wait_ge(s_y, i * 2 * N + 2 * N - 1 + c)
                    act.sem_inc(s_own, 1)
                    nc.scalar.activation(chunk2(U, c, i), ps_y[c][:], ACT.Copy).then_inc(s_out, 1)

            def chunk_of(b, h):
                i = b * 2 + h
                for g in range(N):
                    k = g % 2
                    if past(i, 1) or g >= 2:
                        act.wait_ge(s_h, i * 2 * N + 2 * (g - 1))
                        if h == 0 and g >= 2:
                            save(g - 2)
                        elif h == 1 and g < 2:
                            save(N - 2 + g)
                        else:
                            act.sem_inc(s_own, 1)
                    for c in range(2):
                        nc.scalar.activation(dA[:, k, c, :], chunk2(DT, c, i), ACT.Exp,
                                             scale=A[:, c, g:g + 1]).then_inc(s_da, 1)
                    act.wait_ge(s_c, i * N + g + 1)
                    if past(i, 1) or g >= 2:
                        act.wait_ge(s_hc, i * 2 * N + 2 * (g - 1))
                    nc.scalar.activation(C_sb[:, k, :], ps_c[k][:], ACT.Copy).then_inc(s_cs, 1)
                    if g == 2 and past(i, 1):
                        y_out(i - 1)
            chunk_of(0, 0)
            chunk_of(0, 1)
            with act.Fori(1, BATCH) as b:
                for h in range(2):
                    chunk_of(b, h)
            y_out(NCH - 1)

        @block.vector
        def _(dve):
            for q in range(4):
                nc.vector.tensor_copy(sel[:, :, q * 32:(q + 1) * 32], selw[:]).then_inc(s_sel, 1)
            dve.wait_ge(s_a, 1)
            nc.vector.tensor_scalar(A[:], A[:], -1.0, None, ALU.mult).then_inc(s_a, 1)
            dve.wait_ge(s_w, 32)
            for c in range(2):
                nc.vector.tensor_scalar(diag[:, c, :], ident[:], Dw[:, c:c + 1], None, ALU.mult).then_inc(s_sel, 1)

            def chunk_of(b, h):
                i = b * 2 + h
                for c in range(2):
                    nc.vector.tensor_tensor(DU[:, h, c, :], chunk2(DT, c, i), chunk2(U, c, i), ALU.mult).then_inc(s_du, 1)
                for g in range(N):
                    k = g % 2
                    dve.wait_ge(s_b, i * N + g + 1)
                    for c in range(2):
                        if g == 0:
                            dve.wait_ge(s_du, i * 2 + c + 1)
                        if past(i, 1) or g >= 2:
                            dve.wait_ge(s_h, i * 2 * N + 2 * (g - 2) + c + 1)
                        nc.vector.tensor_tensor((ps_d[k] if c == 0 else ps_b[k])[:], DU[:, h, c, :], ps_b[k][:],
                                                ALU.mult).then_inc(s_in, 1)
                    for c in range(2):
                        n = i * 2 * N + 2 * g + c
                        dve.wait_ge(s_in, n + 1)
                        dve.wait_ge(s_da, n + 1)
                        if past(i, 1) or g >= 2:
                            dve.wait_ge(s_hc, n - 3)
                        if h == 0 and g >= 2:
                            dve.wait_ge(s_hl, b * N + g - 1)
                        elif h == 1 and g < 2:
                            dve.wait_ge(s_hl, b * N + N - 1 + g)
                        nc.vector.tensor_tensor_scan(H[:, k, c, :], dA[:, k, c, :], (ps_d[k] if c == 0 else ps_b[k])[:],
                                                     last[:, c, g:g + 1] if h else 0.0, ALU.mult, ALU.add).then_inc(s_h, 1)
            chunk_of(0, 0)
            chunk_of(0, 1)
            with dve.Fori(1, BATCH) as b:
                for h in range(2):
                    chunk_of(b, h)

        @block.tensor
        def _(pe):
            pe.wait_ge(s_sel, 6)

            def spread(i, g):
                k = g % 2
                if past(i, 1) or g >= 2:
                    pe.wait_ge(s_h, i * 2 * N + 2 * (g - 1))
                nc.tensor.matmul(ps_b[k][:], sel[:, g, :], chunk(G, i), start=True, stop=True).then_inc(s_b, 1)
                if past(i, 1) or g >= 2:
                    pe.wait_ge(s_cs, i * N + g - 1)
                nc.tensor.matmul(ps_c[k][:], sel[:, N + g, :], chunk(G, i), start=True, stop=True).then_inc(s_c, 1)

            def add(i, g):
                if g == N // 2:
                    for c in range(2):
                        nc.tensor.matmul(ps_y[c][:], diag[:, c, :], chunk2(U, c, i), start=False, stop=False, skip_group_check=True)
                for c in range(2):
                    pe.wait_ge(s_hc, i * 2 * N + 2 * g + c + 1)
                    if g == 0 and past(i, 1):
                        pe.wait_ge(s_out, i * 2 - 1 + c)
                    nc.tensor.matmul(ps_y[c][:], ident[:], HC[:, g % RING, c, :], start=g == 0, stop=g == N - 1,
                                     skip_group_check=True).then_inc(s_y, 1)

            def chunk_of(i, last):
                for g in range(N):
                    if g + 2 < N:
                        spread(i, g + 2)
                    elif not last:
                        spread(i + 1, g + 2 - N)
                    if g > 0:
                        add(i, g - 1)
                    elif past(i, 1):
                        add(i - 1, N - 1)
            spread(0, 0)
            spread(0, 1)
            chunk_of(0, False)
            with pe.Fori(1, NCH - 1) as i:
                chunk_of(i, False)
            chunk_of(NCH - 1, True)
            add(NCH - 1, N - 1)


def mamba_back(nc, io, keep):
    XN, U, XT, X1 = keep["XN"], keep["U"], keep["XT"], keep["X1"]
    ones, ident, eps = keep["ones"], keep["ident"], keep["eps"]
    with ExitStack() as ctx:
        sb = lambda n, s, d=F32: ctx.enter_context(nc.sbuf_tensor("k_" + n, s, d))
        sem = lambda n: ctx.enter_context(nc.semaphore("k_" + n))
        banks = lambda n: [ctx.enter_context(nc.psum_tensor(f"k_{n}{k}", [P, CH], F32)) for k in range(2)]
        z_w = sb("z_w", [P, D_IN])
        out_w = sb("out_w", [P, 2, P])
        norm_w = sb("norm_w", [P, 1])
        centre = sb("centre", [P, P])
        SZ = sb("SZ", [P, 2, T])
        SQ = sb("SQ", [P, 2, CH])
        R = sb("R", [P, 2, CH])
        SQ2 = sb("SQ2", [P, 2, CH])
        R2 = sb("R2", [P, 2, CH])
        ps_o, ps_m, ps_c, ps_v = banks("ps_o"), banks("ps_m"), banks("ps_c"), banks("ps_v")
        ps_z = (ps_c, ps_v)
        s_w, s_z, s_sz, s_g, s_ce, s_o, s_t, s_sq, s_m = (sem(n) for n in (
            "weights", "z_psum", "silu_z", "gated", "centring", "out_psum", "out", "squares", "mean_square"))
        s_ln, s_r, s_n, s_x, s_c, s_q2, s_v, s_l2, s_r2, s_f = (sem(n) for n in (
            "ln", "inv_rms", "rms_normed", "x_added", "centred", "squares2", "variance", "ln2", "inv_std", "x1"))

        ctx.enter_context(nc.allow_non_contiguous_dma(reason="small per-feature vectors"))
        block = ctx.enter_context(nc.Block())

        def pipeline(*stages):
            for step in range(NCH + 3):
                for lag, stage in stages:
                    if 0 <= step - lag < NCH:
                        stage(step - lag, (step - lag) % 2)

        @block.sync
        def _(sp):
            sp.dma_start(z_w[:], io["in_wT"][:, D_IN:2 * D_IN]).then_inc(s_w, 16)
            sp.dma_start(out_w[:], io["out_wT"].rearrange("(c p) n -> p c n", p=P)).then_inc(s_w, 16)
            sp.dma_start(norm_w[:], io["norm_f_w"].rearrange("(p a) -> p a", a=1)).then_inc(s_w, 16)

        @block.gpsimd
        def _(pool):
            for used in keep["used"]:
                pool.sem_clear(used)

        @block.scalar
        def _(act):
            nc.scalar.preload_act_table(ACT.Silu)

            def silu(i, k):
                for c in range(2):
                    act.wait_ge(s_z, i * 2 + c + 1)
                    nc.scalar.activation(chunk2(SZ, c, i), ps_z[k][c][:], ACT.Silu).then_inc(s_sz, 1)
            twos(act, NCH, silu)
            nc.scalar.preload_act_table_set(LN_EXP)

            def squares(i, k):
                act.wait_ge(s_t, i + 1)
                if i >= 2:
                    act.wait_ge(s_m, i - 1)
                nc.scalar.activation(SQ[:, k, :], chunk(X1, i), ACT.Square).then_inc(s_sq, 1)

            def inv_rms(i, k):
                act.wait_ge(s_m, i + 1)
                if i >= 2:
                    act.wait_ge(s_n, i - 1)
                nc.scalar.activation(R[:, k, :], ps_m[k][:], ACT.Ln, bias=eps[:, 0:1]).then_inc(s_ln, 1)
                act.wait_ge(s_ln, i + 1)
                nc.scalar.activation(R[:, k, :], R[:, k, :], ACT.Exp, scale=-0.5).then_inc(s_r, 1)

            def squares2(i, k):
                act.wait_ge(s_c, i + 1)
                if i >= 2:
                    act.wait_ge(s_v, i - 1)
                nc.scalar.activation(SQ2[:, k, :], ps_c[k][:], ACT.Square).then_inc(s_q2, 1)

            def inv_std(i, k):
                act.wait_ge(s_v, i + 1)
                if i >= 2:
                    act.wait_ge(s_f, i - 1)
                nc.scalar.activation(R2[:, k, :], ps_v[k][:], ACT.Ln, bias=eps[:, 0:1]).then_inc(s_l2, 1)
                act.wait_ge(s_l2, i + 1)
                nc.scalar.activation(R2[:, k, :], R2[:, k, :], ACT.Exp, scale=-0.5).then_inc(s_r2, 1)
            pipeline((0, squares), (1, inv_rms), (2, squares2), (3, inv_std))

        @block.vector
        def _(dve):
            nc.vector.tensor_tensor(centre[:], ident[:], ones[:], ALU.subtract).then_inc(s_ce, 1)
            with dve.Fori(0, NCH) as i:
                for c in range(2):
                    dve.wait_ge(s_sz, i * 2 + c + 1)
                    nc.vector.tensor_tensor(chunk2(U, c, i), chunk2(U, c, i), chunk2(SZ, c, i), ALU.mult).then_inc(s_g, 1)
            dve.wait_ge(s_w, 48)

            def residual(i, k):
                dve.wait_ge(s_o, i + 1)
                nc.vector.tensor_tensor(chunk(X1, i), ps_o[k][:], chunk(XT, i), ALU.add).then_inc(s_t, 1)

            def rms_norm(i, k):
                dve.wait_ge(s_r, i + 1)
                dve.wait_ge(s_sq, i + 1)
                nc.vector.scalar_tensor_tensor(out=chunk(X1, i), in0=chunk(X1, i), scalar=norm_w[:, 0:1],
                                               in1=R[:, k, :], op0=ALU.mult, op1=ALU.mult).then_inc(s_n, 1)
                dve.wait_ge(s_n, i + 1)
                nc.vector.tensor_tensor(chunk(X1, i), chunk(X1, i), chunk(XT, i), ALU.add).then_inc(s_x, 1)

            def layer_norm(i, k):
                dve.wait_ge(s_r2, i + 1)
                nc.vector.tensor_tensor(chunk(X1, i), ps_c[k][:], R2[:, k, :], ALU.mult).then_inc(s_f, 1)
            pipeline((0, residual), (1, rms_norm), (3, layer_norm))

        @block.tensor
        def _(pe):
            pe.wait_ge(s_w, 48)

            def z_proj(i, k):
                for c in range(2):
                    if past(i):
                        pe.wait_ge(s_sz, i * 2 + c - 3)
                    nc.tensor.matmul(ps_z[k][c][:], z_w[:, c * P:(c + 1) * P], chunk(XN, i), start=True, stop=True).then_inc(s_z, 1)
            twos(pe, NCH, z_proj)
            pe.wait_ge(s_ce, 1)

            def out_proj(i, k):
                pe.wait_ge(s_g, i * 2 + 2)
                if i >= 2:
                    pe.wait_ge(s_t, i - 1)
                for c in range(2):
                    mm = nc.tensor.matmul(ps_o[k][:], out_w[:, c, :], chunk2(U, c, i), start=c == 0, stop=c == 1)
                mm.then_inc(s_o, 1)

            def mean_square(i, k):
                pe.wait_ge(s_sq, i + 1)
                if i >= 2:
                    pe.wait_ge(s_ln, i - 1)
                nc.tensor.matmul(ps_m[k][:], ones[:], SQ[:, k, :], start=True, stop=True).then_inc(s_m, 1)

            def centred(i, k):
                pe.wait_ge(s_x, i + 1)
                if i >= 2:
                    pe.wait_ge(s_f, i - 1)
                nc.tensor.matmul(ps_c[k][:], centre[:], chunk(X1, i), start=True, stop=True).then_inc(s_c, 1)

            def variance(i, k):
                pe.wait_ge(s_q2, i + 1)
                if i >= 2:
                    pe.wait_ge(s_l2, i - 1)
                nc.tensor.matmul(ps_v[k][:], ones[:], SQ2[:, k, :], start=True, stop=True).then_inc(s_v, 1)
            pipeline((0, out_proj), (1, mean_square), (2, centred), (3, variance))


def mamba(nc, io, keep):
    with ExitStack() as ctx:
        sb = lambda n, s, d=F32: ctx.enter_context(nc.sbuf_tensor("m_" + n, s, d))
        own = dict(keep, used=[], XT=sb("XT", [P, T]), XN=sb("XN", [P, T]), U=sb("U", [P, 2, T]))
        with ExitStack() as inner:
            sb = lambda n, s, d=F32: inner.enter_context(nc.sbuf_tensor("m_" + n, s, d))
            own.update(DT=sb("DT", [P, 2, T]), G=sb("G", [P, T], F32R), selw=sb("selw", [P, 2 * NST, P // 4]))
            mamba_front(nc, io, own)
            mamba_scan(nc, io, own)
        mamba_back(nc, io, own)


NT = T // P
PER = CH // P


E0 = 8
HID = 512
HM = HID // P
BIG = 1e30
DIFFERENCE = 15
COMB = DIFFERENCE + 6
HT2 = NT // 2
FIRST = 2 * HT2 + 1
AFFINE = FIRST + 1 + HT2 + 2
SECOND = AFFINE + FIRST
PER_HALF = SECOND + 1 + HT2


def wide(ap, n):
    return ap.unsqueeze(2).broadcast_to([ap.shape[0], ap.shape[1], n])


def row_wide(ap, n):
    return ap.unsqueeze(1).broadcast_to([ap.shape[0], n, ap.shape[1]])


def ffn(nc, io, keep):
    X1, X2, X2t, ident, eps = keep["X1"], keep["X2"], keep["X2t"], keep["ident"], keep["eps"]
    with ExitStack() as ctx:
        sb = lambda n, s, d=F32: ctx.enter_context(nc.sbuf_tensor("f_" + n, s, d))
        sem = lambda n: ctx.enter_context(nc.semaphore("f_" + n))
        bank = lambda n: ctx.enter_context(nc.psum_tensor("f_" + n, [P, CH], F32))
        ACC = X2t
        X1t = sb("X1t", [P, NT, P])
        stage = sb("stage", [P, 2, CH])
        gate_w = sb("gate_w", [P, E0])
        sh_w = sb("sh_w", [P, P])
        sh_b = sb("sh_b", [P, P])
        b2big = sb("b2big", [P, NT // 2, P])
        gamma = sb("gamma", [P, P])
        beta = sb("beta", [P, P])
        L = sb("L", [P, NT, E0])
        iota_i = sb("iota_i", [P, NT, E0], I32)
        iota = sb("iota", [P, NT, E0])
        oh = sb("oh", [P, 2, NT, E0])
        eq = sb("eq", [P, NT, E0])
        top = sb("top", [P, 2, NT])
        idx = sb("idx", [P, 2, NT])
        wt = sb("wt", [P, 3, NT])
        comb = sb("comb", [P, NT, E0])
        combE = sb("combE", [P, E0 * NT])
        combT = sb("combT", [P, 2, P])
        w1 = sb("w1", [P, 2, HID])
        w2 = sb("w2", [P, 2, HM, P])
        b1 = sb("b1", [P, 2, HM])
        HT = sb("HT", [P, 2, HM, CH])
        stats = sb("stats", [P, NT, 6])
        mv = sb("mv", [P, NT, 2])
        rstd = sb("rstd", [P, NT])
        ps_h = [bank(f"ps_h{m}") for m in range(HM)]
        ps_y = [bank(f"ps_y{k}") for k in range(2)]
        ps_t = [bank(f"ps_t{k}") for k in range(2)]
        s_w, s_b2, s_z, s_st, s_g, s_sh, s_tr = (sem(n) for n in ("weights", "b2_loaded", "zeroed", "staged", "logits", "shared", "transposed"))
        s_l, s_gelu, s_x1t, s_rt, s_exp, s_ct, s_ctc, s_b2m = (sem(n) for n in ("logits_copied", "shared_gelu", "x_token_major", "route", "gate_exp", "comb_t", "comb_t_copied", "b2_sum"))
        s_acc, s_shb, s_xb, s_own = sem("acc"), sem("shared_bias"), sem("x_and_beta"), sem("own_step")
        s_ew = [sem(f"expert_weights{k}") for k in range(2)]
        s_h, s_ht, s_y = sem("hidden"), sem("hidden_gelu"), sem("expert_out")
        s_ln, s_sq, s_fin, s_x2 = sem("norm"), sem("norm_sqrt"), sem("x2_token_major"), sem("x2_transposed")

        ctx.enter_context(nc.allow_non_contiguous_dma(reason="small per-feature vectors"))
        block = ctx.enter_context(nc.Block())

        @block.sync
        def _(sp):
            for dst, src in (
                (gate_w[:], io["gate_w"]), (sh_w[:], io["sh_w"]),
                (sh_b[:], io["sh_b"].rearrange("(a n) -> a n", a=1).broadcast_to([P, P])),
                (gamma[:], io["gamma"].rearrange("(a n) -> a n", a=1).broadcast_to([P, P])),
                (beta[:], io["beta"].rearrange("(a n) -> a n", a=1).broadcast_to([P, P])),
            ):
                sp.dma_start(dst, src).then_inc(s_w, 16)
            sp.wait_ge(s_z, 1)
            for t in range(NT // 2):
                sp.dma_start(b2big[t * E0:(t + 1) * E0, t, :], io["b2"]).then_inc(s_b2, 16)

            def weights(e, k):
                if past(e):
                    sp.wait_ge(s_y, (e - 1) * NCH)
                one_e = bass.ds(e, 1)
                sp.dma_start(w1[:, k, :], io["W1"][one_e].rearrange("a p n -> p (a n)")).then_inc(s_ew[k], 16)
                sp.dma_start(w2[:, k, :, :], io["W2"][one_e].rearrange("a (m p) n -> p (a m) n", p=P)).then_inc(s_ew[k], 16)
                sp.dma_start(b1[:, k, :], io["b1T"][one_e].rearrange("a p m -> p (a m)")).then_inc(s_ew[k], 16)
            twos(sp, E0, weights)

        @block.gpsimd
        def _(pool):
            nc.gpsimd.memset(b2big[:], 0.0).then_inc(s_z, 1)
            nc.gpsimd.iota(iota_i[:], pattern=[[0, NT], [1, E0]], base=0, channel_multiplier=0).then_inc(s_z, 1)

            def stage_in(i, k):
                if past(i):
                    pool.wait_ge(s_tr, i - 1)
                nc.gpsimd.tensor_copy(stage[:, k, :], chunk(X1, i)).then_inc(s_st, 1)
            twos(pool, NCH, stage_in)

        @block.scalar
        def _(act):
            nc.scalar.preload_act_table(ACT.Gelu)

            def shared(i, k):
                act.wait_ge(s_shb, i + 1)
                act.sem_inc(s_own, 1)
                part = ACC[:, bass.ds(i * PER, PER), :].rearrange("p t n -> p (t n)")
                nc.scalar.activation(part, part, ACT.Gelu).then_inc(s_gelu, 1)
                act.wait_ge(s_tr, i + 1)
                nc.scalar.activation(X1t[:, bass.ds(i * PER, PER), :].rearrange("p t n -> p (t n)"), ps_t[k][:], ACT.Copy).then_inc(s_x1t, 1)
            twos(act, NCH, shared)
            act.wait_ge(s_rt, DIFFERENCE)
            nc.scalar.activation(wt[:, 2, :], wt[:, 0, :], ACT.Exp).then_inc(s_exp, 1)

            def hidden(e, i, ke, k):
                g = e * NCH + i
                for m in range(HM):
                    act.wait_ge(s_h, g * HM + m + 1)
                    if past(e, 1) or past(i):
                        act.wait_ge(s_y, g - 1)
                    nc.scalar.activation(HT[:, k, m, :], ps_h[m][:], ACT.Gelu, bias=b1[:, ke, m:m + 1]).then_inc(s_ht, 1)
            nc.scalar.preload_act_table(ACT.Gelu)
            twos(act, NCH, lambda i, k: hidden(0, i, 0, k))
            with act.Fori(0, NCH // 2) as j:
                for k in range(2):
                    hidden(1, j * 2 + k, 1, k)
            with act.Fori(1, E0 // 2 - 1) as ep:
                for ke in range(2):
                    with act.Fori(0, NCH // 2) as j:
                        for k in range(2):
                            hidden(ep * 2 + ke, j * 2 + k, ke, k)
            with act.Fori(0, NCH // 2) as j:
                for k in range(2):
                    hidden(E0 - 2, j * 2 + k, 0, k)
            with act.Fori(0, NCH // 2 - 1) as j:
                for k in range(2):
                    hidden(E0 - 1, j * 2 + k, 1, k)

            def root(h, n):
                act.wait_ge(s_ln, h * PER_HALF + n)
                part = rstd[:, h * HT2:(h + 1) * HT2]
                nc.scalar.activation(part, part, ACT.Sqrt).then_inc(s_sq, 1)
            hidden(E0 - 1, NCH - 2, 1, 0)
            root(0, FIRST)
            hidden(E0 - 1, NCH - 1, 1, 1)
            root(0, SECOND)
            root(1, FIRST)
            root(1, SECOND)

            def x2_copy(i, k):
                act.wait_ge(s_x2, i + 1)
                nc.scalar.activation(chunk(X2, i), ps_t[k][:], ACT.Copy).then_inc(s_fin, 1)
            twos(act, NCH, x2_copy)

        @block.vector
        def _(dve):
            dve.wait_ge(s_w, 16 * 5)

            def logits(i, k):
                dve.wait_ge(s_g, i + 1)
                nc.vector.tensor_copy(L[:, bass.ds(i * PER, PER), :].rearrange("p t e -> p (t e)"), ps_h[k][:, 0:PER * E0]).then_inc(s_l, 1)
                dve.wait_ge(s_sh, i + 1)
                nc.vector.tensor_tensor(ACC[:, bass.ds(i * PER, PER), :], ps_y[k][:].rearrange("p (t n) -> p t n", n=P),
                                        row_wide(sh_b[:], PER), ALU.add).then_inc(s_shb, 1)
            twos(dve, NCH, logits)
            dve.wait_ge(s_z, 2)
            nc.vector.tensor_copy(iota[:], iota_i[:]).then_inc(s_rt, 1)
            dve.wait_ge(s_l, NCH)
            dve.wait_ge(s_rt, 1)
            n = 1
            for r in range(2):
                nc.vector.tensor_reduce(top[:, r, :], L[:], AX.X, ALU.max).then_inc(s_rt, 1)
                dve.wait_ge(s_rt, n + 1)
                nc.vector.tensor_tensor(eq[:], L[:], wide(top[:, r, :], E0), ALU.is_equal).then_inc(s_rt, 1)
                dve.wait_ge(s_rt, n + 2)
                nc.vector.scalar_tensor_tensor(out=eq[:], in0=eq[:], scalar=-float(E0), in1=iota[:], op0=ALU.mult, op1=ALU.add).then_inc(s_rt, 1)
                dve.wait_ge(s_rt, n + 3)
                nc.vector.tensor_reduce(idx[:, r, :], eq[:], AX.X, ALU.min).then_inc(s_rt, 1)
                dve.wait_ge(s_rt, n + 4)
                nc.vector.tensor_scalar(idx[:, r, :], idx[:, r, :], float(E0), None, ALU.add).then_inc(s_rt, 1)
                dve.wait_ge(s_rt, n + 5)
                nc.vector.tensor_tensor(oh[:, r], iota[:], wide(idx[:, r, :], E0), ALU.is_equal).then_inc(s_rt, 1)
                n += 6
                dve.wait_ge(s_rt, n)
                if r == 0:
                    nc.vector.scalar_tensor_tensor(out=L[:], in0=oh[:, 0], scalar=-BIG, in1=L[:], op0=ALU.mult, op1=ALU.add).then_inc(s_rt, 1)
                    n += 1
                    dve.wait_ge(s_rt, n)
            nc.vector.tensor_tensor(wt[:, 0, :], top[:, 1, :], top[:, 0, :], ALU.subtract).then_inc(s_rt, 1)
            dve.wait_ge(s_exp, 1)
            nc.vector.tensor_scalar(wt[:, 0, :], wt[:, 2, :], 1.0, None, ALU.add).then_inc(s_rt, 1)
            dve.wait_ge(s_rt, DIFFERENCE + 1)
            nc.vector.reciprocal(wt[:, 1, :], wt[:, 0, :]).then_inc(s_rt, 1)
            dve.wait_ge(s_rt, DIFFERENCE + 2)
            nc.vector.tensor_tensor(wt[:, 2, :], wt[:, 2, :], wt[:, 1, :], ALU.mult).then_inc(s_rt, 1)
            dve.wait_ge(s_rt, DIFFERENCE + 3)
            for r in range(2):
                nc.vector.tensor_tensor(oh[:, r], oh[:, r], wide(wt[:, 1 + r, :], E0), ALU.mult).then_inc(s_rt, 1)
            dve.wait_ge(s_rt, DIFFERENCE + 5)
            nc.vector.tensor_tensor(comb[:], oh[:, 0], oh[:, 1], ALU.add).then_inc(s_rt, 1)
            dve.wait_ge(s_rt, COMB)
            nc.vector.tensor_copy(combE[:].rearrange("p (e t) -> p e t", e=E0), comb[:].rearrange("p t e -> p e t")).then_inc(s_rt, 1)
            for h in range(2):
                dve.wait_ge(s_ct, h + 1)
                nc.vector.tensor_copy(combT[:, h, :], ps_t[h][:, 0:P]).then_inc(s_ctc, 1)
            dve.wait_ge(s_gelu, NCH)

            def start_acc(i, k):
                dve.wait_ge(s_b2m, i + 1)
                part = ACC[:, bass.ds(i * PER, PER), :].rearrange("p t n -> p (t n)")
                nc.vector.scalar_tensor_tensor(out=part, in0=part, scalar=0.5, in1=ps_y[k][:], op0=ALU.mult, op1=ALU.add).then_inc(s_acc, PER)
            twos(dve, NCH, start_acc)
            dve.wait_ge(s_rt, COMB + 1)
            dve.wait_ge(s_x1t, NCH)
            nc.vector.tensor_tensor(X1t[:], X1t[:], row_wide(beta[:], NT), ALU.add).then_inc(s_xb, 1)

            def add_expert(e, i, k):
                g = e * NCH + i
                dve.wait_ge(s_y, g + 1)
                for t in range(PER):
                    dve.wait_ge(s_acc, g * PER + t + 1)
                    tile = ACC[:, bass.ds(i * PER + t, 1), :].rearrange("p a n -> p (a n)")
                    nc.vector.scalar_tensor_tensor(out=tile, in0=ps_y[k][:, t * P:(t + 1) * P],
                                                   scalar=combE[:, bass.ds(e * NT + i * PER + t, 1)], in1=tile,
                                                   op0=ALU.mult, op1=ALU.add).then_inc(s_acc, 1)
            with dve.Fori(0, E0 - 1) as e:
                with dve.Fori(0, NCH // 2) as j:
                    for k in range(2):
                        add_expert(e, j * 2 + k, k)
            with dve.Fori(0, NCH // 4) as j:
                for k in range(2):
                    add_expert(E0 - 1, j * 2 + k, k)
            dve.wait_ge(s_xb, 1)

            def statistics(h, n):
                dve.wait_ge(s_acc, NT * E0 + NT // 2 * (h + 1))
                for t in range(h * HT2, (h + 1) * HT2):
                    nc.vector.bn_stats(stats[:, t, :], ACC[:, t, :]).then_inc(s_ln, 1)
                for t in range(HT2):
                    dve.wait_ge(s_ln, n + t + 1)
                    nc.vector.bn_aggr(mv[:, h * HT2 + t, :], stats[:, h * HT2 + t, :]).then_inc(s_ln, 1)
                part = slice(h * HT2, (h + 1) * HT2)
                dve.wait_ge(s_ln, n + 2 * HT2)
                nc.vector.tensor_scalar(rstd[:, part], mv[:, part, 1], EPS, None, ALU.add).then_inc(s_ln, 1)

            def normalise(h, n):
                part = slice(h * HT2, (h + 1) * HT2)
                dve.wait_ge(s_sq, 2 * h + (1 if n == FIRST + h * PER_HALF else 2))
                nc.vector.reciprocal(rstd[:, part], rstd[:, part]).then_inc(s_ln, 1)
                dve.wait_ge(s_ln, n + 1)
                for t in range(h * HT2, (h + 1) * HT2):
                    nc.vector.tensor_scalar(ACC[:, t, :], ACC[:, t, :], mv[:, t, 0:1], rstd[:, t:t + 1],
                                            ALU.subtract, ALU.mult).then_inc(s_ln, 1)

            def affine(h, n):
                rows = ACC[:, h * HT2:(h + 1) * HT2, :]
                for s, (other, op) in enumerate(((row_wide(gamma[:], HT2), ALU.mult), (X1t[:, h * HT2:(h + 1) * HT2, :], ALU.add))):
                    dve.wait_ge(s_ln, n + s)
                    nc.vector.tensor_tensor(rows, rows, other, op).then_inc(s_ln, 1)
                dve.wait_ge(s_ln, n + 2)

            add_expert(E0 - 1, NCH // 2, 0)
            statistics(0, 0)
            add_expert(E0 - 1, NCH // 2 + 1, 1)
            normalise(0, FIRST)
            affine(0, FIRST + 1 + HT2)
            add_expert(E0 - 1, NCH // 2 + 2, 0)
            statistics(0, AFFINE)
            add_expert(E0 - 1, NCH // 2 + 3, 1)
            normalise(0, SECOND)
            statistics(1, PER_HALF)
            normalise(1, PER_HALF + FIRST)
            affine(1, PER_HALF + FIRST + 1 + HT2)
            statistics(1, PER_HALF + AFFINE)
            normalise(1, PER_HALF + SECOND)

        @block.tensor
        def _(pe):
            pe.wait_ge(s_w, 16 * 5)

            def token_major(i, k):
                pe.wait_ge(s_st, i + 1)
                tiles = [stage[:, k, t * P:(t + 1) * P] for t in range(PER)]
                if past(i):
                    pe.wait_ge(s_l, i - 1)
                for t in range(PER):
                    mm = nc.tensor.matmul(ps_h[k][:, t * E0:(t + 1) * E0], tiles[t], gate_w[:], start=True, stop=True)
                mm.then_inc(s_g, 1)
                if past(i):
                    pe.wait_ge(s_shb, i - 1)
                for t in range(PER):
                    mm = nc.tensor.matmul(ps_y[k][:, t * P:(t + 1) * P], tiles[t], sh_w[:], start=True, stop=True)
                mm.then_inc(s_sh, 1)
                if past(i):
                    pe.wait_ge(s_x1t, i - 1)
                for t in range(PER):
                    mm = nc.tensor.transpose(ps_t[k][:, t * P:(t + 1) * P], tiles[t], ident[:])
                mm.then_inc(s_tr, 1)
            twos(pe, NCH, token_major)
            def up(e, i, ke):
                g = e * NCH + i
                for m in range(HM):
                    if past(e, 1) or past(i, 1):
                        pe.wait_ge(s_ht, g * HM + m - HM + 1)
                    nc.tensor.matmul(ps_h[m][:], w1[:, ke, m * P:(m + 1) * P], chunk(X1, i), start=True, stop=True).then_inc(s_h, 1)
            pe.wait_ge(s_l, NCH)
            pe.wait_ge(s_ew[0], 48)
            up(0, 0, 0)
            pe.wait_ge(s_rt, COMB)
            pe.wait_ge(s_x1t, NCH)
            for h in range(2):
                nc.tensor.transpose(ps_t[h][:, 0:P], comb[:, h * 16:(h + 1) * 16, :].rearrange("p t e -> p (t e)"), ident[:]).then_inc(s_ct, 1)
            pe.wait_ge(s_b2, 16 * NT // 2)
            pe.wait_ge(s_ctc, 2)
            pe.wait_ge(s_gelu, NCH)

            for i in range(NCH):
                if i >= 2:
                    pe.wait_ge(s_acc, PER * (i - 1))
                cols = b2big[:, (i % 4) * PER:(i % 4 + 1) * PER, :].rearrange("p t n -> p (t n)")
                nc.tensor.matmul(ps_y[i % 2][:], combT[:, i // 4, :], cols, start=True, stop=True).then_inc(s_b2m, 1)

            def down(e, i, ke, k):
                g = e * NCH + i
                pe.wait_ge(s_ht, g * HM + HM)
                pe.wait_ge(s_acc, g * PER + NT - PER)
                for t in range(PER):
                    for m in range(HM):
                        mm = nc.tensor.matmul(ps_y[k][:, t * P:(t + 1) * P], HT[:, k, m, t * P:(t + 1) * P], w2[:, ke, m, :],
                                              start=m == 0, stop=m == HM - 1)
                mm.then_inc(s_y, 1)

            def expert(e, ke, first, last):
                if first:
                    up(e, 1, ke)
                    down(e, 0, ke, 0)
                    up(e, 2, ke)
                    down(e, 1, ke, 1)
                with pe.Fori(1 if first else 0, NCH // 2 - 1) as j:
                    for k in range(2):
                        up(e, j * 2 + k + 1, ke)
                        down(e, j * 2 + k, ke, k)
                up(e, NCH - 1, ke)
                down(e, NCH - 2, ke, 0)
                if not last:
                    pe.wait_ge(s_ew[1 - ke], (e + 1 - (1 - ke)) * 24 + 48)
                    up(e + 1, 0, 1 - ke)
                down(e, NCH - 1, ke, 1)
            expert(0, 0, True, False)
            expert(1, 1, False, False)
            with pe.Fori(1, E0 // 2 - 1) as ep:
                for ke in range(2):
                    expert(ep * 2 + ke, ke, False, False)
            expert(E0 - 2, 0, False, False)
            expert(E0 - 1, 1, False, True)

            for i in range(NCH):
                pe.wait_ge(s_ln, i // (NCH // 2) * PER_HALF + SECOND + 1 + (i % (NCH // 2) + 1) * PER)
                if i >= 2:
                    pe.wait_ge(s_fin, i - 1)
                for t in range(PER):
                    mm = nc.tensor.transpose(ps_t[i % 2][:, t * P:(t + 1) * P], ACC[:, i * PER + t, :], ident[:])
                mm.then_inc(s_x2, 1)


NH = 16
DK = 8
PARTS = 3
GH = 4
NG = NH // GH
QT = SEQ // P
ROWS = PARTS * PARTS * DK
MROW = ROWS
VW = 32
NEG = -1e30
BLOCKS = [(c, kt, max(kt - c * PER, 0)) for c in range(2) for kt in range((c + 1) * PER)]
PIECES = dict(a=lambda j: [(j, qt, 0) for qt in range(PER)], b=lambda j: [(j, qt, 0) for qt in range(PER, QT)],
              c=lambda j: [(j, qt, 1) for qt in range(PER, QT)])
ITEMS = [piece for kind, j in ("a0", "a1", "b0", "b1", "a2", "a3", "c0", "c1", "c2", "c3", "b2", "b3") for piece in PIECES[kind](int(j))]
NB, NI = len(BLOCKS), len(ITEMS)
LOADS = 16 * (2 * PARTS + 1)
RP = 3


E1 = 64
TOPK = 4
CAP = P
SLOTS = E1 * CAP


def load_heads(sp, dram, keep, b, g, zeros):
    Q, K, s_ld = keep["Q"][g], keep["K"][g], keep["s_ld"][g]
    heads = lambda x: dram["qk"][x, :, bass.ds(b, 1), :, g * GH:(g + 1) * GH, :].rearrange("c b d j t -> c (b d) (j t)")
    for a in range(PARTS):
        rows = slice(a * PARTS * DK, (a + 1) * PARTS * DK)
        for buf, src in ((Q, heads(0)[a:a + 1].broadcast_to([PARTS, DK, GH * SEQ])), (K, heads(1))):
            sp.dma_start(buf[rows].rearrange("r j t -> r (j t)"), src).then_inc(s_ld, 16)
    sp.dma_start(Q[MROW:MROW + PARTS].rearrange("r j t -> r (j t)"), zeros).then_inc(s_ld, 16)


def attn_project(nc, io, keep, dram):
    X2, Vt, Q, K = keep["X2"], keep["Vt"], keep["Q"], keep["K"]
    with ExitStack() as ctx:
        sb = lambda n, s, d=F32: ctx.enter_context(nc.sbuf_tensor("p_" + n, s, d))
        sem = lambda n: ctx.enter_context(nc.semaphore("p_" + n))
        bank = lambda n: ctx.enter_context(nc.psum_tensor("p_" + n, [P, CH], F32))
        w = [sb(f"w{j}", [P, P]) for j in range(3)]
        bias = sb("bias", [P, 2])
        v_b = sb("v_b", [P, P])
        stage = sb("stage", [P, 2, CH])
        zero = sb("zero", [P, 2 * CH], BF16)
        parts = sb("parts", [P, 2, 2, PARTS, CH], BF16)
        rest = sb("rest", [P, 2, 2, CH])
        ps = [[bank(f"ps{k}{x}") for x in range(2)] for k in range(2)]
        ps_v = [bank(f"ps_v{k}") for k in range(2)]
        s_w, s_z, s_zd, s_ps, s_p0, s_r, s_p1, s_p2 = (sem(n) for n in ("weights", "zeroed", "zeros_stored", "qk_psum", "part0", "rest", "part1", "part2"))
        s_st, s_v, s_vt, s_q = sem("staged"), sem("v_psum"), sem("v"), sem("head_buffers")
        s_d = [sem(f"stored{k}") for k in range(2)]

        ctx.enter_context(nc.allow_non_contiguous_dma(reason="small per-feature vectors"))
        block = ctx.enter_context(nc.Block())

        @block.sync
        def _(sp):
            for dst, src in (
                [(w[j][:], io[n]) for j, n in enumerate(("Wq", "Wk", "Wv"))]
                + [(bias[:, j:j + 1], io[n].rearrange("h (k a) -> (h k) a", a=1)) for j, n in enumerate(("bq", "bk"))]
                + [(v_b[:], io["bv"].rearrange("(a h) k -> a (h k)", a=1).broadcast_to([P, P]))]
            ):
                sp.dma_start(dst, src).then_inc(s_w, 16)
            sp.wait_ge(s_z, 1)
            sp.dma_start(dram["zeros"].rearrange("r (a n) -> (r a) n", a=GH), zero[0:PARTS * GH, :]).then_inc(s_zd, 16)

            def store(i, k):
                for x in range(2):
                    sp.wait_ge(s_p2, i * 2 + x + 1)
                    for a in range(PARTS):
                        rows = dram["qk"][x, a, i // 2, :, :, k * CH:(k + 1) * CH].rearrange("d h t -> h d t")
                        sp.dma_start(rows, parts[:, k, x, a, :]).then_inc(s_d[k], 16)
            store(0, 0)
            store(1, 1)
            sp.wait_ge(s_zd, 16)
            for k in range(2):
                sp.wait_ge(s_d[k], 16 * 2 * PARTS)
            sp.wait_ge(s_q, 2)
            load_heads(sp, dram, keep, 0, 0, dram["zeros"])
            for i in range(2, NCH):
                store(i, i % 2)
            for k in range(2):
                sp.wait_ge(s_d[k], 16 * 2 * PARTS * NCH // 2)

        @block.gpsimd
        def _(pool):
            nc.gpsimd.memset(zero[:], 0.0).then_inc(s_z, 1)
            for i in range(NCH):
                if i >= 2:
                    pool.wait_ge(s_v, i - 1)
                nc.gpsimd.tensor_copy(stage[:, i % 2, :], chunk(X2, i)).then_inc(s_st, 1)
                if i % 2 == 0:
                    nc.gpsimd.memset(Q[i // 2][:].rearrange("p j t -> p (j t)").bitcast(F32), 0.0).then_inc(s_q, 1)
                else:
                    nc.gpsimd.memset(K[i // 2][:].rearrange("p j t -> p (j t)"), 1.0).then_inc(s_q, 1)

        @block.scalar
        def _(act):
            act.wait_ge(s_w, 16 * 6)

            def split(i, k):
                if past(i):
                    act.wait_ge(s_d[k], (i - k) * 16 * PARTS)
                for x in range(2):
                    act.wait_ge(s_ps, i * 2 + x + 1)
                    nc.scalar.activation(parts[:, k, x, 0, :], ps[k][x][:], ACT.Identity, bias=bias[:, x:x + 1]).then_inc(s_p0, 1)
                for x in range(2):
                    act.wait_ge(s_r, i * 2 + x + 1)
                    nc.scalar.activation(parts[:, k, x, 1, :], rest[:, k, x, :], ACT.Copy).then_inc(s_p1, 1)
            twos(act, NCH, split)

        @block.vector
        def _(dve):
            dve.wait_ge(s_w, 16 * 6)

            def third(i, k):
                for x in range(2):
                    dve.wait_ge(s_p1, i * 2 + x + 1)
                    nc.vector.tensor_tensor(parts[:, k, x, 2, :], rest[:, k, x, :], parts[:, k, x, 1, :], ALU.subtract).then_inc(s_p2, 1)

            def split(i, k):
                for x in range(2):
                    dve.wait_ge(s_p0, i * 2 + x + 1)
                    nc.vector.scalar_tensor_tensor(out=rest[:, k, x, :], in0=ps[k][x][:], scalar=bias[:, x:x + 1], in1=parts[:, k, x, 0, :],
                                                   op0=ALU.add, op1=ALU.subtract).then_inc(s_r, 1)
                dve.wait_ge(s_v, i + 1)
                nc.vector.tensor_tensor(Vt[:, bass.ds(i * PER, PER), :], ps_v[k][:].rearrange("p (t n) -> p t n", n=P),
                                        row_wide(v_b[:], PER), ALU.add).then_inc(s_vt, 1)
                third(i, k)
            twos(dve, NCH, split)

        @block.tensor
        def _(pe):
            pe.wait_ge(s_w, 16 * 6)

            def project(i, k):
                for x in range(2):
                    if past(i):
                        pe.wait_ge(s_r, i * 2 + x - 3)
                    nc.tensor.matmul(ps[k][x][:], w[x][:], chunk(X2, i), start=True, stop=True).then_inc(s_ps, 1)
                pe.wait_ge(s_st, i + 1)
                if past(i):
                    pe.wait_ge(s_vt, i - 1)
                for t in range(PER):
                    mm = nc.tensor.matmul(ps_v[k][:, t * P:(t + 1) * P], stage[:, k, t * P:(t + 1) * P], w[2][:], start=True, stop=True)
                mm.then_inc(s_v, 1)
            twos(pe, NCH, project)


def attn_scores(nc, io, keep, dram):
    Vt, CX, ident, Q, K, s_ld = keep["Vt"], keep["CX"], keep["ident"], keep["Q"], keep["K"], keep["s_ld"]
    with ExitStack() as ctx:
        sb = lambda n, s, d=F32: ctx.enter_context(nc.sbuf_tensor("t_" + n, s, d))
        sem = lambda n: ctx.enter_context(nc.semaphore("t_" + n))
        bank = lambda n, m=1: ctx.enter_context(nc.psum_tensor("t_" + n, [P, m * CH], F32))
        VG = sb("VG", [P, 2, QT, GH * VW])
        PT = sb("PT", [P, RP, GH, CH])
        CT = sb("CT", [P, 2, CH])
        den = sb("den", [P, 2, PER, GH])
        negm = sb("negm", [P, 2, GH, QT])
        negm2 = sb("negm2", [P, 2, GH, PER])
        msb = sb("msb", [GH * QT, P])
        mrest = sb("mrest", [GH * QT, P])
        mp = sb("mp", [GH * QT, 2, PARTS, P], BF16)
        maskf = sb("maskf", [P, P])
        mask = sb("mask", [P, P], BF16)
        identb = sb("identb", [P, P], BF16)
        ps_1 = [bank(f"ps_1{k}") for k in range(2)]
        ps_s = [bank(f"ps_s{p}", 2) for p in range(2)]
        ps_c = [bank(f"ps_c{c}") for c in range(2)]
        s_m, s_mb = sem("mask_f32"), sem("mask")
        s_ms = [sem(f"max_stored{g}") for g in range(NG)]
        s_ml = [sem(f"max_loaded{g}") for g in range(NG)]
        s_p1, s_mx, s_cmb, s_mt, s_mc, s_mp = (sem(n) for n in ("scores1", "maxed", "max_joined", "max_transposed", "max_copied", "max_parts"))
        s_st, s_exp, s_mk, s_pv, s_vg = (sem(n) for n in ("scores2", "exped", "masked", "context", "v_group"))
        s_ev, s_ct, s_cx = sem("context_copied"), sem("context_transposed"), sem("normed")
        s_pool, s_sp = sem("pool_step"), sem("sync_step")
        s_dr, s_mq = sem("reciprocal"), sem("max_chain")
        AHEAD = 2
        assert NB % RP == 0

        ctx.enter_context(nc.allow_non_contiguous_dma(reason="rows of heads"))
        block = ctx.enter_context(nc.Block())

        def batches(eng, body, first=0):
            if first:
                body(0, False)
            with eng.Fori(first, BATCH - 1) as b:
                body(b, False)
            body(BATCH - 1, True)

        def before(b, g):
            return (b, g - 1) if g else (b - 1, NG - 1) if past(b, 1) else None

        @block.sync
        def _(sp):
            def maxima(b, g):
                gi = b * NG + g
                sp.wait_ge(s_mp, gi + 2)
                for a in range(PARTS):
                    sp.dma_start(dram["max"][g, a].rearrange("(r n) -> r n", n=P), mp[:, g % 2, a, :]).then_inc(s_ms[g], 16)
                sp.wait_ge(s_ms[g], b * 16 * PARTS + 16 * PARTS)
                sp.wait_ge(s_p1, gi * NI + NI)
                sp.dma_start(Q[g][MROW:MROW + PARTS].rearrange("r j t -> r (j t)"), dram["max"][g]).then_inc(s_ml[g], 16)

            for g in range(1, NG):
                load_heads(sp, dram, keep, 0, g, dram["zeros"])
            maxima(0, 0)

            def body(b, last):
                for g in range(NG):
                    gi = b * NG + g
                    if not (last and g == NG - 1):
                        maxima(b + (g + 1) // NG, (g + 1) % NG)
                    if not last:
                        sp.wait_ge(s_st, gi * 2 * NB + 2 * NB)
                        sp.sem_inc(s_sp, 1)
                        sp.wait_ge(s_ml[g], b * 16 + 16)
                        load_heads(sp, dram, keep, b + 1, g, dram["zeros"])
            batches(sp, body)

        @block.gpsimd
        def _(pool):
            nc.gpsimd.memset(VG[:].rearrange("p k t n -> p (k t n)"), 0.0).then_inc(s_m, 1)
            nc.gpsimd.memset(maskf[:], 0.0).then_inc(s_m, 1)
            pool.wait_ge(s_m, 2)
            nc.gpsimd.affine_select(out=maskf[:], in_=maskf[:], compare_op=ALU.is_ge, fill=NEG, base=0,
                                    pattern=[[-1, P]], channel_multiplier=1).then_inc(s_m, 1)
            nc.gpsimd.memset(VG[:].rearrange("p k t (j n) -> p (k t j) n", n=VW)[:, :, DK:DK + 1], 1.0).then_inc(s_m, 1)
            pool.wait_ge(s_m, 4)

            def v_group(b, g):
                gi = b * NG + g
                if past(gi, 1):
                    pool.wait_ge(s_pv, gi * NB - NB + RP)
                out = VG[:, g % 2].rearrange("p t (j n) -> p t j n", n=VW)[:, :, :, 0:DK]
                src = Vt[:, bass.ds(b * QT, QT), g * GH * DK:(g + 1) * GH * DK].rearrange("p t (j k) -> p t j k", k=DK)
                for t in range(QT):
                    ins = nc.gpsimd.tensor_copy(out[:, t], src[:, t])
                ins.then_inc(s_vg, 1)
            v_group(0, 0)

            def body(b, last):
                for g in range(NG):
                    gi = b * NG + g
                    d = 0
                    for n, (c, kt, r) in enumerate(BLOCKS):
                        if n == 2 and not (last and g == NG - 1):
                            v_group(b + (g + 1) // NG, (g + 1) % NG)
                        if kt < c * PER:
                            continue
                        pool.wait_ge(s_exp, gi * 2 * NB + 2 * n + 2 + AHEAD)
                        pool.sem_inc(s_pool, 1)
                        part = PT[:, n % RP, :, 0:P]
                        nc.gpsimd.affine_select(out=part, in_=part, compare_op=ALU.is_ge, fill=0.0, base=0,
                                                pattern=[[0, GH], [1, P]], channel_multiplier=-1).then_inc(s_mk, 1)
            batches(pool, body)

        @block.scalar
        def _(act):
            act.sem_inc(s_exp, AHEAD)

            def context(b, g, c):
                gi = b * NG + g
                act.wait_ge(s_pv, gi * NB + (NB if c else PER) + RP)
                act.wait_ge(s_ct, gi * 2 + c - 1 + AHEAD)
                nc.scalar.activation(CT[:, c, :], ps_c[c][:], ACT.Copy).then_inc(s_ev, 1)

            def body(b, last):
                for g in range(NG):
                    gi = b * NG + g
                    for n, (c, kt, r) in enumerate(BLOCKS):
                        w = CH - r * P
                        for p in range(2):
                            act.wait_ge(s_st, gi * 2 * NB + 2 * n + p + 1)
                            act.wait_ge(s_pv, gi * NB + n + 1)
                            src = ps_s[p][:].rearrange("p (j t) -> p j t", j=2)[:, :, 0:w]
                            nc.scalar.activation(PT[:, n % RP, 2 * p:2 * p + 2, 0:w], src, ACT.Exp, scale=DK ** -0.5).then_inc(s_exp, 1)
                        if n == 1 and before(b, g):
                            context(*before(b, g), 1)
                        if n == PER + 1:
                            context(b, g, 0)
            batches(act, body, 1)
            context(BATCH - 1, NG - 1, 1)

        @block.vector
        def _(dve):
            dve.sem_inc(s_mx, AHEAD)
            dve.sem_inc(s_cx, AHEAD)
            dve.sem_inc(s_mp, 1)
            dve.wait_ge(s_m, 3)
            nc.vector.tensor_copy(mask[:], maskf[:]).then_inc(s_mb, 1)
            nc.vector.tensor_copy(identb[:], ident[:]).then_inc(s_mb, 1)

            def first_pass(b, g, n):
                gi = b * NG + g
                j, qt, c = ITEMS[n]
                width = min((qt + 1) * P - c * CH, CH)
                dve.wait_ge(s_p1, gi * NI + n + 1)
                out = (negm2[:, g % 2, j, qt - PER:qt - PER + 1] if c else negm[:, g % 2, j, qt:qt + 1])
                nc.vector.tensor_reduce(out, ps_1[n % 2][:, 0:width], AX.X, ALU.max, negate=True).then_inc(s_mx, 1)

            def join(b, g):
                gi = b * NG + g
                dve.wait_ge(s_mx, gi * NI + NI + AHEAD)
                nc.vector.tensor_tensor(negm[:, g % 2, :, PER:QT], negm[:, g % 2, :, PER:QT], negm2[:, g % 2], ALU.min).then_inc(s_cmb, 1)

            def parts(b, g):
                gi = b * NG + g
                dve.wait_ge(s_mt, gi + 1)
                dve.wait_ge(s_mp, gi + 1)
                nc.vector.tensor_copy(msb[:], ps_1[0][0:GH * QT, 0:P]).then_inc(s_mc, 1)
                dve.wait_ge(s_mc, gi + 1)
                nc.vector.tensor_copy(mp[:, g % 2, 0, :], msb[:]).then_inc(s_mq, 1)
                dve.wait_ge(s_mq, gi * 3 + 1)
                nc.vector.tensor_tensor(mrest[:], msb[:], mp[:, g % 2, 0, :], ALU.subtract).then_inc(s_mq, 1)
                dve.wait_ge(s_mq, gi * 3 + 2)
                nc.vector.tensor_copy(mp[:, g % 2, 1, :], mrest[:]).then_inc(s_mq, 1)
                dve.wait_ge(s_mq, gi * 3 + 3)
                nc.vector.tensor_tensor(mp[:, g % 2, 2, :], mrest[:], mp[:, g % 2, 1, :], ALU.subtract).then_inc(s_mp, 1)

            def divide(b, g, c):
                gi = b * NG + g
                dve.wait_ge(s_ct, gi * 2 + c + 1 + AHEAD)
                src = ps_c[c][:].rearrange("p (t j n) -> p t j n", t=PER, n=VW)
                nc.vector.reciprocal(den[:, c], src[:, :, :, DK]).then_inc(s_dr, 1)
                dve.wait_ge(s_dr, gi * 2 + c + 1)
                out = CX[:, bass.ds(b * QT + c * PER, PER), g * GH * DK:(g + 1) * GH * DK].rearrange("p t (j k) -> p t j k", k=DK)
                for t in range(PER):
                    ins = nc.vector.tensor_tensor(out[:, t], src[:, t, :, 0:DK], den[:, c, t].unsqueeze(2).broadcast_to([P, GH, DK]), ALU.mult)
                ins.then_inc(s_cx, 1)

            for n in range(NI):
                first_pass(0, 0, n)
            join(0, 0)
            parts(0, 0)
            for n in range(NI):
                first_pass(0, 1, n)
            join(0, 1)

            def body(b, last):
                for g in range(NG):
                    if not (last and g == NG - 1):
                        parts(b + (g + 1) // NG, (g + 1) % NG)
                    ahead = not (last and g >= NG - 2)
                    b2, g2 = b + (g + 2) // NG, (g + 2) % NG
                    if ahead:
                        for n in range(4 * PER):
                            first_pass(b2, g2, n)
                    if before(b, g):
                        divide(*before(b, g), 1)
                    if ahead:
                        for n in range(4 * PER, 9 * PER):
                            first_pass(b2, g2, n)
                    divide(b, g, 0)
                    if ahead:
                        for n in range(9 * PER, NI):
                            first_pass(b2, g2, n)
                        join(b2, g2)
            batches(dve, body, 1)
            divide(BATCH - 1, NG - 1, 1)

        @block.tensor
        def _(pe):
            pe.sem_inc(s_pv, RP)
            pe.sem_inc(s_ct, AHEAD)
            pe.wait_ge(s_mb, 2)

            def item(b, g, n):
                gi = b * NG + g
                j, qt, c = ITEMS[n]
                width = min((qt + 1) * P - c * CH, CH)
                diagonal = qt // PER == c
                if n == 0:
                    pe.wait_ge(s_ld[g], (b + 1) * LOADS)
                    if past(gi, 1):
                        pe.wait_ge(s_mc, gi)
                pe.wait_ge(s_mx, gi * NI + n - 1 + AHEAD)
                mm = nc.tensor.matmul(ps_1[n % 2][:, 0:width], Q[g][:, j, qt * P:(qt + 1) * P], K[g][:, j, c * CH:c * CH + width],
                                      start=True, stop=not diagonal, skip_group_check=True)
                if diagonal:
                    mm = nc.tensor.matmul(ps_1[n % 2][:, width - P:width], identb[:], mask[:], start=False, stop=True,
                                          skip_group_check=True)
                mm.then_inc(s_p1, 1)

            def turn_max(b, g):
                gi = b * NG + g
                pe.wait_ge(s_cmb, gi + 1)
                nc.tensor.transpose(ps_1[0][0:GH * QT, 0:P], negm[:, g % 2].rearrange("p j t -> p (j t)"), ident[:]).then_inc(s_mt, 1)

            def scores(b, g, n, p):
                gi = b * NG + g
                c, kt, r = BLOCKS[n]
                w = CH - r * P
                pe.wait_ge(s_exp, gi * 2 * NB + 2 * n + p - 1 + AHEAD)
                for h in range(2):
                    mm = nc.tensor.matmul(ps_s[p][:, h * CH:h * CH + w], K[g][:, 2 * p + h, kt * P:(kt + 1) * P],
                                          Q[g][:, 2 * p + h, c * CH + r * P:(c + 1) * CH], start=True, stop=True)
                mm.then_inc(s_st, 1)

            def product(b, g, n):
                gi = b * NG + g
                c, kt, r = BLOCKS[n]
                w = CH - r * P
                if kt >= c * PER:
                    pe.wait_ge(s_mk, gi * 2 * PER + c * PER + (kt - c * PER) + 1)
                else:
                    pe.wait_ge(s_exp, gi * 2 * NB + 2 * n + 2 + AHEAD)
                if kt == 0:
                    pe.wait_ge(s_cx, gi * 2 + c - 1 + AHEAD)
                for j in range(GH):
                    mm = nc.tensor.matmul(ps_c[c][j * VW:(j + 1) * VW, r * P:CH], VG[:, g % 2, kt, j * VW:(j + 1) * VW],
                                          PT[:, n % RP, j, 0:w], start=kt == 0, stop=kt == (c + 1) * PER - 1, skip_group_check=True)
                mm.then_inc(s_pv, 1)

            def turn_context(b, g, c):
                gi = b * NG + g
                pe.wait_ge(s_ev, gi * 2 + c + 1)
                for t in range(PER):
                    mm = nc.tensor.transpose(ps_c[c][:, t * P:(t + 1) * P], CT[:, c, t * P:(t + 1) * P], ident[:])
                mm.then_inc(s_ct, 1)

            for n in range(NI):
                item(0, 0, n)
            turn_max(0, 0)
            for n in range(NI):
                item(0, 1, n)

            def body(b, last):
                for g in range(NG):
                    ahead = not (last and g >= NG - 2)
                    b2, g2 = b + (g + 2) // NG, (g + 2) % NG
                    if not (last and g == NG - 1):
                        turn_max(b + (g + 1) // NG, (g + 1) % NG)
                    pe.wait_ge(s_ml[g], b * 16 + 16)
                    pe.wait_ge(s_vg, b * NG + g + 1)
                    for n in range(NB):
                        for p in range(2):
                            scores(b, g, n, p)
                            if ahead:
                                item(b2, g2, PER * n + p)
                        if n >= 2:
                            product(b, g, n - 2)
                        elif before(b, g):
                            product(*before(b, g), NB - 2 + n)
                        if ahead:
                            item(b2, g2, PER * n + 2)
                        if n == 3 and before(b, g):
                            turn_context(*before(b, g), 1)
                        if n == 7:
                            turn_context(b, g, 0)
                        if ahead:
                            item(b2, g2, PER * n + 3)
            batches(pe, body, 1)
            product(BATCH - 1, NG - 1, NB - 2)
            product(BATCH - 1, NG - 1, NB - 1)
            turn_context(BATCH - 1, NG - 1, 1)


def attention(nc, io, keep):
    dram = dict(
        qk=nc.dram_tensor("qk_parts", [2, PARTS, BATCH, DK, NH, SEQ], BF16).ap(),
        zeros=nc.dram_tensor("zero_rows", [PARTS, GH * SEQ], BF16).ap(),
        max=nc.dram_tensor("max_parts", [NG, PARTS, GH * SEQ], BF16).ap(),
    )
    with ExitStack() as ctx:
        sb = lambda n, s, d=F32: ctx.enter_context(nc.sbuf_tensor("c_" + n, s, d))
        own = dict(keep, Vt=sb("Vt", [P, NT, P]),
                   Q=[sb(f"Q{g}", [P, GH, SEQ], BF16) for g in range(NG)], K=[sb(f"K{g}", [P, GH, SEQ], BF16) for g in range(NG)],
                   s_ld=[ctx.enter_context(nc.semaphore(f"heads_loaded{g}")) for g in range(NG)])
        attn_project(nc, io, own, dram)
        attn_scores(nc, io, own, dram)


I1 = 64
GE = 4
NGE = E1 // GE
QTR = NT // BATCH
BEYOND = 1 << 17


def out_and_route(nc, io, keep, slots):
    CX, X, LG, ident, prob, idx_g = (keep[n] for n in ("CX", "X2t", "LG", "ident", "prob", "idx_g"))
    with ExitStack() as ctx:
        sb = lambda n, s, d=F32: ctx.enter_context(nc.sbuf_tensor("r_" + n, s, d))
        sem = lambda n: ctx.enter_context(nc.semaphore("r_" + n))
        bank = lambda n: ctx.enter_context(nc.psum_tensor("r_" + n, [P, CH], F32))
        w = sb("w", [P, P])
        bo = sb("bo", [1, PER, P])
        ones_row = sb("ones_row", [1, P])
        CXT = sb("CXT", [P, 2, CH])
        stats = sb("stats", [P, NT, 6])
        mv = sb("mv", [P, NT, 2])
        rstd = sb("rstd", [P, NT])
        router = sb("router", [P, E1])
        zero = sb("zero", [P, SLOTS // 4])
        top = sb("top", [P, NT, 8])
        idx = sb("idx", [P, NT, 8], U32)
        idxf = sb("idxf", [P, NT, 8])
        ex = sb("ex", [P, NT, E1])
        ex4 = sb("ex4", [P, NT, TOPK])
        den = sb("den", [P, NT])
        iota_i = sb("iota_i", [P, QTR, E1], I32)
        iota = sb("iota", [P, QTR, E1])
        oh = sb("oh", [P, TOPK, QTR, E1])
        pair = sb("pair", [P, 2, QTR, E1])
        M = sb("M", [P, 2, QTR, E1], BF16)
        trif = sb("trif", [P, P])
        tri = sb("tri", [P, P], BF16)
        ones = sb("ones", [P, P], BF16)
        base = sb("base", [P, NT + 1, E1])
        pos = sb("pos", [P, QTR, E1])
        posj = sb("posj", [P, TOPK, QTR])
        slot = sb("slot", [P, TOPK, QTR])
        over = sb("over", [P, TOPK, QTR])
        idx_s = sb("idx_s", [P, TOPK, NT], I32)
        ps_t = [bank(f"ps_t{k}") for k in range(2)]
        ps_o = [bank(f"ps_o{k}") for k in range(2)]
        ps_l = [bank(f"ps_l{k}") for k in range(2)]
        ps_p, ps_n = bank("ps_p"), bank("ps_n")
        s_w, s_z, s_zb, s_zw, s_c0, s_t, s_c, s_u, s_r = (sem(n) for n in (
            "weights", "shapes", "slots_zeroed", "w2_zeroed", "consts", "turned", "copied", "used", "residual"))
        s_st, s_ag, s_v, s_sq, s_rc, s_n, s_lc = (sem(n) for n in (
            "stats", "aggregated", "variance", "sqrt", "rstd", "normed", "logits_copied"))
        s_top, s_i, s_if, s_e, s_pr, s_m, s_rk, s_b, s_x, s_sc = (sem(n) for n in (
            "top", "index", "index_f32", "exp_in", "exp", "mask", "rank", "chain", "slots", "scattered"))

        ctx.enter_context(nc.allow_non_contiguous_dma(reason="rows of experts"))
        block = ctx.enter_context(nc.Block())

        @block.sync
        def _(sp):
            sp.dma_start(w[:], io["Wo"]).then_inc(s_w, 16)
            sp.dma_start(bo[:], io["bo"].rearrange("(a b n) -> a b n", a=1, b=1).broadcast_to([1, PER, P])).then_inc(s_w, 16)
            sp.dma_start(router[:], io["router_w"]).then_inc(s_w, 16)
            sp.wait_ge(s_z, 2)
            for q in range(4):
                rows = slots[q * (SLOTS // 4):(q + 1) * (SLOTS // 4), :].rearrange("(p a) n -> p (a n)", p=P)
                sp.dma_start(rows, zero[:]).then_inc(s_zb, 16)
            for e in range(0, E1, GE):
                sp.dma_start(keep["w1"][:, e:e + GE, :], io["w1"][e:e + GE].rearrange("e d f -> d e f")).then_inc(keep["s_ew"], 16)
            sp.wait_ge(s_zw, 1)
            for q in range(2):
                src = io["w2"].rearrange("(c q) i n -> q i c n", q=2)[q]
                dst = keep["w2"][q * I1:(q + 1) * I1, q:E1:2, :]
                sp.dma_start(dst, src).then_inc(keep["s_ew"], 16)

        @block.gpsimd
        def _(pool):
            nc.gpsimd.memset(ones_row[:], 1.0).then_inc(s_z, 1)
            nc.gpsimd.memset(zero[:], 0.0).then_inc(s_z, 1)
            nc.gpsimd.iota(iota_i[:], pattern=[[0, QTR], [1, E1]], base=0, channel_multiplier=0).then_inc(s_z, 1)
            nc.gpsimd.memset(trif[:], 1.0).then_inc(s_z, 1)
            pool.wait_ge(s_z, 4)
            nc.gpsimd.affine_select(out=trif[:], in_=trif[:], compare_op=ALU.is_gt, fill=0.0, base=0,
                                    pattern=[[1, P]], channel_multiplier=-1).then_inc(s_z, 1)
            nc.gpsimd.memset(keep["w2"][:].rearrange("p e n -> p (e n)"), 0.0).then_inc(s_zw, 1)
            pool.wait_ge(s_zb, 16 * 4)
            for q in range(BATCH):
                pool.wait_ge(s_x, q + 1)
                for t in range(q * QTR, (q + 1) * QTR):
                    for j in range(TOPK):
                        pool.indirect_dma_start(out=slots, out_offset=bass.IndirectOffsetOnAxis(ap=idx_s[:, j, t:t + 1].bitcast(U32), axis=0),
                                                in_=X[:, t, :], in_offset=None, bounds_check=SLOTS - 1,
                                                oob_is_err=False).then_inc(s_sc, 16)
            pool.wait_ge(s_sc, 16 * TOPK * NT)

        @block.scalar
        def _(act):
            def copy(m):
                act.wait_ge(s_t, m + 1)
                if m >= 2:
                    act.wait_ge(s_u, m - 1)
                nc.scalar.activation(CXT[:, m % 2, :], ps_t[m % 2][:], ACT.Copy).then_inc(s_c, 1)
            for q in range(BATCH):
                copy(4 * q)
                copy(4 * q + 1)
                act.wait_ge(s_v, q + 1)
                part = rstd[:, q * QTR:(q + 1) * QTR]
                nc.scalar.activation(part, part, ACT.Sqrt).then_inc(s_sq, 1)
                copy(4 * q + 2)
                copy(4 * q + 3)
            act.wait_ge(s_e, 2)
            nc.scalar.activation(ex[:], ex[:], ACT.Exp).then_inc(s_pr, 1)
            nc.scalar.activation(ex4[:], ex4[:], ACT.Exp).then_inc(s_pr, 1)

        @block.vector
        def _(dve):
            dve.wait_ge(s_z, 5)
            nc.vector.tensor_copy(iota[:], iota_i[:]).then_inc(s_c0, 1)
            nc.vector.tensor_copy(tri[:], trif[:]).then_inc(s_c0, 1)
            nc.vector.memset(ones[:], 1.0).then_inc(s_c0, 1)
            nc.vector.memset(base[:, 0, :], 0.0).then_inc(s_c0, 1)
            dve.wait_ge(s_c0, 4)

            n = 0

            def link(ins):
                nonlocal n
                n += 1
                ins.then_inc(s_b, 1)
                dve.wait_ge(s_b, n)

            def layer_norm(q):
                for i in (2 * q, 2 * q + 1):
                    dve.wait_ge(s_u, 4 * q + i % 2 + 1)
                    rows = X[:, i * PER:(i + 1) * PER, :].rearrange("p t n -> p (t n)")
                    nc.vector.tensor_tensor(rows, rows, ps_o[i % 2][:], ALU.add).then_inc(s_r, 1)
                    dve.wait_ge(s_r, i + 1)
                    for t in range(i * PER, (i + 1) * PER):
                        nc.vector.bn_stats(stats[:, t, :], X[:, t, :]).then_inc(s_st, 1)
                for t in range(q * QTR, (q + 1) * QTR):
                    dve.wait_ge(s_st, t + 1)
                    nc.vector.bn_aggr(mv[:, t, :], stats[:, t, :]).then_inc(s_ag, 1)
                tiles = slice(q * QTR, (q + 1) * QTR)
                dve.wait_ge(s_ag, (q + 1) * QTR)
                nc.vector.tensor_scalar(rstd[:, tiles], mv[:, tiles, 1], EPS, None, ALU.add).then_inc(s_v, 1)
                dve.wait_ge(s_sq, q + 1)
                nc.vector.reciprocal(rstd[:, tiles], rstd[:, tiles]).then_inc(s_rc, 1)
                dve.wait_ge(s_rc, q + 1)
                for t in range(q * QTR, (q + 1) * QTR):
                    nc.vector.tensor_scalar(X[:, t, :], X[:, t, :], mv[:, t, 0:1], rstd[:, t:t + 1],
                                            ALU.subtract, ALU.mult).then_inc(s_n, 1)

            def top_four(q):
                dve.wait_ge(s_u, 4 * q + 4)
                tiles = slice(q * QTR, (q + 1) * QTR)
                nc.vector.tensor_copy(LG[:, tiles, :].rearrange("p t e -> p (t e)"), ps_l[q % 2][:]).then_inc(s_lc, 1)
                dve.wait_ge(s_lc, q + 1)
                for t in range(q * QTR, (q + 1) * QTR):
                    nc.vector.max(top[:, t, :], LG[:, t, :]).then_inc(s_top, 1)
                for t in range(q * QTR, (q + 1) * QTR):
                    dve.wait_ge(s_top, t + 1)
                    nc.vector.max_index(idx[:, t, :], top[:, t, :], LG[:, t, :]).then_inc(s_i, 1)
                dve.wait_ge(s_i, (q + 1) * QTR)
                nc.vector.tensor_copy(idxf[:, tiles, :], idx[:, tiles, :]).then_inc(s_if, 1)
                dve.wait_ge(s_if, q + 1)

            def place(q):
                nonlocal n
                tiles = slice(q * QTR, (q + 1) * QTR)
                for j in range(TOPK):
                    ins = nc.vector.tensor_tensor(oh[:, j], iota[:], wide(idxf[:, tiles, j], E1), ALU.is_equal)
                    if j < TOPK - 1:
                        ins.then_inc(s_b, 1)
                        n += 1
                link(ins)
                for j in range(2):
                    ins = nc.vector.tensor_tensor(pair[:, j], oh[:, 2 * j], oh[:, 2 * j + 1], ALU.add)
                    if j == 0:
                        ins.then_inc(s_b, 1)
                        n += 1
                link(ins)
                nc.vector.tensor_tensor(M[:, q % 2], pair[:, 0], pair[:, 1], ALU.add).then_inc(s_m, 1)
                dve.wait_ge(s_rk, 2 * q + 2)
                for t in range(QTR):
                    g = q * QTR + t
                    link(nc.vector.tensor_tensor(base[:, g + 1, :], base[:, g, :], ps_n[:, t * E1:(t + 1) * E1], ALU.add))
                link(nc.vector.tensor_tensor(pos[:], ps_p[:].rearrange("p (t e) -> p t e", e=E1), base[:, tiles, :], ALU.add))
                for j in range(TOPK):
                    ins = nc.vector.tensor_tensor(oh[:, j], oh[:, j], pos[:], ALU.mult)
                    if j < TOPK - 1:
                        ins.then_inc(s_b, 1)
                        n += 1
                link(ins)
                link(nc.vector.tensor_reduce(posj[:], oh[:], AX.X, ALU.add))
                experts = idxf[:, tiles, 0:TOPK].rearrange("p t j -> p j t")
                link(nc.vector.tensor_scalar(slot[:], posj[:], float(CAP - 1), None, ALU.min))
                link(nc.vector.scalar_tensor_tensor(out=slot[:], in0=experts, scalar=float(CAP), in1=slot[:], op0=ALU.mult, op1=ALU.add))
                link(nc.vector.tensor_copy(idx_g[:, :, tiles], slot[:]))
                link(nc.vector.tensor_scalar(over[:], posj[:], float(CAP), float(BEYOND), ALU.is_ge, ALU.mult))
                link(nc.vector.tensor_tensor(over[:], over[:], slot[:], ALU.add))
                nc.vector.tensor_copy(idx_s[:, :, tiles], over[:]).then_inc(s_x, 1)

            for q in range(BATCH):
                layer_norm(q)
                top_four(q)
                place(q)
            nc.vector.tensor_tensor(ex[:], LG[:], wide(top[:, :, 0], E1), ALU.subtract).then_inc(s_e, 1)
            nc.vector.tensor_tensor(ex4[:], top[:, :, 0:TOPK], wide(top[:, :, 0], TOPK), ALU.subtract).then_inc(s_e, 1)
            dve.wait_ge(s_pr, 2)
            link(nc.vector.tensor_reduce(den[:], ex[:], AX.X, ALU.add))
            link(nc.vector.reciprocal(den[:], den[:]))
            link(nc.vector.tensor_tensor(prob[:], ex4[:], wide(den[:], TOPK), ALU.mult))

        @block.tensor
        def _(pe):
            pe.wait_ge(s_w, 48)
            pe.wait_ge(s_c0, 4)
            pe.wait_ge(s_z, 1)

            def turn(m, rows, i):
                if m >= 2:
                    pe.wait_ge(s_c, m - 1)
                for t in range(PER):
                    mm = nc.tensor.transpose(ps_t[m % 2][:, t * P:(t + 1) * P], rows[:, i * PER + t, :], ident[:])
                mm.then_inc(s_t, 1)
            for q in range(BATCH):
                for h in range(2):
                    turn(4 * q + h, CX, 2 * q + h)
                for h in range(2):
                    i = 2 * q + h
                    pe.wait_ge(s_c, 4 * q + h + 1)
                    if i >= 2:
                        pe.wait_ge(s_r, i - 1)
                    nc.tensor.matmul(ps_o[h][:], ones_row[:], bo[:].rearrange("a t n -> a (t n)"), start=True, stop=False)
                    for t in range(PER):
                        mm = nc.tensor.matmul(ps_o[h][:, t * P:(t + 1) * P], CXT[:, h, t * P:(t + 1) * P], w[:], start=False, stop=t == PER - 1)
                    mm.then_inc(s_u, 1)
                for h in range(2):
                    pe.wait_ge(s_n, (2 * q + h + 1) * PER)
                    turn(4 * q + 2 + h, X, 2 * q + h)
                if q >= 2:
                    pe.wait_ge(s_lc, q - 1)
                for h in range(2):
                    pe.wait_ge(s_c, 4 * q + 2 + h + 1)
                    for t in range(PER):
                        col = (h * PER + t) * E1
                        mm = nc.tensor.matmul(ps_l[q % 2][:, col:col + E1], CXT[:, h, t * P:(t + 1) * P], router[:], start=True, stop=True)
                    mm.then_inc(s_u, 1)
                pe.wait_ge(s_m, q + 1)
                if q >= 1:
                    pe.wait_ge(s_x, q)
                rows = M[:, q % 2].rearrange("p t e -> p (t e)")
                nc.tensor.matmul(ps_n[:], ones[:], rows, start=True, stop=True).then_inc(s_rk, 1)
                nc.tensor.matmul(ps_p[:], tri[:], rows, start=True, stop=True).then_inc(s_rk, 1)


def moe_experts(nc, io, keep, slots, outs):
    ident, w1, w2 = keep["ident"], keep["w1"], keep["w2"]
    RX = 4
    with ExitStack() as ctx:
        sb = lambda n, s, d=F32: ctx.enter_context(nc.sbuf_tensor("e_" + n, s, d))
        sem = lambda n: ctx.enter_context(nc.semaphore("e_" + n))
        bank = lambda n: ctx.enter_context(nc.psum_tensor("e_" + n, [P, CH], F32))
        x = sb("x", [P, RX, GE, P])
        xT = sb("xT", [P, 2, CH])
        S = sb("S", [P, 2, GE, I1])
        H = sb("H", [P, 2, GE, I1])
        HT = sb("HT", [P, 2, GE // 2, P])
        Y = sb("Y", [P, 2, GE, P])
        ps_x = [bank(f"ps_x{k}") for k in range(2)]
        ps_h = [bank(f"ps_h{k}") for k in range(2)]
        ps_t = [bank(f"ps_t{k}") for k in range(2)]
        ps_y = [bank(f"ps_y{k}") for k in range(2)]
        s_ld = [sem(f"loaded{r}") for r in range(RX)]
        s_st = [sem(f"stored{k}") for k in range(2)]
        s_x, s_xc, s_u, s_s, s_h, s_t, s_tc, s_y, s_yc = (sem(n) for n in (
            "turned", "copied", "up", "silu", "gated", "h_turned", "h_copied", "out", "out_copied"))

        block = ctx.enter_context(nc.Block())

        def ring(eng, step):
            for r in range(RX):
                step(r, r)
            with eng.Fori(1, NGE // RX) as j:
                for r in range(RX):
                    step(j * RX + r, r)

        @block.sync
        def _(sp):
            def load(i, r):
                if past(i, RX):
                    sp.wait_ge(s_x, i - (RX - 1))
                sp.dma_start(x[:, r], slots[bass.ds(i * (GE * CAP), GE * CAP), :].rearrange("(e s) n -> s e n", e=GE)).then_inc(s_ld[r], 16)
            ring(sp, load)

        @block.gpsimd
        def _(pool):
            def store(i, k):
                pool.wait_ge(s_yc, i + 1)
                pool.dma_start(outs[bass.ds(i * (GE * CAP), GE * CAP), :].rearrange("(e s) n -> s e n", e=GE), Y[:, k]).then_inc(s_st[k], 16)
            twos(pool, NGE, store)
            for k in range(2):
                pool.wait_ge(s_st[k], 16 * NGE // 2)

        @block.scalar
        def _(act):
            nc.scalar.preload_act_table(ACT.Silu)

            def x_copy(i, k):
                act.wait_ge(s_x, i + 1)
                if past(i):
                    act.wait_ge(s_u, i - 1)
                nc.scalar.activation(xT[:, k, :], ps_x[k][:], ACT.Copy).then_inc(s_xc, 1)

            def silu(i, k):
                act.wait_ge(s_u, i + 1)
                if past(i):
                    act.wait_ge(s_h, i - 1)
                half = ps_h[k][:].rearrange("p (e n) -> p e n", e=GE)[:, :, 0:I1]
                nc.scalar.activation(S[:, k], half, ACT.Silu).then_inc(s_s, 1)

            def h_copy(i, k):
                act.wait_ge(s_t, i + 1)
                if past(i):
                    act.wait_ge(s_y, i - 1)
                nc.scalar.activation(HT[:, k].rearrange("p c n -> p (c n)"), ps_t[k][:, 0:GE // 2 * P], ACT.Copy).then_inc(s_tc, 1)
            x_copy(0, 0)

            def step(i, k):
                if not (isinstance(i, int) and i == NGE - 1):
                    x_copy(i + 1, 1 - k)
                silu(i, k)
                h_copy(i, k)
            step(0, 0)
            step(1, 1)
            with act.Fori(1, NGE // 2 - 1) as j:
                for k in range(2):
                    step(j * 2 + k, k)
            step(NGE - 2, 0)
            step(NGE - 1, 1)

        @block.vector
        def _(dve):
            def step(i, k):
                dve.wait_ge(s_s, i + 1)
                if past(i):
                    dve.wait_ge(s_t, i - 1)
                half = ps_h[k][:].rearrange("p (e n) -> p e n", e=GE)[:, :, I1:2 * I1]
                nc.vector.tensor_tensor(H[:, k], S[:, k], half, ALU.mult).then_inc(s_h, 1)
                dve.wait_ge(s_y, i + 1)
                if past(i):
                    dve.wait_ge(s_st[k], (i - k) * 8)
                nc.vector.tensor_copy(Y[:, k].rearrange("p e n -> p (e n)"), ps_y[k][:]).then_inc(s_yc, 1)
            twos(dve, NGE, step)

        @block.tensor
        def _(pe):
            pe.wait_ge(keep["s_ew"], 16 * (NGE + 2))

            def turn(i, k, r):
                pe.wait_ge(s_ld[r], (i - r) * (16 // RX) + 16)
                if past(i):
                    pe.wait_ge(s_xc, i - 1)
                for e in range(GE):
                    mm = nc.tensor.transpose(ps_x[k][:, e * P:(e + 1) * P], x[:, r, e, :], ident[:])
                mm.then_inc(s_x, 1)

            def up(i, k):
                pe.wait_ge(s_xc, i + 1)
                if past(i):
                    pe.wait_ge(s_h, i - 1)
                for e in range(GE):
                    w = w1[:, bass.ds(i * GE + e, 1), :].rearrange("p a n -> p (a n)")
                    mm = nc.tensor.matmul(ps_h[k][:, e * P:(e + 1) * P], xT[:, k, e * P:(e + 1) * P], w, start=True, stop=True)
                mm.then_inc(s_u, 1)

            def turn_hidden(i, k):
                pe.wait_ge(s_h, i + 1)
                if past(i):
                    pe.wait_ge(s_tc, i - 1)
                for c in range(GE // 2):
                    mm = nc.tensor.transpose(ps_t[k][:, c * P:(c + 1) * P], H[:, k, 2 * c:2 * c + 2, :].rearrange("p e n -> p (e n)"), ident[:])
                mm.then_inc(s_t, 1)

            def down(i, k):
                pe.wait_ge(s_tc, i + 1)
                if past(i):
                    pe.wait_ge(s_yc, i - 1)
                for e in range(GE):
                    w = w2[:, bass.ds(i * GE + e, 1), :].rearrange("p a n -> p (a n)")
                    mm = nc.tensor.matmul(ps_y[k][:, e * P:(e + 1) * P], HT[:, k, e // 2, :], w, start=True, stop=True)
                mm.then_inc(s_y, 1)

            def step(i, k, r):
                turn(i + 1, 1 - k, (r + 1) % RX)
                up(i, k)
                if past(i, 1):
                    down(i - 1, 1 - k)
                turn_hidden(i, k)

            turn(0, 0, 0)
            for r in range(RX):
                step(r, r % 2, r)
            with pe.Fori(1, NGE // RX - 1) as j:
                for r in range(RX):
                    step(j * RX + r, r % 2, r)
            for i in range(NGE - RX, NGE - 1):
                step(i, i % 2, i % RX)
            up(NGE - 1, 1)
            down(NGE - 2, 0)
            turn_hidden(NGE - 1, 1)
            down(NGE - 1, 1)


def moe_combine(nc, io, keep, outs, out):
    X, prob, idx_g = keep["X2t"], keep["prob"], keep["idx_g"]
    RING = 4
    with ExitStack() as ctx:
        sb = lambda n, s, d=F32: ctx.enter_context(nc.sbuf_tensor("y_" + n, s, d))
        sem = lambda n: ctx.enter_context(nc.semaphore("y_" + n))
        Yg = sb("Yg", [P, RING, TOPK, P])
        stats = sb("stats", [P, NT, 6])
        mv = sb("mv", [P, NT, 2])
        rstd = sb("rstd", [P, NT])
        s_g = [sem(f"gathered{k}") for k in range(RING)]
        s_a, s_b, s_v, s_q, s_r, s_n, s_o = (sem(n) for n in ("added", "stats", "variance", "sqrt", "rstd", "normed", "stored"))

        block = ctx.enter_context(nc.Block())
        rows = out.rearrange("b (t p) n -> p (b t) n", p=P)

        @block.gpsimd
        def _(pool):
            for t in range(NT):
                if t >= RING:
                    pool.wait_ge(s_a, TOPK * (t - RING + 1))
                for j in range(TOPK):
                    pool.indirect_dma_start(out=Yg[:, t % RING, j, :], out_offset=None, in_=outs,
                                            in_offset=bass.IndirectOffsetOnAxis(ap=idx_g[:, j, t:t + 1].bitcast(U32), axis=0),
                                            bounds_check=SLOTS - 1, oob_is_err=False).then_inc(s_g[t % RING], 16)

        @block.scalar
        def _(act):
            with act.Fori(0, BATCH) as q:
                act.wait_ge(s_v, q + 1)
                part = rstd[:, bass.ds(q * QTR, QTR)]
                nc.scalar.activation(part, part, ACT.Sqrt).then_inc(s_q, 1)

        @block.vector
        def _(dve):
            for t in range(NT):
                dve.wait_ge(s_g[t % RING], 16 * TOPK * (t // RING + 1))
                for j in range(TOPK):
                    nc.vector.scalar_tensor_tensor(out=X[:, t, :], in0=Yg[:, t % RING, j, :], scalar=prob[:, t, j:j + 1], in1=X[:, t, :],
                                                   op0=ALU.mult, op1=ALU.add).then_inc(s_a, 1)
                    dve.wait_ge(s_a, TOPK * t + j + 1)
                nc.vector.bn_stats(stats[:, t, :], X[:, t, :]).then_inc(s_b, 1)
                dve.wait_ge(s_b, 2 * t + 1)
                nc.vector.bn_aggr(mv[:, t, :], stats[:, t, :]).then_inc(s_b, 1)
                if t % QTR == QTR - 1:
                    q = t // QTR
                    tiles = slice(q * QTR, (q + 1) * QTR)
                    dve.wait_ge(s_b, 2 * t + 2)
                    nc.vector.tensor_scalar(rstd[:, tiles], mv[:, tiles, 1], EPS, None, ALU.add).then_inc(s_v, 1)
                    dve.wait_ge(s_q, q + 1)
                    nc.vector.reciprocal(rstd[:, tiles], rstd[:, tiles]).then_inc(s_r, 1)
                    dve.wait_ge(s_r, q + 1)
                    for u in range(q * QTR, (q + 1) * QTR):
                        nc.vector.tensor_scalar(X[:, u, :], X[:, u, :], mv[:, u, 0:1], rstd[:, u:u + 1],
                                                ALU.subtract, ALU.mult).then_inc(s_n, 1)

        @block.sync
        def _(sp):
            with sp.Fori(0, BATCH) as q:
                sp.wait_ge(s_n, q * QTR + QTR)
                sp.dma_start(rows[:, bass.ds(q * QTR, QTR), :], X[:, bass.ds(q * QTR, QTR), :]).then_inc(s_o, 16)
            sp.wait_ge(s_o, 16 * BATCH)


def moe(nc, io, keep, out):
    slots = nc.dram_tensor("slots", [SLOTS, P], F32).ap()
    outs = nc.dram_tensor("slot_outputs", [SLOTS, P], F32).ap()
    with ExitStack() as ctx:
        own = dict(keep, w1=ctx.enter_context(nc.sbuf_tensor("experts_w1", [P, E1, 2 * I1], F32)),
                   w2=ctx.enter_context(nc.sbuf_tensor("experts_w2", [P, E1, P], F32)),
                   s_ew=ctx.enter_context(nc.semaphore("expert_weights")))
        out_and_route(nc, io, own, slots)
        moe_experts(nc, io, own, slots, outs)
    moe_combine(nc, io, keep, outs, out)


def build(nc, io, out):
    with ExitStack() as ctx:
        sb = lambda n, s, d=F32: ctx.enter_context(nc.sbuf_tensor(n, s, d))
        keep = dict(ones=sb("mean_ones", [P, P]), eps=sb("eps", [P, 1]), one=sb("one", [P, 1]), ident=sb("ident", [P, P]))
        keep["X1"] = sb("X1", [P, T])
        mamba(nc, io, keep)
        keep["X2"] = sb("X2", [P, T])
        keep["X2t"] = sb("X2t", [P, NT, P])
        ffn(nc, io, keep)
        keep["CX"] = sb("CX", [P, NT, P])
        attention(nc, io, keep)
        keep["LG"] = sb("LG", [P, NT, E1])
        keep["prob"] = sb("prob", [P, NT, TOPK])
        keep["idx_g"] = sb("idx_g", [P, TOPK, NT], I32)
        moe(nc, io, keep, out)


def kernel(**inputs):
    import concourse.bacc as _bacc
    from concourse.bass_utils import run_bass_kernel_spmd as _run

    mixer = lambda n: inputs["L0_attn_" + n]
    gated = lambda n: inputs["L0_ffn_" + n]
    laid = dict(
        xT=mixer("x").reshape(T, P).T, norm_w=mixer("norm_w"), in_wT=mixer("in_proj_w").T,
        conv_w=mixer("conv_w"), conv_b=mixer("conv_b"), xp_w=mixer("x_proj_w"), xp_wT=mixer("x_proj_w").T, dt_wT=mixer("dt_proj_w").T,
        dt_b=mixer("dt_proj_b"), A_log=mixer("A_log"), D=mixer("D"), out_wT=mixer("out_proj_w").T, norm_f_w=mixer("norm_f_w"),
        gate_w=gated("gate_W"), sh_w=gated("shared_W"), sh_b=gated("shared_b"), gamma=gated("gamma"), beta=gated("beta"),
        b2=gated("b2"), W1=gated("W1"), W2=gated("W2"), b1T=gated("b1").reshape(E0, HM, P).transpose(0, 2, 1),
        router_w=inputs["L1_ffn_router_w"], w1=inputs["L1_ffn_w1"], w2=inputs["L1_ffn_w2"],
        **{n: inputs["L1_attn_" + n].transpose(1, 0, 2).reshape(P, P) for n in ("Wq", "Wk", "Wv")},
        **{n: inputs["L1_attn_" + n] for n in ("Wo", "bq", "bk", "bv", "bo")},
    )
    nc = _bacc.Bacc("TRN2", target_bir_lowering=False, num_devices=1)
    arrays, io = {}, {}
    for name, a in laid.items():
        a = np.ascontiguousarray(a)
        arrays[f"in_{name}_dram"] = a
        io[name] = nc.dram_tensor(f"in_{name}_dram", a.shape, mybir.dt.from_np(a.dtype), kind="ExternalInput").ap()
    out = nc.dram_tensor("out_0_dram", (BATCH, SEQ, P), F32, kind="ExternalOutput").ap()
    build(nc, io, out)
    r = _run(nc, [arrays], core_ids=[0])
    return r.results[0]["out_0_dram"]
```
